# Optimizing a Trainium2 kernel written in Bass

```python
import numpy as np
import jax
import jax.numpy as jnp

def _softmax(x, axis=-1):
    return jax.nn.softmax(x, axis=axis)

def _gelu(x):
    return jax.nn.gelu(x, approximate=True)

def _silu(x):
    return jax.nn.silu(x)

def _sigmoid(x):
    return jax.nn.sigmoid(x)

def _layernorm(x, axis=-1, eps=1e-05):
    m = jnp.mean(x, axis=axis, keepdims=True)
    v = jnp.var(x, axis=axis, keepdims=True)
    return (x - m) / jnp.sqrt(v + eps)

def _scatter_add(tgt, idx, src, axis=0):
    return tgt.at[idx].add(src)

def _segment_sum(src, seg, n):
    return jax.ops.segment_sum(src, seg, n)
kernel_name = 'mk_xattn_ffn_d1_seqx_r4_8d4906'

def setup_inputs(seed: int=0):
    np.random.seed(seed)
    _w = jnp.asarray

    def _rec_inputs():
        import jax
        import jax.numpy as jnp
        _rk = jax.random.key(seed)
        x = 0.0002417 + 0.9998 * jax.random.normal(jax.random.fold_in(_rk, 1), (4, 1024, 256), jnp.float32)
        _lenS = 1024 - jax.random.randint(jax.random.fold_in(_rk, 7), (4,), 0, max(1, 1024 // 4) + 1, jnp.int32)
        _lenS2 = 154 - jax.random.randint(jax.random.fold_in(_rk, 8), (4,), 0, max(1, 154 // 4) + 1, jnp.int32)
        _ctx_1024P = jax.random.normal(jax.random.fold_in(_rk, 11), (4, 16, 256), jnp.float32)
        _ctx_1024c = jax.random.dirichlet(jax.random.fold_in(_rk, 511), 0.3 * jnp.ones((16,), jnp.float32), (4, 154))
        _ctx_1024t = jnp.einsum('bsk,bkd->bsd', _ctx_1024c, _ctx_1024P)
        _ctx_1024t = _ctx_1024t * jax.lax.rsqrt(jnp.mean(jnp.square(_ctx_1024t)) + 1e-12) * 0.953939
        ctx_1024 = 7.22013e-05 + 1.00017 * (_ctx_1024t + 0.3 * jax.random.normal(jax.random.fold_in(_rk, 611), (4, 154, 256), jnp.float32))
        return (x, ctx_1024)
    x, ctx_1024 = _rec_inputs()

    def _L0_xattn_setup():
        import jax, jax.numpy as jnp
        import numpy as np
        D_MODEL = 256
        B, S = (4, 512)
        key = jax.random.key(seed)
        ks = jax.random.split(key, 10)
        s = 1.0 / np.sqrt(D_MODEL)
        return {'k': jax.random.normal(ks[0], (B, S, D_MODEL), jnp.float32), 'v': jax.random.normal(ks[1], (B, S, D_MODEL), jnp.float32), 'q': jax.random.normal(ks[2], (B, S, D_MODEL), jnp.float32), 'Wk': jax.random.normal(ks[3], (D_MODEL, D_MODEL), jnp.float32) * s, 'Wv': jax.random.normal(ks[4], (D_MODEL, D_MODEL), jnp.float32) * s, 'bv': jnp.zeros((D_MODEL,), jnp.float32), 'Wq': jax.random.normal(ks[5], (D_MODEL, D_MODEL), jnp.float32) * s, 'bq': jnp.zeros((D_MODEL,), jnp.float32), 'Wo': jax.random.normal(ks[6], (D_MODEL, D_MODEL), jnp.float32) * s, 'bo': jnp.zeros((D_MODEL,), jnp.float32)}
    _L0_xattn_all = _L0_xattn_setup()
    _L0_xattn_in = {k: v for k, v in _L0_xattn_all.items() if k in ('Wk', 'Wv', 'bv', 'Wq', 'bq', 'Wo', 'bo')}
    del _L0_xattn_all

    def _L0_ffn_setup():
        import jax, jax.numpy as jnp
        import numpy as np
        D_MODEL = 256
        N_EXPERTS = 8
        TOP_K = 2
        HIDDEN = 4 * D_MODEL
        key = jax.random.key(seed)
        ks = jax.random.split(key, 6)
        B, S = (2, 512)
        x = jax.random.normal(ks[0], (B, S, D_MODEL), dtype=jnp.float32)
        shared_w1 = jax.random.normal(ks[1], (HIDDEN, D_MODEL), dtype=jnp.float32) * 0.02
        shared_w2 = jax.random.normal(ks[2], (D_MODEL, HIDDEN), dtype=jnp.float32) * 0.02
        experts_w1 = jax.random.normal(ks[3], (N_EXPERTS, HIDDEN, D_MODEL), dtype=jnp.float32) * 0.02
        experts_w2 = jax.random.normal(ks[4], (N_EXPERTS, D_MODEL, HIDDEN), dtype=jnp.float32) * 0.02
        gate_w = jax.random.normal(ks[5], (N_EXPERTS, D_MODEL), dtype=jnp.float32) * 0.02
        return {'x': x, 'shared_w1': shared_w1, 'shared_w2': shared_w2, 'experts_w1': experts_w1, 'experts_w2': experts_w2, 'gate_w': gate_w}
    _L0_ffn_all = _L0_ffn_setup()
    _L0_ffn_in = {k: v for k, v in _L0_ffn_all.items() if k in ('shared_w1', 'shared_w2', 'experts_w1', 'experts_w2', 'gate_w')}
    del _L0_ffn_all
    return {'x': x, 'ctx_1024': ctx_1024, 'L0_xattn_Wk': _L0_xattn_in['Wk'], 'L0_xattn_Wv': _L0_xattn_in['Wv'], 'L0_xattn_bv': _L0_xattn_in['bv'], 'L0_xattn_Wq': _L0_xattn_in['Wq'], 'L0_xattn_bq': _L0_xattn_in['bq'], 'L0_xattn_Wo': _L0_xattn_in['Wo'], 'L0_xattn_bo': _L0_xattn_in['bo'], 'L0_ffn_shared_w1': _L0_ffn_in['shared_w1'], 'L0_ffn_shared_w2': _L0_ffn_in['shared_w2'], 'L0_ffn_experts_w1': _L0_ffn_in['experts_w1'], 'L0_ffn_experts_w2': _L0_ffn_in['experts_w2'], 'L0_ffn_gate_w': _L0_ffn_in['gate_w']}

def reference(x, ctx_1024, L0_xattn_Wk, L0_xattn_Wv, L0_xattn_bv, L0_xattn_Wq, L0_xattn_bq, L0_xattn_Wo, L0_xattn_bo, L0_ffn_shared_w1, L0_ffn_shared_w2, L0_ffn_experts_w1, L0_ffn_experts_w2, L0_ffn_gate_w):
    import jax
    import jax.numpy as jnp

    def _L0_xattn_ref(k, v, q, Wk, Wv, bv, Wq, bq, Wo, bo):
        import jax, jax.numpy as jnp
        import numpy as np
        D_MODEL = 256
        B, S = (4, 512)
        kp = jnp.einsum('bsd,ed->bse', k, Wk)
        vp = jnp.einsum('bsd,ed->bse', v, Wv) + bv
        qp = jnp.einsum('bsd,ed->bse', q, Wq) + bq
        scale = 1.0 / jnp.sqrt(jnp.float32(kp.shape[-1]))
        scores = jnp.einsum('bqd,bkd->bqk', qp, kp) * scale
        probs = jax.nn.softmax(scores, axis=-1)
        ctx = jnp.einsum('bqk,bkd->bqd', probs, vp)
        return jnp.einsum('bqd,ed->bqe', ctx, Wo) + bo

    def _L0_ffn_ref(x, shared_w1, shared_w2, experts_w1, experts_w2, gate_w):
        import jax, jax.numpy as jnp
        import numpy as np
        D_MODEL = 256
        N_EXPERTS = 8
        TOP_K = 2
        HIDDEN = 4 * D_MODEL
        B, S, D = x.shape
        T = B * S
        x_flat = x.reshape(T, D)
        shared = jnp.einsum('td,dh->th', x_flat, shared_w1.T)
        shared = jnp.einsum('th,hd->td', jax.nn.silu(shared), shared_w2.T)
        gate_logits = x_flat @ gate_w.T
        top_k_gates, top_k_idx = jax.lax.top_k(gate_logits, TOP_K)
        top_k_gates = jax.nn.softmax(top_k_gates, axis=1)
        gates = jnp.zeros((T, N_EXPERTS), dtype=x.dtype)
        gates = gates.at[jnp.arange(T)[:, None], top_k_idx].set(top_k_gates)
        h = jnp.einsum('td,ehd->teh', x_flat, experts_w1)
        expert_out = jnp.einsum('teh,edh->ted', jax.nn.silu(h), experts_w2)
        selected = jnp.einsum('ted,te->td', expert_out, gates)
        return (shared + selected).reshape(B, S, D)
    x = x + _L0_xattn_ref(ctx_1024, ctx_1024, _layernorm(x, axis=-1), L0_xattn_Wk, L0_xattn_Wv, L0_xattn_bv, L0_xattn_Wq, L0_xattn_bq, L0_xattn_Wo, L0_xattn_bo)
    x = x + _L0_ffn_ref(_layernorm(x, axis=-1), L0_ffn_shared_w1, L0_ffn_shared_w2, L0_ffn_experts_w1, L0_ffn_experts_w2, L0_ffn_gate_w)
    return x

_drawn_inputs = setup_inputs


def setup_inputs(seed=0):
    import zlib

    import numpy as np

    out = dict(_drawn_inputs(seed))
    spreads = {'L0_xattn_bv': (0.0, 0.1), 'L0_xattn_bq': (0.0, 0.354), 'L0_xattn_bo': (0.0, 0.1)}
    factors = {}
    for name, (base, spread) in spreads.items():
        noise = np.random.default_rng([zlib.crc32(name.encode()), seed]).standard_normal(out[name].shape)
        drawn = base * np.exp(spread * noise) if base else spread * noise
        out[name] = jnp.asarray(drawn.astype(out[name].dtype))
    for name, factor in factors.items():
        out[name] = (out[name] * factor).astype(out[name].dtype)
    return out
```

```python
from contextlib import ExitStack

import concourse.bass as bass
from concourse import mybir

F32 = mybir.dt.float32
F16 = mybir.dt.float16
BF16 = mybir.dt.bfloat16
I32 = mybir.dt.int32
U32 = mybir.dt.uint32
ALU = mybir.AluOpType
ACT = mybir.ActivationFunctionType
AX = mybir.AxisListType
SUM = bass.bass_isa.ReduceOp.add

P = 128


def xattn_moe_kernel(nc, x, ctx_in, Wk, Wv, bv, Wq, bq, Wo, bo, sw1, sw2, ew1, ew2, gate_w, out):
    B, S, D = x.shape
    C = ctx_in.shape[1]
    E, HID, _ = ew1.shape
    KD = D // P
    KH = HID // P
    C2 = C - P
    NT = B * S // P
    JT = S // P
    R = 2 * P
    SHARED = B * S // R
    ROUTED = (2 * B * S + E * (R - 1)) // R
    SH1 = 9
    SH2 = SHARED - SH1
    NF = SHARED + ROUTED
    HALVES = 2 * ROUTED
    BANKS = HID * R // P // 512
    CB = KH // BANKS
    NS = E + 1
    SLOT = 4 * KD * HID
    EPS = 1e-5
    ROW_SCALE_LOG = 11
    ROW_SCALE = float(1 << ROW_SCALE_LOG)
    NEG_SCALE = -float(D) ** -0.5
    LAST = NT - JT
    MOMENT_STEPS = 19
    AHEAD = 4
    CONSTANTS = 7
    assert KD == 2 and CB * R == 512 and D * 2 == 512 and NT % 4 == 0

    sb_list = ExitStack()
    with sb_list as es:
        def sb(name, shape, dt):
            return es.enter_context(nc.sbuf_tensor(name, shape, dt))

        def sem(name):
            return es.enter_context(nc.semaphore(name))

        rows_dram = nc.dram_tensor("ln_rows", [NT * P, 2 * D], F16, kind="Internal").ap()
        y_dram = nc.dram_tensor("expert_rows", [ROUTED * R, D], F32, kind="Internal").ap()

        wts = sb("wts", [P, NS, SLOT], F16)
        xres = sb("xres", [P, NT, D], F32)
        stage = sb("stage", [P, 2048], F32)
        work = sb("work", [P, 5120], F32)
        identf = sb("identf", [P, P], F32)
        ident16 = sb("ident16", [P, P], F16)
        upper = sb("upper", [P, P], BF16)
        ones_b = sb("ones_b", [P, P], BF16)
        iota_b = sb("iota_b", [P, P], BF16)
        iota_p = sb("iota_p", [P, 1], F32)
        gateT = sb("gateT", [P, KD, E], F32)
        stats = sb("stats", [P, NT, 6], F32)
        mean = sb("mean", [P, NT], F32)
        rstd = sb("rstd", [P, NT], F32)
        nmr = sb("nmr", [P, NT], F32)
        nt_a = sb("nt_a", [P, NT], F32)
        nt_v = sb("nt_v", [P, NT], F32)
        nt_b = sb("nt_b", [P, NT], F32)
        rowsum = sb("rowsum", [P, 4], F32)
        rinv = sb("rinv", [P, 2], F32)
        negmax = sb("negmax", [P, 2], F32)
        psq = sb("psq", [P, 2], F32)
        asq = sb("asq", [P, 2], F32)
        ebits = sb("ebits", [P, 2], I32)
        wscale = sb("wscale", [P, 2, NS], F32)
        inv1 = sb("inv1", [P, NS], F32)
        hsc = sb("hsc", [P, NS], F32)
        inv2 = sb("inv2", [P, NS], F32)
        tab = sb("tab", [P, 3, NF], F32)
        woff = sb("woff", [P, NF], I32)
        tok = sb("tok", [P, HALVES], U32)
        idx = sb("idx", [P, 2], U32)
        slot_u = sb("slot_u", [P, 2, NT], U32)
        gates = sb("gates", [P, 2, NT], F32)

        wflat = wts[:, :, :].rearrange("p s n -> p (s n)")
        NSL = NS - 1
        att = wts[:, NSL, :].bitcast(F32)
        ktn = att[:, 0:B * KD * C].rearrange("p (b k c) -> p b k c", b=B, k=KD)
        o = B * KD * C
        vct = att[:, o:o + B * 2 * D].rearrange("p (b k d) -> p b k d", b=B, k=2)
        o += B * 2 * D
        biasn = att[:, o:o + B * C].rearrange("p (b c) -> p b c", b=B)
        su = wts[:, NSL - 3:NSL, :].rearrange("p s n -> p (s n)").bitcast(F32)
        rawk, rawv, rawq, rawo, woT, fa, fc = (
            su[:, 512 * i:512 * i + 512].rearrange("p (c d) -> p c d", c=2) for i in range(7))
        o = 3584
        craw = su[:, o:o + B * 512].rearrange("p (b k d) -> p b k d", b=B, k=2)
        o += B * 512
        ctxT = su[:, o:o + B * KD * C].rearrange("p (b k c) -> p b k c", b=B, k=KD)
        o += B * KD * C
        ones_f = su[:, o:o + 128]
        ubc = su[:, o + 128:o + 384].rearrange("p (k n) -> p k n", k=2)
        bvbc = su[:, o + 384:o + 640].rearrange("p (k n) -> p k n", k=2)
        cbs = su[:, o + 640:o + 896]
        bq_c = su[:, o + 896:o + 898]
        bv_c = su[:, o + 898:o + 900]
        u_c = su[:, o + 900:o + 902]
        bo_r = su[0:1, o + 902:o + 1158]
        graw = su[0:E, o + 1158:o + 1158 + D]
        assert o + 1158 + D <= 3 * SLOT // 2

        xn = work[:, 0:512].rearrange("p (u d) -> p u d", u=2)
        xnT = work[:, 512:1024].rearrange("p (u k t) -> p u k t", u=2, k=2)
        sc = work[:, 1024:1024 + 2 * C].rearrange("p (u c) -> p u c", u=2)
        pT = work[:, 1408:1920].rearrange("p (u k t) -> p u k t", u=2, k=2)
        rout = sb("rout", [P, 2048], F32)
        raws = [stage[:, :], rout[:, :]]
        squares = work[:, 3968:4992].bitcast(BF16)

        def ln_buffers(t):
            return (t[:, 0:512].rearrange("p (u d) -> p u d", u=2),
                    t[:, 512:1024].rearrange("p (u k t) -> p u k t", u=2, k=2),
                    t[:, 1024:2048].bitcast(F16).rearrange("p (u d) -> p u d", u=4))

        ln_beside = ln_buffers(work[:, 1920:3968])
        ln_last = ln_buffers(stage[:, :])
        hring = work[:, 0:2048].bitcast(F16).rearrange("p (g s n) -> p g s n", g=BANKS, s=2)
        sring = work[:, 2048:3072].rearrange("p (g n) -> p g n", g=2)
        xT = work[:, 3072:4096].bitcast(F16).rearrange("p (u s k t) -> p u s k t", u=2, s=2, k=2)
        xg = work[:, 4096:4608].bitcast(F16).rearrange("p (h d) -> p h d", h=2)
        ybuf = work[:, 4608:5120]

        def table(i):
            return rout[:, 256 * i:256 * (i + 1)]
        lg, tmp, oh1, oh2, lg2, incl, slotf, rmask = (table(i) for i in range(8))

        def by_token(t):
            return t.rearrange("p (i e) -> p i e", e=E)

        def by_expert(t):
            return t.rearrange("p (e i) -> p e i", e=E)

        nt32 = sb("nt32", [P, 10, NT], F32)
        m1, m2, sel1, sel2, ex, den = (nt32[:, i, :] for i in range(6))
        halff = nt32[:, 6:8, :]
        posf = nt32[:, 8:10, :]
        esm = sb("esm", [P, 6, E], F32)
        cnt_i = sb("cnt_i", [P, E], I32)
        efirst = sb("efirst", [P, E], F32)
        RC = 16
        CHUNKS = 2 * NT // RC
        oh_pos = stage[:, 0:RC * P // 2].bitcast(BF16).rearrange("p (q n) -> p q n", q=RC)
        hw = RC * HALVES // 2
        oh_row = [rout[:, hw * q:hw * (q + 1)].bitcast(BF16).rearrange("p (q n) -> p q n", q=RC)
                  for q in range(2)]
        assert 2 * hw <= 1280
        tkf = rout[:, 1280:1280 + 2 * HALVES]
        eoh = rout[:, 0:ROUTED * E].rearrange("p (j e) -> p j e", e=E)
        eot = rout[:, 512:512 + ROUTED * E].rearrange("p (j e) -> p j e", e=E)
        ejf = rout[:, 1024:1024 + ROUTED]
        iot = sb("iot", [P, ROUTED], F32)
        ioe = sb("ioe", [P, E], F32)
        grow = stage[:, 0:2048].rearrange("p (u k d) -> p u k d", u=4, k=2)

        ps = [es.enter_context(nc.psum_tensor(f"bank{i}", [P, 512], F32)) for i in range(8)]
        pXT, pSC, pPT, pPV = ps[0:4]
        pW = [ps[4 + q] for q in (0, 1, 2, 0, 1, 2, 0, 1)]
        W_BACK = (2, 2, 5, 3, 3, 3, 3, 3)
        pZT, pLG = ps[7][:, 0:D], ps[7][:, D:D + NT * E]
        pH = [ps[i] for i in range(BANKS)]
        pY, pT16 = ps[4], ps[5][:, :].bitcast(F16).rearrange("p (s k t) -> p s k t", s=2, k=2)
        pPre, pTot, pTok = ps[6], ps[7], ps[6]

        names = """x0 x1 x2 x3 w_in c_in b_in const_ready ones_ready u_ready bv_bc u_bc su_pe su_ev values_ready dchain
            pchain raw_in0 raw_in1 raw_sq all_sq scale_step norm1_ready moment_step scale_ready wt_ps whi wlo xn_done xt_ps
            xnt_done sc_ps sc_sum sc_done exp_done pt_ps ptt_done pv_ps rinv_done x2_done stat_done
            z_done z_hi z_lo zt_ps ztt_done lg_ps rows0 rows1 rows2 rows3 gate_diff gate_exp mask_ready count_ps
            oneh_ready tok_ps routed_ready tabs0 rows_in xg_t xt_done h_ps silu_done hi_done lo_done
            y_ps y_done y_store idx_ready grow_in0 grow_in1 grow_in2 grow_in3 comb_part
            comb_done out_st passed""".split()
        sm = {n: sem(n) for n in names}
        raw_in = [sm["raw_in0"], sm["raw_in1"]]
        rows_st = [sm[f"rows{i}"] for i in range(4)]
        grow_in = [sm[f"grow_in{i}"] for i in range(4)]

        block = es.enter_context(nc.Block())

        def alone(eng):
            eng.sem_inc(sm["passed"], 1)

        def combined(m):
            ends = [0] + [min(-(-NT * q // (SH2 - 1)), 2 * (SH1 + q)) for q in range(1, SH2)] + [NT]
            return range(ends[m - 1], ends[m])

        def last_norm(tau, g):
            z = LAST + BANKS * tau + g - 2
            return z if LAST <= z <= NT else None

        def w1_part(slot_off, s, k, lo, n):
            at = slot_off + (s * KD + k) * HID + lo
            return wflat[:, bass.ds(at, n)]

        def w2_part(slot_off, s, c):
            at = slot_off + 2 * KD * HID + (s * KH + c) * D
            return wflat[:, bass.ds(at, D)]

        def tile_pairs(eng, lo, hi, body):
            if lo % 2 and lo < hi:
                body(lo, 1)
                lo += 1
            pairs = (hi - lo) // 2
            if pairs > 1:
                with eng.Fori(lo // 2, lo // 2 + pairs) as t:
                    body(2 * t, 0)
                    body(2 * t + 1, 1)
                lo += 2 * pairs
            while lo < hi:
                body(lo, lo % 2)
                lo += 1

        @block.sync
        def _(sp):
            for b in range(B):
                sp.dma_start(craw[:, b, 0, :], ctx_in[b, 0:P, :]).then_inc(sm["c_in"], 16)
                sp.dma_start(craw[0:C2, b, 1, :], ctx_in[b, P:C, :]).then_inc(sm["c_in"], 16)
            for t, w in ((rawk, Wk), (rawq, Wq), (rawv, Wv)):
                sp.dma_start(t, w.rearrange("(p c) d -> p c d", c=2)).then_inc(sm["w_in"], 16)
            sp.dma_start(rawo, Wo.rearrange("(c p) d -> p c d", p=P)).then_inc(sm["w_in"], 16)
            sp.dma_start(bq_c, bq.rearrange("(p c) -> p c", c=2)).then_inc(sm["b_in"], 16)
            sp.dma_start(bv_c, bv.rearrange("(p c) -> p c", c=2)).then_inc(sm["b_in"], 16)
            sp.dma_start(bo_r, bo.rearrange("(a d) -> a d", a=1)).then_inc(sm["b_in"], 16)
            sp.dma_start(graw, gate_w).then_inc(sm["b_in"], 16)
            for b in range(B):
                sp.dma_start(xres[:, b * JT:(b + 1) * JT, :],
                             x[b].rearrange("(p j) d -> p j d", j=JT)).then_inc(sm[f"x{b}"], 16)

            def load_w1(t, src):
                if not isinstance(t, int) or t > 0:
                    sp.wait_ge(sm["wt_ps"], 8 * t - 4)
                sp.dma_start(raws[0].rearrange("p (c d) -> p c d", c=KH), src).then_inc(raw_in[0], 16)

            def load_w2(t, src):
                if not isinstance(t, int) or t > 0:
                    sp.wait_ge(sm["wt_ps"], 8 * t)
                sp.dma_start(raws[1].rearrange("p (a h) -> p a h", a=KD), src).then_inc(raw_in[1], 16)

            load_w1(0, sw1.rearrange("(c p) d -> p c d", p=P))
            load_w2(0, sw2.rearrange("(a p) h -> p a h", p=P))
            def load_expert_w1(t):
                load_w1(t, ew1[bass.ds(t - 1, 1)].rearrange("a (c p) d -> p (a c) d", p=P))

            def load_expert_w2(t):
                load_w2(t, ew2[bass.ds(t - 1, 1)].rearrange("a (q p) h -> p (a q) h", p=P))

            def store_rows(z, w, zrow):
                sp.wait_ge(sm["z_lo"], AHEAD + z + 1)
                sp.dma_start(rows_dram[bass.ds(z * P, P), :], zrow[:, w, :]).then_inc(rows_st[w], 16)

            for q in range(4):
                sp.sem_inc(rows_st[q], 4 * AHEAD)
            for t in (1, 2):
                load_expert_w1(t)
                load_expert_w2(t)
            with sp.Fori(1, B) as b:
                load_expert_w1(2 * b + 1)
                load_expert_w2(2 * b + 1)
                load_expert_w1(2 * b + 2)
                for q in range(4):
                    store_rows(b * JT - JT + q, q, ln_beside[2])
                load_expert_w2(2 * b + 2)
                for q in range(4):
                    store_rows(b * JT - JT + 4 + q, q, ln_beside[2])
            for z in range(LAST, NT):
                store_rows(z, z % 4, ln_last[2])

            def store_y(j, u):
                sp.wait_ge(sm["y_done"], j + SH1 + 1)
                sp.dma_start(y_dram[bass.ds(j * R, R), :].rearrange("(h p) d -> p h d", p=P),
                             ybuf.rearrange("p (h d) -> p h d", h=2)).then_inc(sm["y_store"], 16)

            tile_pairs(sp, 0, ROUTED, store_y)
            for i in range(0, NT, 2):
                sp.wait_ge(sm["comb_done"], i + 2)
                if i // 2 >= SH1:
                    sp.wait_ge(sm["y_done"], ROUTED + i // 2 + 1)
                b, j = i // JT, i % JT
                sp.dma_start(out[b].rearrange("(p j) d -> p j d", j=JT)[:, j:j + 2, :],
                             xres[:, i:i + 2, :]).then_inc(sm["out_st"], 16)
            sp.wait_ge(sm["out_st"], 16 * NT // 2)

        @block.gpsimd
        def _(pool):
            n = [0]

            def link(ins):
                n[0] += 1
                ins.then_inc(sm["pchain"], 1)
                pool.wait_ge(sm["pchain"], n[0])

            link(pool.memset(identf[:, :], 0.0))
            pool.affine_select(out=identf[:, :], in_=identf[:, :], compare_op=ALU.not_equal, fill=1.0,
                               base=0, pattern=[[-1, P]], channel_multiplier=1).then_inc(sm["const_ready"], 1)
            link(pool.memset(ident16[:, :], 0.0))
            link(pool.affine_select(out=ident16[:, :], in_=ident16[:, :], compare_op=ALU.not_equal, fill=1.0,
                                    base=0, pattern=[[-1, P]], channel_multiplier=1))
            link(pool.memset(ones_b[:, :], 1.0))
            link(pool.affine_select(out=upper[:, :], in_=ones_b[:, :], compare_op=ALU.is_gt, fill=0.0,
                                    base=0, pattern=[[1, P]], channel_multiplier=-1))
            pool.iota(iota_b[:, :], pattern=[[1, P]], base=0, channel_multiplier=0,
                      allow_small_or_imprecise_dtypes=True).then_inc(sm["const_ready"], 1)
            pool.iota(iota_p[:, :], pattern=[[1, 1]], base=0, channel_multiplier=1,
                      allow_small_or_imprecise_dtypes=True).then_inc(sm["const_ready"], 1)
            pool.iota(efirst[:, :], pattern=[[-1, E]], base=E, channel_multiplier=0,
                      allow_small_or_imprecise_dtypes=True).then_inc(sm["const_ready"], 1)
            pool.memset(woff[:, :], 0).then_inc(sm["const_ready"], 1)
            for t_, n_ in ((iot, ROUTED), (ioe, E)):
                pool.iota(t_[:, :], pattern=[[1, n_]], base=0, channel_multiplier=0,
                          allow_small_or_imprecise_dtypes=True).then_inc(sm["const_ready"], 1)

            def across(t, m):
                pool.wait_ge(sm["raw_sq"], 2 * t + m + 1)
                if not isinstance(t, int) or t > 0:
                    pool.wait_ge(sm["scale_ready"], 2 * t + m - 1)
                alone(pool)
                pool.partition_all_reduce(asq[:, m:m + 1], psq[:, m:m + 1], P, SUM)\
                    .then_inc(sm["all_sq"], 1)

            across(0, 0)
            across(0, 1)
            with pool.Fori(1, NS) as t:
                across(t, 0)
                across(t, 1)

            for q in range(4):
                pool.wait_ge(rows_st[q], 4 * (AHEAD + LAST))

            def rows_in_order(i, tau, u):
                pool.wait_ge(sm["xg_t"], tau)
                alone(pool)
                pool.dma_start(xg[:, :, :], rows_dram[bass.ds(i * R, R), :].rearrange("(h p) d -> p h d", p=P))\
                    .then_inc(sm["rows_in"], 32)

            def rows_by_slot(j, u):
                pool.wait_ge(sm["xg_t"], j + SH1)
                alone(pool)
                pool.tensor_copy(idx[:, :], tok[:, bass.ds(2 * j, 2)]).then_inc(sm["idx_ready"], 1)
                pool.wait_ge(sm["idx_ready"], j + 1)
                alone(pool)
                for h in range(2):
                    pool.indirect_dma_start(xg[:, h, :], None, rows_dram,
                                            bass.IndirectOffsetOnAxis(idx[:, h:h + 1], 0))\
                        .then_inc(sm["rows_in"], 16)

            pool.dma_start(xg[:, :, :], rows_dram[0:R, :].rearrange("(h p) d -> p h d", p=P))\
                .then_inc(sm["rows_in"], 32)
            tile_pairs(pool, 1, SH1, lambda i, u: rows_in_order(i, i, u))
            for q in range(4):
                pool.wait_ge(rows_st[q], 4 * (AHEAD + NT))
            pool.wait_ge(sm["routed_ready"], 1)
            tile_pairs(pool, 0, ROUTED, rows_by_slot)

            def gather_outputs(i):
                q = i % 4
                if i >= 4:
                    pool.wait_ge(sm["comb_done"], i - 3)
                for k in range(2):
                    pool.indirect_dma_start(grow[:, q, k, :], None, y_dram,
                                            bass.IndirectOffsetOnAxis(slot_u[:, k, i:i + 1], 0))\
                        .then_inc(grow_in[q], 16)

            def back_tile(m):
                rows_in_order(SH1 + m, SH1 + ROUTED + m, 0)

            back_tile(0)
            back_tile(1)
            pool.wait_ge(sm["y_store"], 16 * ROUTED)
            for m in range(1, SH2):
                if m + 1 < SH2:
                    back_tile(m + 1)
                for i in combined(m):
                    gather_outputs(i)
            for i in combined(SH2):
                gather_outputs(i)

        @block.tensor
        def _(pe):
            pe.wait_ge(sm["const_ready"], 1)
            pe.wait_ge(sm["c_in"], 16 * 2 * B)
            n = [0]

            def bank_read(step):
                batch, part = divmod(step - 9, 3)
                if step < 9:
                    pe.wait_ge(sm["su_ev"], step + 1)
                elif part < 2:
                    pe.wait_ge(sm["su_ev"], 9 + 2 * batch + part + 1)
                else:
                    pe.wait_ge(sm["values_ready"], batch + 1)

            def bank():
                b = n[0] % 4
                if n[0] >= 4:
                    bank_read(n[0] - 4)
                n[0] += 1
                return ps[b]

            for b in range(B):
                q = bank()
                for k in range(KD):
                    pe.transpose(q[:, k * 256:k * 256 + P], craw[:, b, 0, k * P:(k + 1) * P], identf[:, :])
                    last = pe.transpose(q[:, k * 256 + P:k * 256 + C], craw[0:C2, b, 1, k * P:(k + 1) * P],
                                        identf[0:C2, 0:C2])
                last.then_inc(sm["su_pe"], 1)
            pe.wait_ge(sm["w_in"], 64)
            pe.wait_ge(sm["b_in"], 64)
            q = bank()
            for c in range(2):
                for r in range(2):
                    last = pe.transpose(q[:, c * 256 + r * P:c * 256 + (r + 1) * P],
                                        rawo[:, r, c:D:2], identf[:, :])
            last.then_inc(sm["su_pe"], 1)
            q = bank()
            for a in range(KD):
                for c in range(2):
                    last = pe.matmul(q[:, a * 256:(a + 1) * 256], rawk[:, c, a * P:(a + 1) * P], rawq[:, c, :],
                                     start=(c == 0), stop=(c == 1))
            last.then_inc(sm["su_pe"], 1)
            q = bank()
            for a in range(KD):
                for c in range(2):
                    pe.matmul(q[:, a:a + 1], rawk[:, c, a * P:(a + 1) * P], bq_c[:, c:c + 1],
                              start=(c == 0), stop=(c == 1))
            for k in range(KD):
                last = pe.transpose(q[:, 16 + k * E:16 + (k + 1) * E], graw[:, k * P:(k + 1) * P],
                                    identf[0:E, 0:E])
            last.then_inc(sm["su_pe"], 1)
            pe.wait_ge(sm["su_ev"], 5)
            q = bank()
            for a in range(KD):
                for c in range(2):
                    last = pe.matmul(q[:, a * 256:(a + 1) * 256], rawv[:, c, a * P:(a + 1) * P], woT[:, c, :],
                                     start=(c == 0), stop=(c == 1))
            last.then_inc(sm["su_pe"], 1)
            q = bank()
            pe.wait_ge(sm["bv_bc"], 1)
            for c in range(2):
                pe.matmul(q[:, 0:D], bvbc[:, c, :], woT[:, c, :], start=(c == 0), stop=False)
            pe.matmul(q[:, 0:D], ones_f[0:1, :], bo_r, start=False, stop=True).then_inc(sm["su_pe"], 1)
            for b in range(B):
                q = bank()
                pe.wait_ge(sm["su_ev"], 6)
                for r in range(KD):
                    for a in range(KD):
                        last = pe.matmul(q[:, r * 256:r * 256 + C], fa[:, a, r * P:(r + 1) * P],
                                         ctxT[:, b, a, :], start=(a == 0), stop=(a == 1))
                last.then_inc(sm["su_pe"], 1)
                q = bank()
                pe.wait_ge(sm["u_bc"], 1)
                for a in range(KD):
                    last = pe.matmul(q[:, 0:C], ubc[:, a, :], ctxT[:, b, a, :], start=(a == 0), stop=(a == 1))
                last.then_inc(sm["su_pe"], 1)
                q = bank()
                pe.wait_ge(sm["su_ev"], 9)
                for r, rows in ((0, P), (1, C2)):
                    for a in range(KD):
                        last = pe.matmul(q[0:rows, r * 256:(r + 1) * 256], ctxT[:, b, a, r * P:r * P + rows],
                                         fc[:, a, :], start=(a == 0), stop=(a == 1))
                last.then_inc(sm["su_pe"], 1)
            bank_read(n[0] - 2)
            bank_read(n[0] - 1)

            def transpose_x(i, u):
                pe.wait_ge(sm["xn_done"], i + 1)
                if not isinstance(i, int) or i > 0:
                    pe.wait_ge(sm["xnt_done"], i)
                for k in range(KD):
                    last = pe.transpose(pXT[:, k * P:(k + 1) * P], xn[:, u, k * P:(k + 1) * P], identf[:, :])
                last.then_inc(sm["xt_ps"], 1)

            def scores(i, u, b):
                pe.wait_ge(sm["xnt_done"], i + 1)
                if not isinstance(i, int) or i > 0:
                    pe.wait_ge(sm["sc_done"], i)
                for k in range(KD):
                    last = pe.matmul(pSC[:, 0:C], xnT[:, u, k, :],
                                     ktn[:, bass.ds(b, 1), k, :].rearrange("p a c -> p (a c)"),
                                     start=(k == 0), stop=(k == 1))
                last.then_inc(sm["sc_ps"], 1)

            def transpose_p(i, u):
                pe.wait_ge(sm["exp_done"], i + 1)
                if not isinstance(i, int) or i > 0:
                    pe.wait_ge(sm["ptt_done"], 2 * i)
                pe.transpose(pPT[:, 0:P], sc[:, u, 0:P], identf[:, :])
                pe.transpose(pPT[0:C2, P:2 * P], sc[:, u, P:C], identf[:, :]).then_inc(sm["pt_ps"], 1)

            def values(i, u, b):
                pe.wait_ge(sm["ptt_done"], 2 * i + 2)
                if not isinstance(i, int) or i > 0:
                    pe.wait_ge(sm["x2_done"], i)
                pe.matmul(pPV[:, 0:D], pT[:, u, 0, :], vct[:, bass.ds(b, 1), 0, :].rearrange("p a d -> p (a d)"),
                          start=True, stop=False)
                pe.matmul(pPV[:, 0:D], pT[0:C2, u, 1, :],
                          vct[0:C2, bass.ds(b, 1), 1, :].rearrange("p a d -> p (a d)"),
                          start=False, stop=True).then_inc(sm["pv_ps"], 1)

            def weight_bank(t, g):
                q = pW[g]
                m = g // 4
                if g % 4 == 0:
                    pe.wait_ge(raw_in[m], 16 * t + 16)
                if g >= 3 or not isinstance(t, int) or t > 0:
                    pe.wait_ge(sm["wlo"], 8 * t + g + 1 - W_BACK[g])
                for r in range(4):
                    if m == 0:
                        k, c = g // 2, (g % 2) * 4 + r
                        src = raws[0][:, c * D + k * P:c * D + (k + 1) * P]
                    else:
                        c, a = 2 * (g - 4) + r // 2, r % 2
                        src = raws[1][:, a * HID + c * P:a * HID + (c + 1) * P]
                    last = pe.transpose(q[:, r * P:(r + 1) * P], src, identf[:, :])
                last.then_inc(sm["wt_ps"], 1)

            TRANSFERS = ((None, 0, 1), (2, 3, None), (4, 5, None), (6, 7, None))

            def step(i, t, s, b1, b3, beside=lambda place: None):
                start, middle, end = TRANSFERS[s]
                transpose_x(i, s % 2)
                if start is not None:
                    weight_bank(t, start)
                if not isinstance(i, int) or i >= 1:
                    scores(i - 1, (s - 1) % 2, b1)
                if not isinstance(i, int) or i >= 2:
                    transpose_p(i - 2, s % 2)
                weight_bank(t, middle)
                beside(0)
                if not isinstance(i, int) or i >= 3:
                    values(i - 3, (s - 3) % 2, b3)
                if end is not None:
                    weight_bank(t, end)
                beside(1)

            def transpose_z(z, w, bufs):
                pe.wait_ge(sm["z_done"], z + 1)
                for k in range(KD):
                    last = pe.transpose(pZT[:, k * P:(k + 1) * P],
                                        bufs[0][:, w % 2, k * P:(k + 1) * P], identf[:, :])
                last.then_inc(sm["zt_ps"], 1)

            def logits(z, w, bufs):
                pe.wait_ge(sm["ztt_done"], AHEAD + z + 1)
                for k in range(KD):
                    last = pe.matmul(pLG[:, bass.ds(z * E, E)], bufs[1][:, w % 2, k, :], gateT[:, k, :],
                                     start=(k == 0), stop=(k == 1))
                last.then_inc(sm["lg_ps"], 1)

            pe.sem_inc(sm["zt_ps"], AHEAD)
            pe.sem_inc(sm["lg_ps"], AHEAD)
            for i in range(JT):
                step(i, i // 4, i % 4, 0, 0)
            with pe.Fori(1, B) as b:
                for j in range(JT):
                    def beside(place):
                        w = 2 * (j - 4) + place
                        z = b * JT - JT + w
                        if w > 0:
                            logits(z - 1, w - 1, ln_beside)
                        if w >= 0 and j >= 4:
                            transpose_z(z, w, ln_beside)

                    step(b * JT + j, b * (JT // 4) + j // 4, j % 4, b if j >= 1 else b - 1,
                         b if j >= 3 else b - 1, beside)
                logits(b * JT - 1, JT - 1, ln_beside)
            for i in range(NT, NT + 3):
                if i - 1 < NT:
                    scores(i - 1, (i - 1) % 2, B - 1)
                if i - 2 < NT:
                    transpose_p(i - 2, i % 2)
                values(i - 3, (i - 3) % 2, B - 1)

            def transpose_rows(tau, u):
                pe.wait_ge(sm["rows_in"], 32 * tau + 32)
                if not isinstance(tau, int) or tau > 0:
                    pe.wait_ge(sm["xt_done"], tau)
                if isinstance(tau, int) and tau == 1:
                    pe.wait_ge(sm["wlo"], 8 * NS)
                for h in range(2):
                    for s in range(2):
                        for k in range(KD):
                            last = pe.transpose(pT16[:, s, k, h * P:(h + 1) * P],
                                                xg[:, h, s * D + k * P:s * D + (k + 1) * P], ident16[:, :])
                last.then_inc(sm["xg_t"], 1)

            def up(tau, u, g, off):
                n = BANKS * tau + g
                if g == 0:
                    pe.wait_ge(sm["xt_done"], tau + 1)
                if not isinstance(tau, int) or tau > 0:
                    pe.wait_ge(sm["silu_done"], n - BANKS + 1)
                for r in range(CB):
                    c = g * CB + r
                    first = True
                    for k in range(KD):
                        for sw, sx in ((0, 0), (0, 1), (1, 0)):
                            last = pe.matmul(pH[g][:, r * R:(r + 1) * R], w1_part(off, sw, k, c * P, P),
                                             xT[:, u, sx, k, :], start=first, stop=(k == 1 and sw == 1))
                            first = False
                last.then_inc(sm["h_ps"], 1)

            def down(tau, g, off):
                pe.wait_ge(sm["lo_done"], BANKS * tau + g + 1)
                if g == 0 and (not isinstance(tau, int) or tau > 0):
                    pe.wait_ge(sm["y_done"], tau)
                for r in range(CB):
                    c = g * CB + r
                    for sw, sh in ((0, 0), (0, 1), (1, 0)):
                        for h in range(2):
                            first = g == 0 and r == 0 and sw == 0 and sh == 0
                            last = pe.matmul(
                                pY[:, h * D:(h + 1) * D],
                                hring[:, g, sh, r * R + h * P:r * R + (h + 1) * P],
                                w2_part(off, sw, c), start=first and h == 0,
                                stop=(g == BANKS - 1 and r == CB - 1 and sw == 1), skip_group_check=True)
                last.then_inc(sm["y_ps"], 1)

            def offset(tau):
                if isinstance(tau, int) and (tau < SH1 or tau >= SH1 + ROUTED):
                    return 0
                return pe.value_load(woff[0:1, bass.ds(tau, 1)], min_val=0, max_val=E * SLOT)

            def ffn(tau, u, now, before, more=True, beside=lambda g: None):
                off = now(tau)
                up(tau, u, 0, off)
                beside(0)
                if before is not None:
                    old = before(tau - 1)
                    down(tau - 1, 2, old)
                up(tau, u, 1, off)
                beside(1)
                if before is not None:
                    down(tau - 1, 3, old)
                if more:
                    transpose_rows(tau + 1, 1 - u)
                up(tau, u, 2, off)
                beside(2)
                down(tau, 0, off)
                up(tau, u, 3, off)
                beside(3)
                down(tau, 1, off)

            def fixed(tau):
                return 0

            def count():
                mask = slotf[:, 0:128].bitcast(BF16)
                pe.wait_ge(sm["mask_ready"], 1)
                pe.matmul(pPre[:, 0:NT * E], upper[:, :], mask, start=True, stop=True)
                pe.matmul(pTot[:, 0:NT * E], ones_b[:, :], mask, start=True, stop=True)\
                    .then_inc(sm["count_ps"], 1)

            def invert(c):
                pe.wait_ge(sm["oneh_ready"], c + 1)
                for q in range(RC):
                    for h in range(2):
                        last = pe.matmul(pTok[:, h * HALVES:(h + 1) * HALVES], oh_pos[:, q, :],
                                         oh_row[h][:, q, :], start=(c == 0 and q == 0 and h == 0),
                                         stop=(c == CHUNKS - 1 and q == RC - 1), skip_group_check=True)
                last.then_inc(sm["tok_ps"], 1)

            pe.wait_ge(sm["const_ready"], CONSTANTS)
            pe.wait_ge(sm["wlo"], 8 * (NS - 1))
            transpose_rows(0, 0)
            for g in range(4):
                if g == 1:
                    pe.wait_ge(sm["xt_done"], 1)
                weight_bank(NS - 1, g)

            def beside_first(tau, g):
                if tau == 0 and g < 2:
                    for q in (0, 1):
                        weight_bank(NS - 1, 4 + 2 * g + q)
                z = last_norm(tau, g)
                if z is not None:
                    if z > LAST:
                        logits(z - 1, (z - 1) % 4, ln_last)
                    if z < NT:
                        transpose_z(z, z % 4, ln_last)

            ffn(0, 0, fixed, None, beside=lambda g: beside_first(0, g))
            for tau in range(1, SH1):
                ffn(tau, tau % 2, fixed, fixed, more=tau < SH1 - 1, beside=lambda g: beside_first(tau, g))
                if tau == 3:
                    count()
                if 5 <= tau < 5 + CHUNKS:
                    invert(tau - 5)
            transpose_rows(SH1, SH1 % 2)
            pe.wait_ge(sm["routed_ready"], 1)
            ffn(SH1, SH1 % 2, offset, fixed)
            tile_pairs(pe, SH1 + 1, SH1 + ROUTED, lambda tau, u: ffn(tau, u, offset, offset))
            tau = SH1 + ROUTED
            ffn(tau, tau % 2, fixed, offset)
            tile_pairs(pe, tau + 1, NF - 1, lambda tau, u: ffn(tau, u, fixed, fixed))
            ffn(NF - 1, (NF - 1) % 2, fixed, fixed, more=False)
            down(NF - 1, 2, 0)
            down(NF - 1, 3, 0)

        @block.scalar
        def _(act):
            def take(step):
                act.wait_ge(sm["su_pe"], step + 1)
                return ps[step % 4]

            for b in range(B):
                q = take(b)
                act.activation(ctxT[:, b, :, :], q[:, :].rearrange("p (k n) -> p k n", k=2)[:, :, 0:C],
                               ACT.Copy).then_inc(sm["su_ev"], 1)
            q = take(4)
            act.activation(woT.rearrange("p c d -> p (c d)"), q[:, :], ACT.Copy).then_inc(sm["su_ev"], 1)
            q = take(5)
            act.activation(fa.rearrange("p c d -> p (c d)"), q[:, :], ACT.Copy).then_inc(sm["su_ev"], 1)
            q = take(6)
            act.activation(u_c, q[:, 0:2], ACT.Copy).then_inc(sm["u_ready"], 1)
            act.activation(gateT[:, :, :].rearrange("p k e -> p (k e)"), q[:, 16:16 + 2 * E], ACT.Copy)\
                .then_inc(sm["su_ev"], 1)
            q = take(7)
            act.activation(fc.rearrange("p c d -> p (c d)"), q[:, :], ACT.Copy).then_inc(sm["su_ev"], 1)
            q = take(8)
            act.activation(cbs, q[:, 0:D], ACT.Copy).then_inc(sm["su_ev"], 1)
            for b in range(B):
                q = take(9 + 3 * b)
                act.activation(ktn[:, b, :, :], q[:, :].rearrange("p (k n) -> p k n", k=2)[:, :, 0:C],
                               ACT.Copy, scale=NEG_SCALE).then_inc(sm["su_ev"], 1)
                q = take(10 + 3 * b)
                act.activation(biasn[:, b, :], q[:, 0:C], ACT.Copy, scale=NEG_SCALE).then_inc(sm["su_ev"], 1)

            def x_to_sbuf(i, u):
                act.wait_ge(sm["xt_ps"], i + 1)
                if not isinstance(i, int) or i >= 2:
                    act.wait_ge(sm["sc_ps"], i - 1)
                act.activation(xnT[:, u, :, :].rearrange("p k t -> p (k t)"), pXT[:, 0:D], ACT.Copy)\
                    .then_inc(sm["xnt_done"], 1)

            def exponentials(i, u, r):
                act.wait_ge(sm["sc_done"], i + 1)
                act.activation(sc[:, u, :], sc[:, u, :], ACT.Exp, bias=negmax[:, u:u + 1], scale=-1.0,
                               accum_out=rowsum[:, r:r + 1]).then_inc(sm["exp_done"], 1)

            def p_to_sbuf(i, u):
                act.wait_ge(sm["pt_ps"], i + 1)
                if not isinstance(i, int) or i >= 2:
                    act.wait_ge(sm["pv_ps"], i - 1)
                act.activation(pT[:, u, 0, :], pPT[:, 0:P], ACT.Copy).then_inc(sm["ptt_done"], 1)
                act.activation(pT[0:C2, u, 1, :], pPT[0:C2, P:2 * P], ACT.Copy).then_inc(sm["ptt_done"], 1)

            def weight_high(t, g):
                m, q = g // 4, pW[g]
                if g % 4 == 0:
                    act.wait_ge(sm["scale_ready"], 2 * t + m + 1)
                act.wait_ge(sm["wt_ps"], 8 * t + g + 1)
                alone(act)
                at = t * SLOT + (m * 2 * KD * HID) + (g % 4) * 512
                act.activation(wflat[:, bass.ds(at, 512)], q[:, :], ACT.Copy,
                               scale=wscale[:, m, bass.ds(t, 1)]).then_inc(sm["whi"], 1)

            def raw_squares(t, m):
                act.wait_ge(raw_in[m], 16 * t + 16)
                if not isinstance(t, int) or t > 0:
                    act.wait_ge(sm["all_sq"], 2 * t + m - 1)
                if not isinstance(t, int) or 2 * t + m > 0:
                    act.wait_ge(sm["raw_sq"], 2 * t + m)
                act.activation(squares, raws[m], ACT.Square, accum_out=psq[:, m:m + 1])\
                    .then_inc(sm["raw_sq"], 1)

            def normalize(i, u):
                if not isinstance(i, int) or i >= 2:
                    act.wait_ge(sm["xt_ps"], i - 1)
                alone(act)
                act.activation(xn[:, u, :], xres[:, bass.ds(i, 1), :].rearrange("p a d -> p (a d)"),
                               ACT.Identity, bias=nmr[:, bass.ds(i, 1)], scale=rstd[:, bass.ds(i, 1)])\
                    .then_inc(sm["xn_done"], 1)

            def high(z, w, bufs):
                act.wait_ge(sm["z_done"], z + 1)
                act.wait_ge(rows_st[w % 4], 4 * (AHEAD + z - w % 4))
                act.activation(bufs[2][:, w % 4, 0:D], bufs[0][:, w % 2, :], ACT.Copy).then_inc(sm["z_hi"], 1)

            def z_to_sbuf(z, w, bufs):
                act.wait_ge(sm["zt_ps"], AHEAD + z + 1)
                act.wait_ge(sm["lg_ps"], AHEAD + z - 1)
                act.activation(bufs[1][:, w % 2, :, :].rearrange("p k t -> p (k t)"), pZT, ACT.Copy)\
                    .then_inc(sm["ztt_done"], 1)

            def att(i, b, j):
                one = not isinstance(i, int)
                s = j % 4
                beside_ln = j >= 4 and (one or i >= JT)
                t, tp = b * (JT // 4) + j // 4, b * (JT // 4) + (j - 1) // 4
                if one or i < NT:
                    x_to_sbuf(i, s % 2)
                if one or 0 < i <= NT:
                    weight_high(tp, 2 * ((j - 1) % 4) + 1)
                if one or i + 1 < NT:
                    normalize(i + 1, (s + 1) % 2)
                if one or 0 <= i - 1 < NT:
                    exponentials(i - 1, (s - 1) % 2, (s - 1) % 4)
                z, w = b * JT - JT + 2 * (j - 4), 2 * (j - 4)
                if beside_ln:
                    high(z, w, ln_beside)
                    high(z + 1, w + 1, ln_beside)
                    z_to_sbuf(z, w, ln_beside)
                if one or 0 <= i - 2 < NT:
                    p_to_sbuf(i - 2, s % 2)
                if one or i < NT:
                    weight_high(t, 2 * s)
                    if s == 1:
                        raw_squares(t, 1)
                    if s == 3:
                        raw_squares(t + 1, 0)
                if beside_ln:
                    z_to_sbuf(z + 1, w + 1, ln_beside)

            act.sem_inc(sm["ztt_done"], AHEAD)
            act.wait_ge(sm["norm1_ready"], 1)
            raw_squares(0, 0)
            normalize(0, 0)
            for j in range(JT):
                att(j, 0, j)
            with act.Fori(1, B - 1) as b:
                for j in range(JT):
                    att(b * JT + j, b, j)
            for j in range(JT):
                att(LAST + j, B - 1, j)
            for j in range(2):
                att(NT + j, B, j)
            raw_squares(NS - 1, 1)
            act.wait_ge(sm["x2_done"], NT)
            for g in range(4):
                weight_high(NS - 1, g)
            def hidden(tau, u, beside=lambda g: None):
                for g in range(BANKS):
                    n = BANKS * tau + g
                    act.wait_ge(sm["h_ps"], n + 1)
                    if not isinstance(tau, int) or n >= 2:
                        act.wait_ge(sm["lo_done"], n - 1)
                    alone(act)
                    act.activation(sring[:, g % 2, :], pH[g][:, :], ACT.Silu,
                                   scale=tab[:, 0, bass.ds(tau, 1)]).then_inc(sm["silu_done"], 1)
                    act.wait_ge(sm["silu_done"], n + 1)
                    if not isinstance(tau, int) or tau > 0:
                        act.wait_ge(sm["y_ps"], n - BANKS + 1)
                    alone(act)
                    act.activation(hring[:, g, 0, :], sring[:, g % 2, :], ACT.Copy,
                                   scale=tab[:, 1, bass.ds(tau, 1)]).then_inc(sm["hi_done"], 1)
                    beside(g)

            def beside_first(tau, g):
                if tau == 0 and g < 2:
                    for q in (0, 1):
                        weight_high(NS - 1, 4 + 2 * g + q)
                z = last_norm(tau, g)
                if z is not None and z < NT:
                    high(z, z % 4, ln_last)
                    z_to_sbuf(z, z % 4, ln_last)

            act.wait_ge(sm["tabs0"], 1)
            for tau in range(3):
                hidden(tau, tau % 2, lambda g: beside_first(tau, g))
            tile_pairs(act, 3, SH1 - 1, hidden)
            act.wait_ge(sm["gate_diff"], 1)
            act.activation(ex, m2, ACT.Exp, scale=1.0 / ROW_SCALE).then_inc(sm["gate_exp"], 1)
            hidden(SH1 - 1, (SH1 - 1) % 2)
            act.wait_ge(sm["routed_ready"], 1)
            tile_pairs(act, SH1, SH1 + ROUTED, hidden)
            tile_pairs(act, SH1 + ROUTED, NF, hidden)

        @block.vector
        def _(dve):
            n = [0]

            def link(ins):
                n[0] += 1
                ins.then_inc(sm["dchain"], 1)
                dve.wait_ge(sm["dchain"], n[0])

            def moments(at, n, target, step):
                st, mu = stats[:, bass.ds(at, n), :], mean[:, bass.ds(at, n)]
                y, a, v, b = rstd[:, bass.ds(at, n)], nt_a[:, 0:n], nt_v[:, 0:n], nt_b[:, 0:n]
                step(dve.tensor_tensor(a, st[:, :, 1], st[:, :, 4], ALU.add))
                step(dve.tensor_scalar(mu, a, 0.5, None, ALU.mult))
                step(dve.tensor_tensor(a, st[:, :, 1], st[:, :, 4], ALU.subtract))
                step(dve.scalar_tensor_tensor(out=b, in0=a, scalar=0.25, in1=a, op0=ALU.mult, op1=ALU.mult))
                step(dve.tensor_tensor(v, st[:, :, 2], st[:, :, 5], ALU.add))
                step(dve.scalar_tensor_tensor(out=v, in0=v, scalar=1.0 / D, in1=b, op0=ALU.mult, op1=ALU.add))
                step(dve.tensor_scalar(v, v, EPS, None, ALU.add))
                step(dve.tensor_scalar(a.bitcast(I32), v.bitcast(I32), 1, None, ALU.logical_shift_right))
                step(dve.tensor_scalar(b.bitcast(I32), a.bitcast(I32), -1.0, float(0x5F3759DF),
                                       ALU.mult, ALU.add))
                for q in range(3):
                    step(dve.scalar_tensor_tensor(out=a, in0=b, scalar=-0.5, in1=b, op0=ALU.mult, op1=ALU.mult))
                    step(dve.tensor_tensor(a, a, v, ALU.mult))
                    step(dve.scalar_tensor_tensor(out=b, in0=a, scalar=1.5, in1=b, op0=ALU.add, op1=ALU.mult))
                step(dve.tensor_scalar(y, b, target, None, ALU.mult))

            def row(i):
                return xres[:, bass.ds(i, 1), :].rearrange("p a d -> p (a d)")

            dve.memset(ones_f, 1.0).then_inc(sm["ones_ready"], 1)
            dve.wait_ge(sm["ones_ready"], 1)
            dve.wait_ge(sm["b_in"], 64)
            link(dve.tensor_scalar(bvbc[:, 0, :], ones_f, bv_c[:, 0:1], None, ALU.mult))
            dve.tensor_scalar(bvbc[:, 1, :], ones_f, bv_c[:, 1:2], None, ALU.mult).then_inc(sm["bv_bc"], 1)
            for i in range(NT):
                if i % JT == 0:
                    dve.wait_ge(sm[f"x{i // JT}"], 16)
                last = dve.bn_stats(stats[:, i, :], xres[:, i, :])
            link(last)
            dve.wait_ge(sm["u_ready"], 1)
            link(dve.tensor_scalar(ubc[:, 0, :], ones_f, u_c[:, 0:1], None, ALU.mult))
            dve.tensor_scalar(ubc[:, 1, :], ones_f, u_c[:, 1:2], None, ALU.mult).then_inc(sm["u_bc"], 1)
            moments(0, NT, 1.0, link)
            dve.scalar_tensor_tensor(out=nmr[:, :], in0=mean[:, :], scalar=-1.0, in1=rstd[:, :],
                                     op0=ALU.mult, op1=ALU.mult).then_inc(sm["norm1_ready"], 1)
            for b in range(B):
                dve.wait_ge(sm["su_pe"], 9 + 3 * b + 3)
                q = ps[(11 + 3 * b) % 4]
                dve.wait_ge(sm["su_ev"], 9)
                link(dve.tensor_tensor(vct[:, b, 0, :], q[:, 0:D], cbs, ALU.add))
                dve.tensor_tensor(vct[0:C2, b, 1, :], q[0:C2, D:2 * D], cbs[0:C2, :], ALU.add)\
                    .then_inc(sm["values_ready"], 1)

            def scale(t, m):
                dve.wait_ge(sm["all_sq"], 2 * t + m + 1)
                q = 2 * (2 * t + m)
                dve.tensor_scalar(ebits[:, 0:1], asq[:, m:m + 1].bitcast(I32), 24, None,
                                  ALU.logical_shift_right).then_inc(sm["scale_step"], 1)
                dve.wait_ge(sm["scale_step"], q + 1)
                dve.tensor_scalar(ebits[:, 1:2], ebits[:, 0:1], 17.0, -float(1 << 23), ALU.max, ALU.mult)\
                    .then_inc(sm["scale_step"], 1)
                dve.wait_ge(sm["scale_step"], q + 2)
                dve.tensor_scalar(wscale[:, m, bass.ds(t, 1)].bitcast(I32), ebits[:, 1:2], float(204 << 23),
                                  None, ALU.add).then_inc(sm["scale_ready"], 1)
                dve.wait_ge(sm["scale_ready"], 2 * t + m + 1)

            def weight_low(t, g):
                m, q = g // 4, pW[g]
                at = t * SLOT + (m * 2 * KD * HID) + (g % 4) * 512
                dve.wait_ge(sm["whi"], 8 * t + g + 1)
                dve.scalar_tensor_tensor(out=wflat[:, bass.ds(at + KD * HID, 512)], in0=q[:, :],
                                         scalar=wscale[:, m, bass.ds(t, 1)], in1=wflat[:, bass.ds(at, 512)],
                                         op0=ALU.mult, op1=ALU.subtract).then_inc(sm["wlo"], 1)

            def negated_scores(i, u, b):
                dve.wait_ge(sm["sc_ps"], i + 1)
                if not isinstance(i, int) or i >= 2:
                    dve.wait_ge(sm["pt_ps"], i - 1)
                dve.tensor_tensor(sc[:, u, :], pSC[:, 0:C], biasn[:, bass.ds(b, 1), :]
                                  .rearrange("p a c -> p (a c)"), ALU.add).then_inc(sm["sc_sum"], 1)
                dve.wait_ge(sm["sc_sum"], i + 1)
                dve.tensor_reduce(negmax[:, u:u + 1], sc[:, u, :], AX.X, ALU.min).then_inc(sm["sc_done"], 1)

            def add_attention(i, u, r):
                dve.wait_ge(sm["exp_done"], i + 1)
                dve.reciprocal(rinv[:, u:u + 1], rowsum[:, r:r + 1]).then_inc(sm["rinv_done"], 1)
                dve.wait_ge(sm["rinv_done"], i + 1)
                dve.wait_ge(sm["pv_ps"], i + 1)
                dve.scalar_tensor_tensor(out=row(i), in0=pPV[:, 0:D], scalar=rinv[:, u:u + 1], in1=row(i),
                                         op0=ALU.mult, op1=ALU.add).then_inc(sm["x2_done"], 1)
                dve.wait_ge(sm["x2_done"], i + 1)
                alone(dve)
                dve.bn_stats(stats[:, bass.ds(i, 1), :].rearrange("p a s -> p (a s)"), row(i))\
                    .then_inc(sm["stat_done"], 1)

            def rows_to_sbuf(tau, u):
                dve.wait_ge(sm["xg_t"], tau + 1)
                dve.tensor_copy(xT[:, u, :, :, :].rearrange("p s k t -> p (s k t)"),
                                pT16.rearrange("p s k t -> p (s k t)")).then_inc(sm["xt_done"], 1)

            def second_norm(z, w, bufs):
                dve.wait_ge(sm["zt_ps"], AHEAD + z - 1)
                dve.wait_ge(sm["z_lo"], AHEAD + z - 1)
                dve.tensor_scalar(bufs[0][:, w % 2, :], row(z), mean[:, bass.ds(z, 1)], rstd[:, bass.ds(z, 1)],
                                  ALU.subtract, ALU.mult).then_inc(sm["z_done"], 1)

            def low(z, w, bufs):
                dve.wait_ge(sm["z_hi"], z + 1)
                dve.tensor_tensor(bufs[2][:, w % 4, D:2 * D], bufs[0][:, w % 2, :], bufs[2][:, w % 4, 0:D],
                                  ALU.subtract).then_inc(sm["z_lo"], 1)

            def batch_moments(b):
                k = [0]

                def step(ins):
                    k[0] += 1
                    ins.then_inc(sm["moment_step"], 1)
                    dve.wait_ge(sm["moment_step"], b * MOMENT_STEPS + k[0])

                dve.wait_ge(sm["stat_done"], b * JT + JT)
                moments(b * JT, JT, ROW_SCALE, step)
                assert k[0] == MOMENT_STEPS

            def att(i, b, j):
                one = not isinstance(i, int)
                s, sp_ = j % 4, (j - 1) % 4
                t, tp = b * (JT // 4) + j // 4, b * (JT // 4) + (j - 1) // 4
                z, w = b * JT - JT + 2 * (j - 4), 2 * (j - 4)
                if one and j >= 4:
                    second_norm(z, w, ln_beside)
                    second_norm(z + 1, w + 1, ln_beside)
                if (one or i < NT) and s % 2 == 0:
                    scale(t, s // 2)
                if one or 0 < i <= NT:
                    weight_low(tp, 2 * sp_)
                if one or 0 <= i - 1 < NT:
                    negated_scores(i - 1, (s - 1) % 2, b if j >= 1 else b - 1)
                if one or 0 < i <= NT:
                    weight_low(tp, 2 * sp_ + 1)
                if one or 0 <= i - 3 < NT:
                    add_attention(i - 3, (s - 3) % 2, (s - 3) % 4)
                if one and j == 3:
                    batch_moments(b - 1)
                if one and j >= 4:
                    low(z, w, ln_beside)
                    low(z + 1, w + 1, ln_beside)

            dve.sem_inc(sm["z_lo"], AHEAD)
            for j in range(JT):
                att(j, 0, j)
            with dve.Fori(1, B) as b:
                for j in range(JT):
                    att(b * JT + j, b, j)
            for j in range(3):
                att(NT + j, B, j)
            rows_to_sbuf(0, 0)
            scale(NS - 1, 0)
            scale(NS - 1, 1)
            ONE2 = float(254 << 23)
            link(dve.tensor_scalar(inv1[:, :].bitcast(I32), wscale[:, 0, :].bitcast(I32), -1.0,
                                   ONE2 - float(ROW_SCALE_LOG << 23), ALU.mult, ALU.add))
            link(dve.tensor_scalar(hsc[:, :], wscale[:, 0, :], 2.0 ** -8, None, ALU.mult))
            link(dve.tensor_tensor(inv2[:, :], hsc[:, :], wscale[:, 1, :], ALU.mult))
            link(dve.tensor_scalar(inv2[:, :].bitcast(I32), inv2[:, :].bitcast(I32), -1.0, ONE2,
                                   ALU.mult, ALU.add))
            for a, z in ((0, SH1), (SH1 + ROUTED, NF)):
                for q, src in enumerate((inv1, hsc, inv2)):
                    link(dve.tensor_copy(tab[:, q, a:z], src[:, 0:1].to_broadcast([P, z - a])))
            dve.memset(ybuf[:, 0:1], 0.0).then_inc(sm["tabs0"], 1)
            for g in range(4):
                weight_low(NS - 1, g)
            batch_moments(B - 1)
            dve.wait_ge(sm["const_ready"], CONSTANTS)

            def hidden_low(tau, g):
                dve.wait_ge(sm["hi_done"], BANKS * tau + g + 1)
                dve.scalar_tensor_tensor(out=hring[:, g, 1, :], in0=sring[:, g % 2, :],
                                         scalar=tab[:, 1, bass.ds(tau, 1)], in1=hring[:, g, 0, :],
                                         op0=ALU.mult, op1=ALU.subtract).then_inc(sm["lo_done"], 1)

            def add_shared(i, tau):
                dve.wait_ge(sm["y_ps"], BANKS * tau + BANKS)
                two = xres[:, bass.ds(2 * i, 2), :].rearrange("p a d -> p (a d)")
                dve.scalar_tensor_tensor(out=two, in0=pY[:, :], scalar=inv2[:, 0:1], in1=two,
                                         op0=ALU.mult, op1=ALU.add).then_inc(sm["y_done"], 1)

            def front(tau):
                add_shared(tau, tau)

            def back(tau):
                add_shared(tau - ROUTED, tau)

            def expert_rows(tau):
                dve.wait_ge(sm["y_ps"], BANKS * tau + BANKS)
                if not isinstance(tau, int) or tau > SH1:
                    dve.wait_ge(sm["y_store"], 16 * (tau - SH1))
                dve.tensor_scalar(ybuf, pY[:, :], tab[:, 2, bass.ds(tau, 1)], None, ALU.mult)\
                    .then_inc(sm["y_done"], 1)

            def ffn(tau, u, finish, more=True, beside=lambda g: None):
                hidden_low(tau, 0)
                beside(0)
                hidden_low(tau, 1)
                beside(1)
                if finish is not None:
                    finish(tau - 1)
                if more:
                    rows_to_sbuf(tau + 1, 1 - u)
                hidden_low(tau, 2)
                beside(2)
                hidden_low(tau, 3)
                beside(3)

            def beside_first(tau, g):
                if tau == 0 and g < 2:
                    for q in (0, 1):
                        weight_low(NS - 1, 4 + 2 * g + q)
                if (tau, g) == (0, 1):
                    second_norm(LAST, 0, ln_last)
                z = last_norm(tau, g)
                if z is not None and z < NT:
                    if z + 1 < NT:
                        second_norm(z + 1, (z + 1) % 4, ln_last)
                    low(z, z % 4, ln_last)

            def over_experts(t):
                return t.rearrange("p (i a) -> p i a", a=1).to_broadcast([P, NT, E])

            def choose():
                dve.wait_ge(sm["lg_ps"], AHEAD + NT)
                link(dve.tensor_copy(lg, pLG))
                first = efirst[:, :].rearrange("p (a e) -> p a e", a=1).to_broadcast([P, NT, E])
                for src, m, sel, oh in ((lg, m1, sel1, oh1), (lg2, m2, sel2, oh2)):
                    link(dve.tensor_reduce(m, by_token(src), AX.X, ALU.max))
                    link(dve.tensor_tensor(by_token(tmp), by_token(src), over_experts(m), ALU.is_ge))
                    link(dve.tensor_tensor(by_token(tmp), by_token(tmp), first, ALU.mult))
                    link(dve.tensor_reduce(sel, by_token(tmp), AX.X, ALU.max))
                    link(dve.tensor_tensor(by_token(oh), by_token(tmp), over_experts(sel), ALU.is_equal))
                    if src is lg:
                        link(dve.scalar_tensor_tensor(out=lg2, in0=oh, scalar=-3.0e38, in1=lg,
                                                      op0=ALU.mult, op1=ALU.add))
                link(dve.tensor_tensor(m2, m2, m1, ALU.subtract))
                dve.memset(rmask, 1.0).then_inc(sm["gate_diff"], 1)
                dve.tensor_tensor(by_expert(slotf[:, 0:128].bitcast(BF16)),
                                  oh1.rearrange("p (i e) -> p e i", e=E),
                                  oh2.rearrange("p (i e) -> p e i", e=E), ALU.add)\
                    .then_inc(sm["mask_ready"], 1)

            def places():
                ones_e, ct, cinc, base = (esm[:, q, :] for q in range(4))
                dve.wait_ge(sm["gate_diff"], 1)
                link(dve.memset(by_expert(rmask)[:, :, 0:1], 0.0))
                link(dve.memset(ones_e, 1.0))
                dve.wait_ge(sm["count_ps"], 1)
                link(dve.tensor_tensor_scan(incl, rmask, pTot[:, 0:NT * E], 0.0, ALU.mult, ALU.add))
                link(dve.tensor_scalar(cnt_i[:, :], by_expert(incl)[:, :, NT - 1], float(R - 1), None, ALU.add))
                link(dve.tensor_scalar(cnt_i[:, :], cnt_i[:, :], R.bit_length() - 1, None,
                                       ALU.logical_shift_right))
                link(dve.tensor_copy(ct, cnt_i[:, :]))
                link(dve.tensor_tensor_scan(cinc, ones_e, ct, 0.0, ALU.mult, ALU.add))
                link(dve.tensor_tensor(base, cinc, ct, ALU.subtract))
                link(dve.tensor_scalar(base, base, float(R), None, ALU.mult))
                link(dve.tensor_tensor(slotf, incl, pTot[:, 0:NT * E], ALU.subtract))
                link(dve.tensor_tensor(slotf, slotf, pPre[:, 0:NT * E], ALU.add))
                link(dve.tensor_tensor(by_expert(slotf), by_expert(slotf),
                                       base.rearrange("p (e a) -> p e a", a=1).to_broadcast([P, E, NT]),
                                       ALU.add))
                for k, oh in enumerate((oh1, oh2)):
                    link(dve.tensor_tensor(by_token(tmp), by_token(oh),
                                           slotf.rearrange("p (e i) -> p i e", e=E), ALU.mult))
                    link(dve.tensor_reduce(posf[:, k, :], by_token(tmp), AX.X, ALU.add))
                pair = lg2[:, 0:2 * NT].bitcast(U32).rearrange("p (k i) -> p k i", k=2)
                link(dve.tensor_copy(slot_u[:, :, :], posf))
                link(dve.tensor_scalar(pair, slot_u[:, :, :], 7, None, ALU.logical_shift_right))
                link(dve.tensor_copy(halff, pair))
                link(dve.tensor_scalar(pair, slot_u[:, :, :], P - 1, None, ALU.bitwise_and))
                link(dve.tensor_copy(posf, pair))

            def one_hot(c):
                k, i0 = c * RC // NT, c * RC % NT

                def spread(t, w):
                    return t.rearrange("p (q a) -> p q a", a=1).to_broadcast([P, RC, w])

                if c:
                    dve.wait_ge(sm["tok_ps"], c)
                link(dve.tensor_tensor(oh_pos, iota_b[:, :].rearrange("p (a n) -> p a n", a=1)
                                       .to_broadcast([P, RC, P]), spread(posf[:, k, i0:i0 + RC], P),
                                       ALU.is_equal))
                link(dve.tensor_tensor(oh_row[0], iota_b[:, 0:HALVES].rearrange("p (a n) -> p a n", a=1)
                                       .to_broadcast([P, RC, HALVES]),
                                       spread(halff[:, k, i0:i0 + RC], HALVES), ALU.is_equal))
                link(dve.tensor_scalar(oh_row[1], oh_row[0], iota_p[:, 0:1], None, ALU.mult))
                dve.tensor_tensor(oh_row[0], oh_row[0], spread(iot[:, i0:i0 + RC], HALVES), ALU.mult)\
                    .then_inc(sm["oneh_ready"], 1)

            def tables():
                cinc = esm[:, 2, :]
                dve.wait_ge(sm["tok_ps"], CHUNKS)
                link(dve.tensor_copy(tkf, pTok[:, 0:2 * HALVES]))
                link(dve.scalar_tensor_tensor(out=tok[:, :], in0=tkf[:, 0:HALVES], scalar=float(P),
                                              in1=tkf[:, HALVES:2 * HALVES], op0=ALU.mult, op1=ALU.add))

                def tiles(t):
                    return t.rearrange("p (j a) -> p j a", a=1).to_broadcast([P, ROUTED, E])

                def experts(t):
                    return t.rearrange("p (a e) -> p a e", a=1).to_broadcast([P, ROUTED, E])

                link(dve.tensor_tensor(eoh, tiles(iot[:, :]), experts(cinc), ALU.is_ge))
                link(dve.tensor_reduce(ejf, eoh, AX.X, ALU.add))
                link(dve.tensor_scalar(ejf, ejf, float(E - 1), None, ALU.min))
                link(dve.tensor_scalar(woff[:, SH1:SH1 + ROUTED], ejf, 1.0, float(SLOT), ALU.add, ALU.mult))
                link(dve.tensor_tensor(eoh, experts(ioe[:, :]), tiles(ejf), ALU.is_equal))
                for q, src in enumerate((inv1, hsc, inv2)):
                    link(dve.tensor_tensor(eot, eoh, experts(src[:, 1:NS]), ALU.mult))
                    link(dve.tensor_reduce(tab[:, q, SH1:SH1 + ROUTED], eot, AX.X, ALU.add))
                dve.wait_ge(sm["gate_exp"], 1)
                link(dve.tensor_scalar(den, ex, 1.0, None, ALU.add))
                link(dve.reciprocal(gates[:, 0, :], den))
                dve.tensor_tensor(gates[:, 1, :], ex, gates[:, 0, :], ALU.mult)\
                    .then_inc(sm["routed_ready"], 1)

            for tau in range(SH1):
                ffn(tau, tau % 2, front if tau else None, more=tau < SH1 - 1,
                    beside=lambda g: beside_first(tau, g))
                if tau == 2:
                    choose()
                if tau == 3:
                    places()
                if 4 <= tau < 4 + CHUNKS:
                    one_hot(tau - 4)
            tables()
            rows_to_sbuf(SH1, SH1 % 2)
            ffn(SH1, SH1 % 2, front)
            tile_pairs(dve, SH1 + 1, SH1 + ROUTED, lambda tau, u: ffn(tau, u, expert_rows))

            def combine(i):
                q = i % 4
                dve.wait_ge(grow_in[q], 32 * (i // 4 + 1))
                for k in range(2):
                    last = dve.scalar_tensor_tensor(out=xres[:, i, :], in0=grow[:, q, k, :],
                                                    scalar=gates[:, k, i:i + 1], in1=xres[:, i, :],
                                                    op0=ALU.mult, op1=ALU.add)
                    if k == 0:
                        link(last)
                last.then_inc(sm["comb_done"], 1)

            for m in range(SH2):
                tau = SH1 + ROUTED + m
                ffn(tau, tau % 2, back if m else expert_rows, more=m < SH2 - 1)
                if m >= 1:
                    for i in combined(m):
                        combine(i)
            back(NF - 1)
            dve.wait_ge(sm["y_done"], NF)
            for i in combined(SH2):
                combine(i)


_INS = ['x', 'ctx_1024', 'L0_xattn_Wk', 'L0_xattn_Wv', 'L0_xattn_bv', 'L0_xattn_Wq', 'L0_xattn_bq',
        'L0_xattn_Wo', 'L0_xattn_bo', 'L0_ffn_shared_w1', 'L0_ffn_shared_w2', 'L0_ffn_experts_w1',
        'L0_ffn_experts_w2', 'L0_ffn_gate_w']
_OUTS = [((4, 1024, 256), 'float32')]


def kernel(**inputs):
    import numpy as _np
    import concourse.bacc as _bacc
    from concourse import mybir as _mybir
    from concourse.bass_utils import run_bass_kernel_spmd as _run

    nc = _bacc.Bacc("TRN2", target_bir_lowering=False, num_devices=1, dynamic_dma_scratch_size=4096)
    arrays, args = {}, []
    for name in _INS:
        a = _np.ascontiguousarray(inputs[name])
        arrays[f"in_{name}_dram"] = a
        args.append(nc.dram_tensor(f"in_{name}_dram", a.shape, _mybir.dt.from_np(a.dtype), kind="ExternalInput").ap())
    for i, (shape, dtype) in enumerate(_OUTS):
        dt = _mybir.dt.from_np(_np.dtype(dtype))
        args.append(nc.dram_tensor(f"out_{i}_dram", shape, dt, kind="ExternalOutput").ap())
    xattn_moe_kernel(nc, *args)
    r = _run(nc, [arrays], core_ids=[0])
    got = tuple(r.results[0][f"out_{i}_dram"] for i in range(len(_OUTS)))
    return got[0]
```

```python
from contextlib import ExitStack

import concourse.bass as bass
from concourse import mybir

F32 = mybir.dt.float32
F16 = mybir.dt.float16
BF16 = mybir.dt.bfloat16
I32 = mybir.dt.int32
U32 = mybir.dt.uint32
ALU = mybir.AluOpType
ACT = mybir.ActivationFunctionType
AX = mybir.AxisListType
SUM = bass.bass_isa.ReduceOp.add

P = 128


def xattn_moe_kernel(nc, x, ctx_in, Wk, Wv, bv, Wq, bq, Wo, bo, sw1, sw2, ew1, ew2, gate_w, out):
    B, S, D = x.shape
    C = ctx_in.shape[1]
    E, HID, _ = ew1.shape
    KD = D // P
    KH = HID // P
    C2 = C - P
    NT = B * S // P
    JT = S // P
    R = 2 * P
    SHARED = B * S // R
    ROUTED = (2 * B * S + E * (R - 1)) // R
    SH1 = 9
    SH2 = SHARED - SH1
    NF = SHARED + ROUTED
    HALVES = 2 * ROUTED
    BANKS = HID * R // P // 512
    CB = KH // BANKS
    NS = E + 1
    SLOT = 4 * KD * HID
    EPS = 1e-5
    ROW_SCALE_LOG = 11
    ROW_SCALE = float(1 << ROW_SCALE_LOG)
    NEG_SCALE = -float(D) ** -0.5
    LAST = NT - JT
    GROUP = 4
    MOMENT_STEPS = 17
    LN_LAG = 12
    AHEAD = 4
    CONSTANTS = 7
    assert KD == 2 and CB * R == 512 and D * 2 == 512 and NT % 4 == 0

    sb_list = ExitStack()
    with sb_list as es:
        def sb(name, shape, dt):
            return es.enter_context(nc.sbuf_tensor(name, shape, dt))

        def sem(name):
            return es.enter_context(nc.semaphore(name))

        rows_dram = nc.dram_tensor("ln_rows", [NT * P, 2 * D], F16, kind="Internal").ap()
        y_dram = nc.dram_tensor("expert_rows", [ROUTED * R, D], F32, kind="Internal").ap()

        wts = sb("wts", [P, NS, SLOT], F16)
        xres = sb("xres", [P, NT, D], F32)
        stage = sb("stage", [P, 2048], F32)
        work = sb("work", [P, 5120], F32)
        identf = sb("identf", [P, P], F32)
        ident16 = sb("ident16", [P, P], F16)
        upper = sb("upper", [P, P], BF16)
        ones_b = sb("ones_b", [P, P], BF16)
        iota_b = sb("iota_b", [P, P], BF16)
        iota_p = sb("iota_p", [P, 1], F32)
        gateT = sb("gateT", [P, KD, E], F32)
        stats = sb("stats", [P, NT, 6], F32)
        mean = sb("mean", [P, NT], F32)
        rstd = sb("rstd", [P, NT], F32)
        nt_a = sb("nt_a", [P, NT], F32)
        nt_v = sb("nt_v", [P, NT], F32)
        nt_b = sb("nt_b", [P, NT], F32)
        rowsum = sb("rowsum", [P, 4], F32)
        rinv = sb("rinv", [P, 2], F32)
        negmax = sb("negmax", [P, 2], F32)
        psq = sb("psq", [P, 2, 2], F32)
        asq = sb("asq", [P, 2, 2], F32)
        norm2 = sb("norm2", [P, 2], F32)
        ebits = sb("ebits", [P, 2], I32)
        wscale = sb("wscale", [P, 2, NS], F32)
        inv1 = sb("inv1", [P, NS], F32)
        hsc = sb("hsc", [P, NS], F32)
        inv2 = sb("inv2", [P, NS], F32)
        tab = sb("tab", [P, 3, NF], F32)
        woff = sb("woff", [P, NF], I32)
        tok = sb("tok", [P, HALVES], U32)
        idx = sb("idx", [P, 2], U32)
        slot_u = sb("slot_u", [P, 2, NT], U32)
        gates = sb("gates", [P, 2, NT], F32)

        wflat = wts[:, :, :].rearrange("p s n -> p (s n)")
        NSL = NS - 1
        att = wts[:, NSL, :].bitcast(F32)
        ktn = att[:, 0:B * KD * C].rearrange("p (b k c) -> p b k c", b=B, k=KD)
        o = B * KD * C
        vct = att[:, o:o + B * 2 * D].rearrange("p (b k d) -> p b k d", b=B, k=2)
        o += B * 2 * D
        biasn = att[:, o:o + B * C].rearrange("p (b c) -> p b c", b=B)
        su = wts[:, NSL - 3:NSL, :].rearrange("p s n -> p (s n)").bitcast(F32)
        rawk, rawv, rawq, rawo, woT, fa, fc = (
            su[:, 512 * i:512 * i + 512].rearrange("p (c d) -> p c d", c=2) for i in range(7))
        o = 3584
        craw = su[:, o:o + B * 512].rearrange("p (b k d) -> p b k d", b=B, k=2)
        o += B * 512
        ctxT = su[:, o:o + B * KD * C].rearrange("p (b k c) -> p b k c", b=B, k=KD)
        o += B * KD * C
        ones_f = su[:, o:o + 128]
        ubc = su[:, o + 128:o + 384].rearrange("p (k n) -> p k n", k=2)
        bvbc = su[:, o + 384:o + 640].rearrange("p (k n) -> p k n", k=2)
        cbs = su[:, o + 640:o + 896]
        bq_c = su[:, o + 896:o + 898]
        bv_c = su[:, o + 898:o + 900]
        u_c = su[:, o + 900:o + 902]
        bo_r = su[0:1, o + 902:o + 1158]
        graw = su[0:E, o + 1158:o + 1158 + D]
        assert o + 1158 + D <= 3 * SLOT // 2

        xn = work[:, 0:512].rearrange("p (u d) -> p u d", u=2)
        xnT = work[:, 512:1024].rearrange("p (u k t) -> p u k t", u=2, k=2)
        sc = work[:, 1024:1024 + 2 * C].rearrange("p (u c) -> p u c", u=2)
        pT = work[:, 1408:1920].rearrange("p (u k t) -> p u k t", u=2, k=2)
        rout = sb("rout", [P, 2048], F32)
        raws = [stage[:, :], rout[:, :]]
        squares = work[:, 4608:5120].bitcast(BF16)

        def ln_buffers(t):
            return (t[:, 0:512].rearrange("p (u d) -> p u d", u=2),
                    t[:, 512:1024].rearrange("p (u k t) -> p u k t", u=2, k=2),
                    t[:, 1024:2048].bitcast(F16).rearrange("p (u d) -> p u d", u=4))

        ln_beside = ln_buffers(work[:, 1920:3968])
        ln_last = ln_buffers(stage[:, :])
        hring = work[:, 0:2048].bitcast(F16).rearrange("p (g s n) -> p g s n", g=BANKS, s=2)
        sring = work[:, 2048:3072].rearrange("p (g n) -> p g n", g=2)
        xT = [work[:, a:a + 512].bitcast(F16).rearrange("p (s k t) -> p s k t", s=2, k=2)
              for a in (4608, 3072)]
        xg = work[:, 4096:4608].bitcast(F16).rearrange("p (h d) -> p h d", h=2)
        ybuf = work[:, 3584:4096]

        def table(i):
            return rout[:, 256 * i:256 * (i + 1)]
        lg, tmp, oh1, oh2, lg2, incl, slotf, rmask = (table(i) for i in range(8))

        def by_token(t):
            return t.rearrange("p (i e) -> p i e", e=E)

        def by_expert(t):
            return t.rearrange("p (e i) -> p e i", e=E)

        nt32 = sb("nt32", [P, 10, NT], F32)
        m1, m2, sel1, sel2, ex, den = (nt32[:, i, :] for i in range(6))
        halff = nt32[:, 6:8, :]
        posf = nt32[:, 8:10, :]
        esm = sb("esm", [P, 6, E], F32)
        cnt_i = sb("cnt_i", [P, E], I32)
        efirst = sb("efirst", [P, E], F32)
        RC = 16
        CHUNKS = 2 * NT // RC
        oh_pos = stage[:, 0:RC * P // 2].bitcast(BF16).rearrange("p (q n) -> p q n", q=RC)
        hw = RC * HALVES // 2
        oh_row = [rout[:, hw * q:hw * (q + 1)].bitcast(BF16).rearrange("p (q n) -> p q n", q=RC)
                  for q in range(2)]
        assert 2 * hw <= 1280
        tkf = rout[:, 1280:1280 + 2 * HALVES]
        eoh = rout[:, 0:ROUTED * E].rearrange("p (j e) -> p j e", e=E)
        eot = rout[:, 512:512 + ROUTED * E].rearrange("p (j e) -> p j e", e=E)
        ejf = rout[:, 1024:1024 + ROUTED]
        iot = sb("iot", [P, ROUTED], F32)
        ioe = sb("ioe", [P, E], F32)
        grow = stage[:, 0:2048].rearrange("p (u k d) -> p u k d", u=4, k=2)

        ps = [es.enter_context(nc.psum_tensor(f"bank{i}", [P, 512], F32)) for i in range(8)]
        pXT, pSC, pPT, pPV = ps[0:4]
        pW = [ps[4 + q] for q in (0, 1, 2, 0, 1, 2, 0, 1)]
        W_BACK = (2, 2, 5, 3, 3, 3, 3, 3)
        pZT, pLG = ps[7][:, 0:D], ps[7][:, D:D + NT * E]
        pH = [ps[i] for i in range(BANKS)]
        pY, pT16 = ps[4], ps[5][:, :].bitcast(F16).rearrange("p (s k t) -> p s k t", s=2, k=2)
        pPre, pTot, pTok = ps[6], ps[7], ps[6]

        names = """x0 x1 x2 x3 w_in c_in b_in const_ready ones_ready u_ready bv_bc u_bc su_pe su_ev values_ready dchain
            pchain raw_in0 raw_in1 raw_sq all_sq scale_step moment_step scale_ready wt_ps whi wlo xn_done xt_ps
            xnt_done sc_ps sc_sum sc_done exp_done pt_ps ptt_done pv_ps rinv_done x2_done stat_done
            z_done z_hi z_lo zt_ps ztt_done lg_ps rows0 rows1 rows2 rows3 gate_diff gate_exp mask_ready count_ps
            oneh_ready tok_ps routed_ready slots_ready tabs0 rows_in xg_t xt_done h_ps silu_done hi_done lo_done
            y_ps y_done y_store idx_ready grow_in0 grow_in1 grow_in2 grow_in3 comb_part
            comb_done out_st passed""".split()
        sm = {n: sem(n) for n in names}
        raw_in = [sm["raw_in0"], sm["raw_in1"]]
        rows_st = [sm[f"rows{i}"] for i in range(4)]
        grow_in = [sm[f"grow_in{i}"] for i in range(4)]

        block = es.enter_context(nc.Block())

        def alone(eng):
            eng.sem_inc(sm["passed"], 1)

        def combined(m):
            ends = [0] + [min(-(-NT * q // (SH2 - 1)), 2 * (SH1 + q)) for q in range(1, SH2)] + [NT]
            return range(ends[m - 1], ends[m])

        FULL = -(-LN_LAG // JT)

        def of_first(b):
            return isinstance(b, int) and b == 0

        LAST_BANKS = ((0, 1, 2), (3, 4), (5, 6, 7))

        def last_norm(tau, g):
            z = LAST + BANKS * tau + g - 2
            return z if LAST <= z <= NT else None

        def w1_part(slot_off, s, k, lo, n):
            at = slot_off + (s * KD + k) * HID + lo
            return wflat[:, bass.ds(at, n)]

        def w2_part(slot_off, s, c):
            at = slot_off + 2 * KD * HID + (s * KH + c) * D
            return wflat[:, bass.ds(at, D)]

        def tile_pairs(eng, lo, hi, body):
            if lo % 2 and lo < hi:
                body(lo, 1)
                lo += 1
            pairs = (hi - lo) // 2
            if pairs > 1:
                with eng.Fori(lo // 2, lo // 2 + pairs) as t:
                    body(2 * t, 0)
                    body(2 * t + 1, 1)
                lo += 2 * pairs
            while lo < hi:
                body(lo, lo % 2)
                lo += 1

        @block.sync
        def _(sp):
            for b in range(B):
                sp.dma_start(craw[:, b, 0, :], ctx_in[b, 0:P, :]).then_inc(sm["c_in"], 16)
                sp.dma_start(craw[0:C2, b, 1, :], ctx_in[b, P:C, :]).then_inc(sm["c_in"], 16)
            for t, w in ((rawk, Wk), (rawq, Wq), (rawv, Wv)):
                sp.dma_start(t, w.rearrange("(p c) d -> p c d", c=2)).then_inc(sm["w_in"], 16)
            sp.dma_start(rawo, Wo.rearrange("(c p) d -> p c d", p=P)).then_inc(sm["w_in"], 16)
            sp.dma_start(bq_c, bq.rearrange("(p c) -> p c", c=2)).then_inc(sm["b_in"], 16)
            sp.dma_start(bv_c, bv.rearrange("(p c) -> p c", c=2)).then_inc(sm["b_in"], 16)
            sp.dma_start(bo_r, bo.rearrange("(a d) -> a d", a=1)).then_inc(sm["b_in"], 16)
            sp.dma_start(graw, gate_w).then_inc(sm["b_in"], 16)
            for b in range(B):
                sp.dma_start(xres[:, b * JT:(b + 1) * JT, :],
                             x[b].rearrange("(p j) d -> p j d", j=JT)).then_inc(sm[f"x{b}"], 16)

            def load_w1(t, src):
                if not isinstance(t, int) or t > 0:
                    sp.wait_ge(sm["wt_ps"], 8 * t - 4)
                sp.dma_start(raws[0].rearrange("p (c d) -> p c d", c=KH), src).then_inc(raw_in[0], 16)

            def load_w2(t, src):
                if not isinstance(t, int) or t > 0:
                    sp.wait_ge(sm["wt_ps"], 8 * t)
                sp.dma_start(raws[1].rearrange("p (a h) -> p a h", a=KD), src).then_inc(raw_in[1], 16)

            load_w1(0, sw1.rearrange("(c p) d -> p c d", p=P))
            load_w2(0, sw2.rearrange("(a p) h -> p a h", p=P))
            def load_expert_w1(t):
                load_w1(t, ew1[bass.ds(t - 1, 1)].rearrange("a (c p) d -> p (a c) d", p=P))

            def load_expert_w2(t):
                load_w2(t, ew2[bass.ds(t - 1, 1)].rearrange("a (q p) h -> p (a q) h", p=P))

            def store_rows(z, w, zrow):
                sp.wait_ge(sm["z_lo"], AHEAD + z + 1)
                sp.dma_start(rows_dram[bass.ds(z * P, P), :], zrow[:, w, :]).then_inc(rows_st[w], 16)

            for q in range(4):
                sp.sem_inc(rows_st[q], 4 * AHEAD)
            SLOTS0 = LN_LAG // 4
            for t in range(SLOTS0):
                load_expert_w1(t + 1)
                load_expert_w2(t + 1)
            with sp.Fori(SLOTS0, NS - 1) as t:
                z = 4 * t - LN_LAG
                store_rows(z, 0, ln_beside[2])
                load_expert_w1(t + 1)
                store_rows(z + 1, 1, ln_beside[2])
                store_rows(z + 2, 2, ln_beside[2])
                load_expert_w2(t + 1)
                store_rows(z + 3, 3, ln_beside[2])
            for q in range(4):
                store_rows(LAST - 4 + q, q, ln_beside[2])
            for z in range(LAST, NT):
                store_rows(z, z % 4, ln_last[2])

            def store_y(j, u):
                sp.wait_ge(sm["y_done"], j + SH1 + 1)
                sp.dma_start(y_dram[bass.ds(j * R, R), :].rearrange("(h p) d -> p h d", p=P),
                             ybuf.rearrange("p (h d) -> p h d", h=2)).then_inc(sm["y_store"], 16)

            tile_pairs(sp, 0, ROUTED, store_y)
            for i in range(0, NT, 2):
                sp.wait_ge(sm["comb_done"], i + 2)
                if i // 2 >= SH1:
                    sp.wait_ge(sm["y_done"], ROUTED + i // 2 + 1)
                b, j = i // JT, i % JT
                sp.dma_start(out[b].rearrange("(p j) d -> p j d", j=JT)[:, j:j + 2, :],
                             xres[:, i:i + 2, :]).then_inc(sm["out_st"], 16)
            sp.wait_ge(sm["out_st"], 16 * NT // 2)

        @block.gpsimd
        def _(pool):
            n = [0]

            def link(ins):
                n[0] += 1
                ins.then_inc(sm["pchain"], 1)
                pool.wait_ge(sm["pchain"], n[0])

            link(pool.memset(identf[:, :], 0.0))
            pool.affine_select(out=identf[:, :], in_=identf[:, :], compare_op=ALU.not_equal, fill=1.0,
                               base=0, pattern=[[-1, P]], channel_multiplier=1).then_inc(sm["const_ready"], 1)
            link(pool.memset(ident16[:, :], 0.0))
            link(pool.affine_select(out=ident16[:, :], in_=ident16[:, :], compare_op=ALU.not_equal, fill=1.0,
                                    base=0, pattern=[[-1, P]], channel_multiplier=1))
            link(pool.memset(ones_b[:, :], 1.0))
            link(pool.affine_select(out=upper[:, :], in_=ones_b[:, :], compare_op=ALU.is_gt, fill=0.0,
                                    base=0, pattern=[[1, P]], channel_multiplier=-1))
            pool.iota(iota_b[:, :], pattern=[[1, P]], base=0, channel_multiplier=0,
                      allow_small_or_imprecise_dtypes=True).then_inc(sm["const_ready"], 1)
            pool.iota(iota_p[:, :], pattern=[[1, 1]], base=0, channel_multiplier=1,
                      allow_small_or_imprecise_dtypes=True).then_inc(sm["const_ready"], 1)
            pool.iota(efirst[:, :], pattern=[[-1, E]], base=E, channel_multiplier=0,
                      allow_small_or_imprecise_dtypes=True).then_inc(sm["const_ready"], 1)
            pool.memset(woff[:, :], 0).then_inc(sm["const_ready"], 1)
            for t_, n_ in ((iot, ROUTED), (ioe, E)):
                pool.iota(t_[:, :], pattern=[[1, n_]], base=0, channel_multiplier=0,
                          allow_small_or_imprecise_dtypes=True).then_inc(sm["const_ready"], 1)

            def across(t, m):
                pool.wait_ge(sm["raw_sq"], 4 * t + 2 * m + 2)
                if not isinstance(t, int) or t > 0:
                    pool.wait_ge(sm["scale_ready"], 2 * t + m - 1)
                alone(pool)
                pool.partition_all_reduce(asq[:, m, :], psq[:, m, :], P, SUM)\
                    .then_inc(sm["all_sq"], 1)

            def low(z, w):
                pool.wait_ge(sm["z_hi"], z + 1)
                zf, _, zrow = ln_beside
                pool.tensor_tensor(zrow[:, w % 4, D:2 * D], zf[:, w % 2, :], zrow[:, w % 4, 0:D],
                                   ALU.subtract).then_inc(sm["z_lo"], 1)

            pool.sem_inc(sm["z_lo"], AHEAD)
            across(0, 0)
            for t in range(LN_LAG // 4):
                across(t, 1)
                across(t + 1, 0)

            def slot_part(t):
                z = 4 * t - LN_LAG
                low(z, 0)
                across(t, 1)
                low(z + 1, 1)
                low(z + 2, 2)
                if not isinstance(t, int):
                    across(t + 1, 0)
                low(z + 3, 3)

            with pool.Fori(LN_LAG // 4, NS - 1) as t:
                slot_part(t)
            for q in range(2):
                pool.wait_ge(rows_st[q], 4 * (AHEAD + 4))
            pool.dma_start(xg[:, :, :], rows_dram[0:R, :].rearrange("(h p) d -> p h d", p=P))\
                .then_inc(sm["rows_in"], 32)
            slot_part(NS - 1)

            for q in range(4):
                pool.wait_ge(rows_st[q], 4 * (AHEAD + LAST))

            def rows_in_order(i, tau, u):
                pool.wait_ge(sm["xg_t"], tau)
                alone(pool)
                pool.dma_start(xg[:, :, :], rows_dram[bass.ds(i * R, R), :].rearrange("(h p) d -> p h d", p=P))\
                    .then_inc(sm["rows_in"], 32)

            def rows_by_slot(j, u):
                pool.wait_ge(sm["xg_t"], j + SH1)
                alone(pool)
                pool.tensor_copy(idx[:, :], tok[:, bass.ds(2 * j, 2)]).then_inc(sm["idx_ready"], 1)
                pool.wait_ge(sm["idx_ready"], j + 1)
                alone(pool)
                for h in range(2):
                    pool.indirect_dma_start(xg[:, h, :], None, rows_dram,
                                            bass.IndirectOffsetOnAxis(idx[:, h:h + 1], 0))\
                        .then_inc(sm["rows_in"], 16)

            tile_pairs(pool, 1, SH1, lambda i, u: rows_in_order(i, i, u))
            for q in range(4):
                pool.wait_ge(rows_st[q], 4 * (AHEAD + NT))
            pool.wait_ge(sm["slots_ready"], 1)
            tile_pairs(pool, 0, ROUTED, rows_by_slot)

            def gather_outputs(i):
                q = i % 4
                if i >= 4:
                    pool.wait_ge(sm["comb_done"], i - 3)
                for k in range(2):
                    pool.indirect_dma_start(grow[:, q, k, :], None, y_dram,
                                            bass.IndirectOffsetOnAxis(slot_u[:, k, i:i + 1], 0))\
                        .then_inc(grow_in[q], 16)

            def back_tile(m):
                rows_in_order(SH1 + m, SH1 + ROUTED + m, 0)

            back_tile(0)
            back_tile(1)
            pool.wait_ge(sm["y_store"], 16 * ROUTED)
            for m in range(1, SH2):
                if m + 1 < SH2:
                    back_tile(m + 1)
                for i in combined(m):
                    gather_outputs(i)
            for i in combined(SH2):
                gather_outputs(i)

        @block.tensor
        def _(pe):
            pe.wait_ge(sm["const_ready"], 1)
            pe.wait_ge(sm["c_in"], 16 * 2 * B)
            n = [0]

            def bank_read(step):
                batch, part = divmod(step - 9, 3)
                if step < 9:
                    pe.wait_ge(sm["su_ev"], step + 1)
                elif part < 2:
                    pe.wait_ge(sm["su_ev"], 9 + 2 * batch + part + 1)
                else:
                    pe.wait_ge(sm["values_ready"], batch + 1)

            def bank():
                b = n[0] % 4
                if n[0] >= 4:
                    bank_read(n[0] - 4)
                n[0] += 1
                return ps[b]

            for b in range(B):
                q = bank()
                for k in range(KD):
                    pe.transpose(q[:, k * 256:k * 256 + P], craw[:, b, 0, k * P:(k + 1) * P], identf[:, :])
                    last = pe.transpose(q[:, k * 256 + P:k * 256 + C], craw[0:C2, b, 1, k * P:(k + 1) * P],
                                        identf[0:C2, 0:C2])
                last.then_inc(sm["su_pe"], 1)
            pe.wait_ge(sm["w_in"], 64)
            pe.wait_ge(sm["b_in"], 64)
            q = bank()
            for c in range(2):
                for r in range(2):
                    last = pe.transpose(q[:, c * 256 + r * P:c * 256 + (r + 1) * P],
                                        rawo[:, r, c:D:2], identf[:, :])
            last.then_inc(sm["su_pe"], 1)
            q = bank()
            for a in range(KD):
                for c in range(2):
                    last = pe.matmul(q[:, a * 256:(a + 1) * 256], rawk[:, c, a * P:(a + 1) * P], rawq[:, c, :],
                                     start=(c == 0), stop=(c == 1))
            last.then_inc(sm["su_pe"], 1)
            q = bank()
            for a in range(KD):
                for c in range(2):
                    pe.matmul(q[:, a:a + 1], rawk[:, c, a * P:(a + 1) * P], bq_c[:, c:c + 1],
                              start=(c == 0), stop=(c == 1))
            for k in range(KD):
                last = pe.transpose(q[:, 16 + k * E:16 + (k + 1) * E], graw[:, k * P:(k + 1) * P],
                                    identf[0:E, 0:E])
            last.then_inc(sm["su_pe"], 1)
            pe.wait_ge(sm["su_ev"], 5)
            q = bank()
            for a in range(KD):
                for c in range(2):
                    last = pe.matmul(q[:, a * 256:(a + 1) * 256], rawv[:, c, a * P:(a + 1) * P], woT[:, c, :],
                                     start=(c == 0), stop=(c == 1))
            last.then_inc(sm["su_pe"], 1)
            q = bank()
            pe.wait_ge(sm["bv_bc"], 1)
            for c in range(2):
                pe.matmul(q[:, 0:D], bvbc[:, c, :], woT[:, c, :], start=(c == 0), stop=False)
            pe.matmul(q[:, 0:D], ones_f[0:1, :], bo_r, start=False, stop=True).then_inc(sm["su_pe"], 1)
            for b in range(B):
                q = bank()
                pe.wait_ge(sm["su_ev"], 6)
                for r in range(KD):
                    for a in range(KD):
                        last = pe.matmul(q[:, r * 256:r * 256 + C], fa[:, a, r * P:(r + 1) * P],
                                         ctxT[:, b, a, :], start=(a == 0), stop=(a == 1))
                last.then_inc(sm["su_pe"], 1)
                q = bank()
                pe.wait_ge(sm["u_bc"], 1)
                for a in range(KD):
                    last = pe.matmul(q[:, 0:C], ubc[:, a, :], ctxT[:, b, a, :], start=(a == 0), stop=(a == 1))
                last.then_inc(sm["su_pe"], 1)
                q = bank()
                pe.wait_ge(sm["su_ev"], 9)
                for r, rows in ((0, P), (1, C2)):
                    for a in range(KD):
                        last = pe.matmul(q[0:rows, r * 256:(r + 1) * 256], ctxT[:, b, a, r * P:r * P + rows],
                                         fc[:, a, :], start=(a == 0), stop=(a == 1))
                last.then_inc(sm["su_pe"], 1)
            bank_read(n[0] - 2)
            bank_read(n[0] - 1)

            def transpose_x(i, u):
                pe.wait_ge(sm["xn_done"], i + 1)
                if not isinstance(i, int) or i > 0:
                    pe.wait_ge(sm["xnt_done"], i)
                for k in range(KD):
                    last = pe.transpose(pXT[:, k * P:(k + 1) * P], xn[:, u, k * P:(k + 1) * P], identf[:, :])
                last.then_inc(sm["xt_ps"], 1)

            def scores(i, u, b):
                pe.wait_ge(sm["xnt_done"], i + 1)
                if not isinstance(i, int) or i > 0:
                    pe.wait_ge(sm["sc_done"], i)
                for k in range(KD):
                    last = pe.matmul(pSC[:, 0:C], xnT[:, u, k, :],
                                     ktn[:, bass.ds(b, 1), k, :].rearrange("p a c -> p (a c)"),
                                     start=(k == 0), stop=(k == 1))
                last.then_inc(sm["sc_ps"], 1)

            def transpose_p(i, u):
                pe.wait_ge(sm["exp_done"], i + 1)
                if not isinstance(i, int) or i > 0:
                    pe.wait_ge(sm["ptt_done"], 2 * i)
                pe.transpose(pPT[:, 0:P], sc[:, u, 0:P], identf[:, :])
                pe.transpose(pPT[0:C2, P:2 * P], sc[:, u, P:C], identf[:, :]).then_inc(sm["pt_ps"], 1)

            def values(i, u, b):
                pe.wait_ge(sm["ptt_done"], 2 * i + 2)
                if not isinstance(i, int) or i > 0:
                    pe.wait_ge(sm["x2_done"], i)
                pe.matmul(pPV[:, 0:D], pT[:, u, 0, :], vct[:, bass.ds(b, 1), 0, :].rearrange("p a d -> p (a d)"),
                          start=True, stop=False)
                pe.matmul(pPV[:, 0:D], pT[0:C2, u, 1, :],
                          vct[0:C2, bass.ds(b, 1), 1, :].rearrange("p a d -> p (a d)"),
                          start=False, stop=True).then_inc(sm["pv_ps"], 1)

            def weight_bank(t, g):
                q = pW[g]
                m = g // 4
                if g % 4 == 0:
                    pe.wait_ge(raw_in[m], 16 * t + 16)
                if g >= 3 or not isinstance(t, int) or t > 0:
                    pe.wait_ge(sm["wlo"], 8 * t + g + 1 - W_BACK[g])
                for r in range(4):
                    if m == 0:
                        k, c = g // 2, (g % 2) * 4 + r
                        src = raws[0][:, c * D + k * P:c * D + (k + 1) * P]
                    else:
                        c, a = 2 * (g - 4) + r // 2, r % 2
                        src = raws[1][:, a * HID + c * P:a * HID + (c + 1) * P]
                    last = pe.transpose(q[:, r * P:(r + 1) * P], src, identf[:, :])
                last.then_inc(sm["wt_ps"], 1)

            TRANSFERS = ((None, 0, 1), (2, 3, None), (4, 5, None), (6, 7, None))

            def step(i, t, s, b1, b3, beside=lambda place: None):
                start, middle, end = TRANSFERS[s]
                transpose_x(i, s % 2)
                if start is not None:
                    weight_bank(t, start)
                if not isinstance(i, int) or i >= 1:
                    scores(i - 1, (s - 1) % 2, b1)
                if not isinstance(i, int) or i >= 2:
                    transpose_p(i - 2, s % 2)
                weight_bank(t, middle)
                beside(0)
                if not isinstance(i, int) or i >= 3:
                    values(i - 3, (s - 3) % 2, b3)
                if end is not None:
                    weight_bank(t, end)
                beside(1)

            def transpose_z(z, w, bufs):
                pe.wait_ge(sm["z_done"], z + 1)
                for k in range(KD):
                    last = pe.transpose(pZT[:, k * P:(k + 1) * P],
                                        bufs[0][:, w % 2, k * P:(k + 1) * P], identf[:, :])
                last.then_inc(sm["zt_ps"], 1)

            def logits(z, w, bufs):
                pe.wait_ge(sm["ztt_done"], AHEAD + z + 1)
                for k in range(KD):
                    last = pe.matmul(pLG[:, bass.ds(z * E, E)], bufs[1][:, w % 2, k, :], gateT[:, k, :],
                                     start=(k == 0), stop=(k == 1))
                last.then_inc(sm["lg_ps"], 1)

            pe.sem_inc(sm["zt_ps"], AHEAD)
            pe.sem_inc(sm["lg_ps"], AHEAD)
            def norm_beside(i, s):
                z = i - LN_LAG
                if not isinstance(i, int) or z > 0:
                    logits(z - 1, (s + 3) % 4, ln_beside)
                transpose_z(z, s, ln_beside)

            def batch(b):
                for j in range(JT):
                    i = b * JT + j

                    def beside(place):
                        if place == 0 and (not isinstance(i, int) or i >= LN_LAG):
                            norm_beside(i, j % 4)

                    step(i, b * (JT // 4) + j // 4, j % 4, b if j >= 1 or of_first(b) else b - 1,
                         b if j >= 3 or of_first(b) else b - 1, beside)

            for b in range(FULL):
                batch(b)
            with pe.Fori(FULL, B) as b:
                batch(b)
            for i in range(NT, NT + 4):
                if i - 1 < NT:
                    scores(i - 1, (i - 1) % 2, B - 1)
                if i - 2 < NT:
                    transpose_p(i - 2, i % 2)
                norm_beside(i, i % 4)
                if i - 3 < NT:
                    values(i - 3, (i - 3) % 2, B - 1)
            logits(LAST - 1, 3, ln_beside)

            def transpose_rows(tau, u):
                pe.wait_ge(sm["rows_in"], 32 * tau + 32)
                if not isinstance(tau, int) or tau > 0:
                    pe.wait_ge(sm["xt_done"], tau)
                if isinstance(tau, int) and tau == 1:
                    pe.wait_ge(sm["wlo"], 8 * NS)
                for h in range(2):
                    for s in range(2):
                        for k in range(KD):
                            last = pe.transpose(pT16[:, s, k, h * P:(h + 1) * P],
                                                xg[:, h, s * D + k * P:s * D + (k + 1) * P], ident16[:, :])
                last.then_inc(sm["xg_t"], 1)

            def up(tau, u, g, off):
                n = BANKS * tau + g
                if g == 0:
                    pe.wait_ge(sm["xt_done"], tau + 1)
                if not isinstance(tau, int) or tau > 0:
                    pe.wait_ge(sm["silu_done"], n - BANKS + 1)
                for r in range(CB):
                    c = g * CB + r
                    first = True
                    for k in range(KD):
                        for sw, sx in ((0, 0), (0, 1), (1, 0)):
                            last = pe.matmul(pH[g][:, r * R:(r + 1) * R], w1_part(off, sw, k, c * P, P),
                                             xT[u][:, sx, k, :], start=first, stop=(k == 1 and sw == 1))
                            first = False
                last.then_inc(sm["h_ps"], 1)

            def down(tau, g, off):
                pe.wait_ge(sm["lo_done"], BANKS * tau + g + 1)
                if g == 0 and (not isinstance(tau, int) or tau > 0):
                    pe.wait_ge(sm["y_done"], tau)
                for r in range(CB):
                    c = g * CB + r
                    for sw, sh in ((0, 0), (0, 1), (1, 0)):
                        for h in range(2):
                            first = g == 0 and r == 0 and sw == 0 and sh == 0
                            last = pe.matmul(
                                pY[:, h * D:(h + 1) * D],
                                hring[:, g, sh, r * R + h * P:r * R + (h + 1) * P],
                                w2_part(off, sw, c), start=first and h == 0,
                                stop=(g == BANKS - 1 and r == CB - 1 and sw == 1), skip_group_check=True)
                last.then_inc(sm["y_ps"], 1)

            def offset(tau):
                if isinstance(tau, int) and (tau < SH1 or tau >= SH1 + ROUTED):
                    return 0
                return pe.value_load(woff[0:1, bass.ds(tau, 1)], min_val=0, max_val=E * SLOT)

            def ffn(tau, u, now, before, more=True, beside=lambda g: None, late=False):
                off = now(tau)
                if late:
                    transpose_rows(tau, u)
                    down(tau - 1, 2, before(tau - 1))
                up(tau, u, 0, off)
                beside(0)
                if before is not None:
                    old = before(tau - 1)
                    if not late:
                        down(tau - 1, 2, old)
                up(tau, u, 1, off)
                beside(1)
                if before is not None:
                    down(tau - 1, 3, old)
                if more:
                    transpose_rows(tau + 1, 1 - u)
                up(tau, u, 2, off)
                beside(2)
                down(tau, 0, off)
                up(tau, u, 3, off)
                beside(3)
                down(tau, 1, off)

            def fixed(tau):
                return 0

            def count():
                mask = slotf[:, 0:128].bitcast(BF16)
                pe.wait_ge(sm["mask_ready"], 1)
                pe.matmul(pPre[:, 0:NT * E], upper[:, :], mask, start=True, stop=True)
                pe.matmul(pTot[:, 0:NT * E], ones_b[:, :], mask, start=True, stop=True)\
                    .then_inc(sm["count_ps"], 1)

            def invert(c):
                pe.wait_ge(sm["oneh_ready"], c + 1)
                for q in range(RC):
                    for h in range(2):
                        last = pe.matmul(pTok[:, h * HALVES:(h + 1) * HALVES], oh_pos[:, q, :],
                                         oh_row[h][:, q, :], start=(c == 0 and q == 0 and h == 0),
                                         stop=(c == CHUNKS - 1 and q == RC - 1), skip_group_check=True)
                last.then_inc(sm["tok_ps"], 1)

            pe.wait_ge(sm["const_ready"], CONSTANTS)
            pe.wait_ge(sm["wlo"], 8 * (NS - 1))
            transpose_rows(0, 0)
            for g in LAST_BANKS[0]:
                if g == 1:
                    pe.wait_ge(sm["xt_done"], 1)
                weight_bank(NS - 1, g)

            def beside_first(tau, g):
                if tau == 0 and g < 2:
                    for q in LAST_BANKS[g + 1]:
                        weight_bank(NS - 1, q)
                if g == 3 and 5 <= tau < 5 + CHUNKS:
                    invert(tau - 5)
                z = last_norm(tau, g)
                if z is not None:
                    if z > LAST:
                        logits(z - 1, (z - 1) % 4, ln_last)
                    if z < NT:
                        transpose_z(z, z % 4, ln_last)

            ffn(0, 0, fixed, None, beside=lambda g: beside_first(0, g))
            for tau in range(1, SH1):
                ffn(tau, tau % 2, fixed, fixed, more=tau < SH1 - 1, beside=lambda g: beside_first(tau, g))
                if tau == 3:
                    count()
            pe.wait_ge(sm["routed_ready"], 1)
            ffn(SH1, SH1 % 2, offset, fixed, late=True)
            tile_pairs(pe, SH1 + 1, SH1 + ROUTED, lambda tau, u: ffn(tau, u, offset, offset))
            tau = SH1 + ROUTED
            ffn(tau, tau % 2, fixed, offset)
            tile_pairs(pe, tau + 1, NF - 1, lambda tau, u: ffn(tau, u, fixed, fixed))
            ffn(NF - 1, (NF - 1) % 2, fixed, fixed, more=False)
            down(NF - 1, 2, 0)
            down(NF - 1, 3, 0)

        @block.scalar
        def _(act):
            def take(step):
                act.wait_ge(sm["su_pe"], step + 1)
                return ps[step % 4]

            for b in range(B):
                q = take(b)
                act.activation(ctxT[:, b, :, :], q[:, :].rearrange("p (k n) -> p k n", k=2)[:, :, 0:C],
                               ACT.Copy).then_inc(sm["su_ev"], 1)
            q = take(4)
            act.activation(woT.rearrange("p c d -> p (c d)"), q[:, :], ACT.Copy).then_inc(sm["su_ev"], 1)
            q = take(5)
            act.activation(fa.rearrange("p c d -> p (c d)"), q[:, :], ACT.Copy).then_inc(sm["su_ev"], 1)
            q = take(6)
            act.activation(u_c, q[:, 0:2], ACT.Copy).then_inc(sm["u_ready"], 1)
            act.activation(gateT[:, :, :].rearrange("p k e -> p (k e)"), q[:, 16:16 + 2 * E], ACT.Copy)\
                .then_inc(sm["su_ev"], 1)
            q = take(7)
            act.activation(fc.rearrange("p c d -> p (c d)"), q[:, :], ACT.Copy).then_inc(sm["su_ev"], 1)
            q = take(8)
            act.activation(cbs, q[:, 0:D], ACT.Copy).then_inc(sm["su_ev"], 1)
            for b in range(B):
                q = take(9 + 3 * b)
                act.activation(ktn[:, b, :, :], q[:, :].rearrange("p (k n) -> p k n", k=2)[:, :, 0:C],
                               ACT.Copy, scale=NEG_SCALE).then_inc(sm["su_ev"], 1)
                q = take(10 + 3 * b)
                act.activation(biasn[:, b, :], q[:, 0:C], ACT.Copy, scale=NEG_SCALE).then_inc(sm["su_ev"], 1)

            def x_to_sbuf(i, u):
                act.wait_ge(sm["xt_ps"], i + 1)
                if not isinstance(i, int) or i >= 2:
                    act.wait_ge(sm["sc_ps"], i - 1)
                act.activation(xnT[:, u, :, :].rearrange("p k t -> p (k t)"), pXT[:, 0:D], ACT.Copy)\
                    .then_inc(sm["xnt_done"], 1)

            def exponentials(i, u, r):
                act.wait_ge(sm["sc_done"], i + 1)
                act.activation(sc[:, u, :], sc[:, u, :], ACT.Exp, bias=negmax[:, u:u + 1], scale=-1.0,
                               accum_out=rowsum[:, r:r + 1]).then_inc(sm["exp_done"], 1)

            def p_to_sbuf(i, u):
                act.wait_ge(sm["pt_ps"], i + 1)
                if not isinstance(i, int) or i >= 2:
                    act.wait_ge(sm["pv_ps"], i - 1)
                act.activation(pT[:, u, 0, :], pPT[:, 0:P], ACT.Copy).then_inc(sm["ptt_done"], 1)
                act.activation(pT[0:C2, u, 1, :], pPT[0:C2, P:2 * P], ACT.Copy).then_inc(sm["ptt_done"], 1)

            def weight_high(t, g):
                m, q = g // 4, pW[g]
                if g % 4 == 0:
                    act.wait_ge(sm["scale_ready"], 2 * t + m + 1)
                act.wait_ge(sm["wt_ps"], 8 * t + g + 1)
                alone(act)
                at = t * SLOT + (m * 2 * KD * HID) + (g % 4) * 512
                act.activation(wflat[:, bass.ds(at, 512)], q[:, :], ACT.Copy,
                               scale=wscale[:, m, bass.ds(t, 1)]).then_inc(sm["whi"], 1)

            def raw_squares(t, m, h):
                n = 4 * t + 2 * m + h
                act.wait_ge(raw_in[m], 16 * t + 16)
                if not isinstance(t, int) or t > 0:
                    act.wait_ge(sm["all_sq"], 2 * t + m - 1)
                if not isinstance(t, int) or n > 0:
                    act.wait_ge(sm["raw_sq"], n)
                act.activation(squares, raws[m][:, h * 1024:(h + 1) * 1024], ACT.Square,
                               accum_out=psq[:, m, h:h + 1]).then_inc(sm["raw_sq"], 1)

            def high(z, w, bufs):
                act.wait_ge(sm["z_done"], z + 1)
                act.wait_ge(rows_st[w % 4], 4 * (AHEAD + z - w % 4))
                act.activation(bufs[2][:, w % 4, 0:D], bufs[0][:, w % 2, :], ACT.Copy).then_inc(sm["z_hi"], 1)

            def z_to_sbuf(z, w, bufs):
                act.wait_ge(sm["zt_ps"], AHEAD + z + 1)
                act.wait_ge(sm["lg_ps"], AHEAD + z - 1)
                act.activation(bufs[1][:, w % 2, :, :].rearrange("p k t -> p (k t)"), pZT, ACT.Copy)\
                    .then_inc(sm["ztt_done"], 1)

            def att(i, b, j):
                one = not isinstance(i, int)
                s = j % 4
                t, tp = b * (JT // 4) + j // 4, b * (JT // 4) + (j - 1) // 4
                z = i - LN_LAG
                if one or i < NT:
                    x_to_sbuf(i, s % 2)
                if one or 0 < i <= NT:
                    weight_high(tp, 2 * ((j - 1) % 4) + 1)
                if one or 0 <= i - 1 < NT:
                    exponentials(i - 1, (s - 1) % 2, (s - 1) % 4)
                if (one or i < NT or s < 2) and s % 2 == 1:
                    raw_squares(t + s // 2, 1 - s // 2, 1)
                if one or z >= 0:
                    high(z, s, ln_beside)
                if one or 0 <= i - 2 < NT:
                    p_to_sbuf(i - 2, s % 2)
                if one or i < NT:
                    weight_high(t, 2 * s)
                if one or z >= 0:
                    z_to_sbuf(z, s, ln_beside)
                if (one or i < NT or s < 2) and s % 2 == 0:
                    raw_squares(t + s // 2, 1 - s // 2, 0)

            act.sem_inc(sm["ztt_done"], AHEAD)
            for h in range(2):
                raw_squares(0, 0, h)
            for i in range(FULL * JT):
                att(i, i // JT, i % JT)
            with act.Fori(FULL, B) as b:
                for j in range(JT):
                    att(b * JT + j, b, j)
            for j in range(4):
                att(NT + j, B, j)
            act.wait_ge(sm["x2_done"], NT)
            for g in LAST_BANKS[0]:
                weight_high(NS - 1, g)
            def hidden(tau, u, beside=lambda g: None):
                for g in range(BANKS):
                    n = BANKS * tau + g
                    act.wait_ge(sm["h_ps"], n + 1)
                    if not isinstance(tau, int) or n >= 2:
                        act.wait_ge(sm["lo_done"], n - 1)
                    alone(act)
                    act.activation(sring[:, g % 2, :], pH[g][:, :], ACT.Silu,
                                   scale=tab[:, 0, bass.ds(tau, 1)]).then_inc(sm["silu_done"], 1)
                    act.wait_ge(sm["silu_done"], n + 1)
                    if not isinstance(tau, int) or tau > 0:
                        act.wait_ge(sm["y_ps"], n - BANKS + 1)
                    alone(act)
                    act.activation(hring[:, g, 0, :], sring[:, g % 2, :], ACT.Copy,
                                   scale=tab[:, 1, bass.ds(tau, 1)]).then_inc(sm["hi_done"], 1)
                    beside(g)

            def beside_first(tau, g):
                if tau == 0 and g < 2:
                    for q in LAST_BANKS[g + 1]:
                        weight_high(NS - 1, q)
                z = last_norm(tau, g)
                if z is not None and z < NT:
                    high(z, z % 4, ln_last)
                    z_to_sbuf(z, z % 4, ln_last)

            for q in range(4):
                act.wait_ge(rows_st[q], 4 * (AHEAD + LAST))
            act.wait_ge(sm["tabs0"], 6)
            for tau in range(3):
                hidden(tau, tau % 2, lambda g: beside_first(tau, g))
            act.wait_ge(sm["gate_diff"], 1)
            act.activation(ex, m2, ACT.Exp, scale=1.0 / ROW_SCALE).then_inc(sm["gate_exp"], 1)
            tile_pairs(act, 3, SH1, hidden)
            act.wait_ge(sm["routed_ready"], 1)
            tile_pairs(act, SH1, SH1 + ROUTED, hidden)
            tile_pairs(act, SH1 + ROUTED, NF, hidden)

        @block.vector
        def _(dve):
            n = [0]

            def link(ins):
                n[0] += 1
                ins.then_inc(sm["dchain"], 1)
                dve.wait_ge(sm["dchain"], n[0])

            def moment_step(q, at, n, target, linked):
                st, mu = stats[:, bass.ds(at, n), :], mean[:, bass.ds(at, n)]
                y, a, v, b = rstd[:, bass.ds(at, n)], nt_a[:, 0:n], nt_v[:, 0:n], nt_b[:, 0:n]
                k = 1.0 / target ** 2
                if q == 0:
                    linked(dve.tensor_tensor(a, st[:, :, 1], st[:, :, 4], ALU.add))
                elif q == 1:
                    linked(dve.tensor_scalar(mu, a, 0.5, None, ALU.mult))
                elif q == 2:
                    linked(dve.tensor_tensor(a, st[:, :, 1], st[:, :, 4], ALU.subtract))
                elif q == 3:
                    linked(dve.scalar_tensor_tensor(out=b, in0=a, scalar=0.25 * k, in1=a,
                                                    op0=ALU.mult, op1=ALU.mult))
                elif q == 4:
                    linked(dve.tensor_tensor(v, st[:, :, 2], st[:, :, 5], ALU.add))
                elif q == 5:
                    linked(dve.tensor_scalar(v, v, k / D, k * EPS, ALU.mult, ALU.add))
                elif q == 6:
                    linked(dve.tensor_tensor(v, v, b, ALU.add))
                elif q == 7:
                    linked(dve.tensor_scalar(b.bitcast(I32), v.bitcast(I32), -0.5, float(0x5F3759DF),
                                             ALU.mult, ALU.add))
                elif (q - 8) % 3 == 0:
                    linked(dve.scalar_tensor_tensor(out=a, in0=b, scalar=-0.5, in1=b,
                                                    op0=ALU.mult, op1=ALU.mult))
                elif (q - 8) % 3 == 1:
                    linked(dve.tensor_tensor(a, a, v, ALU.mult))
                else:
                    linked(dve.scalar_tensor_tensor(out=b if q < MOMENT_STEPS - 1 else y, in0=a, scalar=1.5,
                                                    in1=b, op0=ALU.add, op1=ALU.mult))

            def row(i):
                return xres[:, bass.ds(i, 1), :].rearrange("p a d -> p (a d)")

            dve.memset(ones_f, 1.0).then_inc(sm["ones_ready"], 1)
            dve.wait_ge(sm["ones_ready"], 1)
            dve.wait_ge(sm["b_in"], 64)
            link(dve.tensor_scalar(bvbc[:, 0, :], ones_f, bv_c[:, 0:1], None, ALU.mult))
            dve.tensor_scalar(bvbc[:, 1, :], ones_f, bv_c[:, 1:2], None, ALU.mult).then_inc(sm["bv_bc"], 1)
            for i in range(NT):
                if i % JT == 0:
                    dve.wait_ge(sm[f"x{i // JT}"], 16)
                last = dve.bn_stats(stats[:, i, :], xres[:, i, :])
            link(last)
            dve.wait_ge(sm["u_ready"], 1)
            link(dve.tensor_scalar(ubc[:, 0, :], ones_f, u_c[:, 0:1], None, ALU.mult))
            dve.tensor_scalar(ubc[:, 1, :], ones_f, u_c[:, 1:2], None, ALU.mult).then_inc(sm["u_bc"], 1)
            for q in range(MOMENT_STEPS):
                moment_step(q, 0, NT, 1.0, link)
            for b in range(B):
                dve.wait_ge(sm["su_pe"], 9 + 3 * b + 3)
                q = ps[(11 + 3 * b) % 4]
                dve.wait_ge(sm["su_ev"], 9)
                link(dve.tensor_tensor(vct[:, b, 0, :], q[:, 0:D], cbs, ALU.add))
                dve.tensor_tensor(vct[0:C2, b, 1, :], q[0:C2, D:2 * D], cbs[0:C2, :], ALU.add)\
                    .then_inc(sm["values_ready"], 1)

            def scale(t, m):
                dve.wait_ge(sm["all_sq"], 2 * t + m + 1)
                q = 3 * (2 * t + m)
                dve.tensor_tensor(norm2[:, 0:1], asq[:, m, 0:1], asq[:, m, 1:2], ALU.add)\
                    .then_inc(sm["scale_step"], 1)
                dve.wait_ge(sm["scale_step"], q + 1)
                dve.tensor_scalar(ebits[:, 0:1], norm2[:, 0:1].bitcast(I32), 24, None,
                                  ALU.logical_shift_right).then_inc(sm["scale_step"], 1)
                dve.wait_ge(sm["scale_step"], q + 2)
                dve.tensor_scalar(ebits[:, 1:2], ebits[:, 0:1], 17.0, -float(1 << 23), ALU.max, ALU.mult)\
                    .then_inc(sm["scale_step"], 1)
                dve.wait_ge(sm["scale_step"], q + 3)
                dve.tensor_scalar(wscale[:, m, bass.ds(t, 1)].bitcast(I32), ebits[:, 1:2], float(204 << 23),
                                  None, ALU.add).then_inc(sm["scale_ready"], 1)
                dve.wait_ge(sm["scale_ready"], 2 * t + m + 1)

            def weight_low(t, g):
                m, q = g // 4, pW[g]
                at = t * SLOT + (m * 2 * KD * HID) + (g % 4) * 512
                dve.wait_ge(sm["whi"], 8 * t + g + 1)
                dve.scalar_tensor_tensor(out=wflat[:, bass.ds(at + KD * HID, 512)], in0=q[:, :],
                                         scalar=wscale[:, m, bass.ds(t, 1)], in1=wflat[:, bass.ds(at, 512)],
                                         op0=ALU.mult, op1=ALU.subtract).then_inc(sm["wlo"], 1)

            def normalize(i, u):
                if not isinstance(i, int) or i >= 2:
                    dve.wait_ge(sm["xt_ps"], i - 1)
                dve.tensor_scalar(xn[:, u, :], row(i), mean[:, bass.ds(i, 1)], rstd[:, bass.ds(i, 1)],
                                  ALU.subtract, ALU.mult).then_inc(sm["xn_done"], 1)

            def negated_scores(i, u, b):
                dve.wait_ge(sm["sc_ps"], i + 1)
                if not isinstance(i, int) or i >= 2:
                    dve.wait_ge(sm["pt_ps"], i - 1)
                dve.tensor_tensor(sc[:, u, :], pSC[:, 0:C], biasn[:, bass.ds(b, 1), :]
                                  .rearrange("p a c -> p (a c)"), ALU.add).then_inc(sm["sc_sum"], 1)

            def score_maximum(i, u):
                dve.wait_ge(sm["sc_sum"], i + 1)
                dve.tensor_reduce(negmax[:, u:u + 1], sc[:, u, :], AX.X, ALU.min).then_inc(sm["sc_done"], 1)

            def row_factor(i, u, r):
                dve.wait_ge(sm["exp_done"], i + 1)
                dve.reciprocal(rinv[:, u:u + 1], rowsum[:, r:r + 1]).then_inc(sm["rinv_done"], 1)

            def add_attention(i, u):
                dve.wait_ge(sm["rinv_done"], i + 1)
                dve.wait_ge(sm["pv_ps"], i + 1)
                dve.scalar_tensor_tensor(out=row(i), in0=pPV[:, 0:D], scalar=rinv[:, u:u + 1], in1=row(i),
                                         op0=ALU.mult, op1=ALU.add).then_inc(sm["x2_done"], 1)

            def statistics(i):
                dve.wait_ge(sm["x2_done"], i + 1)
                alone(dve)
                dve.bn_stats(stats[:, bass.ds(i, 1), :].rearrange("p a s -> p (a s)"), row(i))\
                    .then_inc(sm["stat_done"], 1)

            def rows_to_sbuf(tau, u):
                dve.wait_ge(sm["xg_t"], tau + 1)
                dve.tensor_copy(xT[u].rearrange("p s k t -> p (s k t)"),
                                pT16.rearrange("p s k t -> p (s k t)")).then_inc(sm["xt_done"], 1)

            def second_norm(z, w, bufs):
                dve.wait_ge(sm["zt_ps"], AHEAD + z - 1)
                dve.wait_ge(sm["z_lo"], AHEAD + z - 1)
                dve.tensor_scalar(bufs[0][:, w % 2, :], row(z), mean[:, bass.ds(z, 1)], rstd[:, bass.ds(z, 1)],
                                  ALU.subtract, ALU.mult).then_inc(sm["z_done"], 1)

            def low(z, w, bufs):
                dve.wait_ge(sm["z_hi"], z + 1)
                dve.tensor_tensor(bufs[2][:, w % 4, D:2 * D], bufs[0][:, w % 2, :], bufs[2][:, w % 4, 0:D],
                                  ALU.subtract).then_inc(sm["z_lo"], 1)

            def group_moment(g, q):
                if q == 0:
                    dve.wait_ge(sm["stat_done"], (g + 1) * GROUP)
                else:
                    dve.wait_ge(sm["moment_step"], g * MOMENT_STEPS + q)
                moment_step(q, g * GROUP, GROUP, ROW_SCALE,
                            lambda ins: ins.then_inc(sm["moment_step"], 1))

            def att(i, b, j):
                one = not isinstance(i, int)
                s, sp_ = j % 4, (j - 1) % 4
                t, tp = b * (JT // 4) + j // 4, b * (JT // 4) + (j - 1) // 4
                moments_beside = one or i >= 2 * GROUP

                def moment(place):
                    q = 5 * s + place
                    if moments_beside and q < MOMENT_STEPS:
                        group_moment(b * (JT // GROUP) + j // GROUP - 2, q)

                scored, added = one or 0 <= i - 1 < NT, one or 0 <= i - 4 < NT
                if one or i >= LN_LAG:
                    dve.wait_ge(sm["moment_step"], MOMENT_STEPS * (b * (JT // GROUP) + j // GROUP - 2))
                    second_norm(i - LN_LAG, s, ln_beside)
                if s % 2 == 0:
                    scale(t, s // 2)
                if one or 0 < i <= NT:
                    weight_low(tp, 2 * sp_)
                moment(0)
                if added:
                    row_factor(i - 4, s % 2, s)
                if scored:
                    negated_scores(i - 1, (s - 1) % 2, b if j >= 1 else b - 1)
                moment(1)
                if added:
                    add_attention(i - 4, s % 2)
                if scored:
                    score_maximum(i - 1, (s - 1) % 2)
                moment(2)
                if added:
                    statistics(i - 4)
                moment(3)
                if one or 0 < i <= NT:
                    weight_low(tp, 2 * sp_ + 1)
                moment(4)
                if one or i + 2 < NT:
                    normalize(i + 2, s % 2)

            normalize(0, 0)
            normalize(1, 1)
            for i in range(FULL * JT):
                att(i, i // JT, i % JT)
            with dve.Fori(FULL, B - 1) as b:
                for j in range(JT):
                    att(b * JT + j, b, j)
            for j in range(JT):
                att(LAST + j, B - 1, j)
            for j in range(3):
                att(NT + j, B, j)
            ONE2 = float(254 << 23)
            link(dve.tensor_scalar(inv1[:, :].bitcast(I32), wscale[:, 0, :].bitcast(I32), -1.0,
                                   ONE2 - float(ROW_SCALE_LOG << 23), ALU.mult, ALU.add))
            link(dve.tensor_scalar(hsc[:, :], wscale[:, 0, :], 2.0 ** -8, None, ALU.mult))
            link(dve.tensor_tensor(inv2[:, :], hsc[:, :], wscale[:, 1, :], ALU.mult))
            link(dve.tensor_scalar(inv2[:, :].bitcast(I32), inv2[:, :].bitcast(I32), -1.0, ONE2,
                                   ALU.mult, ALU.add))
            for a, z in ((0, SH1), (SH1 + ROUTED, NF)):
                for q, src in enumerate((inv1, hsc, inv2)):
                    dve.tensor_copy(tab[:, q, a:z], src[:, 0:1].to_broadcast([P, z - a]))\
                        .then_inc(sm["tabs0"], 1)
            att(NT + 3, B, 3)
            dve.wait_ge(sm["z_lo"], AHEAD + LAST)
            dve.wait_ge(sm["raw_sq"], 4 * NS)
            rows_to_sbuf(0, 0)
            for g in LAST_BANKS[0]:
                weight_low(NS - 1, g)
            dve.wait_ge(sm["moment_step"], MOMENT_STEPS * (NT // GROUP - 1))
            dve.wait_ge(sm["const_ready"], CONSTANTS)

            def hidden_low(tau, g):
                dve.wait_ge(sm["hi_done"], BANKS * tau + g + 1)
                dve.scalar_tensor_tensor(out=hring[:, g, 1, :], in0=sring[:, g % 2, :],
                                         scalar=tab[:, 1, bass.ds(tau, 1)], in1=hring[:, g, 0, :],
                                         op0=ALU.mult, op1=ALU.subtract).then_inc(sm["lo_done"], 1)

            def add_shared(i, tau):
                dve.wait_ge(sm["y_ps"], BANKS * tau + BANKS)
                two = xres[:, bass.ds(2 * i, 2), :].rearrange("p a d -> p (a d)")
                dve.scalar_tensor_tensor(out=two, in0=pY[:, :], scalar=inv2[:, 0:1], in1=two,
                                         op0=ALU.mult, op1=ALU.add).then_inc(sm["y_done"], 1)

            def front(tau):
                add_shared(tau, tau)

            def back(tau):
                add_shared(tau - ROUTED, tau)

            def expert_rows(tau):
                dve.wait_ge(sm["y_ps"], BANKS * tau + BANKS)
                if not isinstance(tau, int) or tau > SH1:
                    dve.wait_ge(sm["y_store"], 16 * (tau - SH1))
                dve.tensor_scalar(ybuf, pY[:, :], tab[:, 2, bass.ds(tau, 1)], None, ALU.mult)\
                    .then_inc(sm["y_done"], 1)

            def ffn(tau, u, finish, more=True, beside=lambda g: None):
                hidden_low(tau, 0)
                beside(0)
                if finish is not None:
                    finish(tau - 1)
                hidden_low(tau, 1)
                beside(1)
                if more:
                    rows_to_sbuf(tau + 1, 1 - u)
                hidden_low(tau, 2)
                beside(2)
                hidden_low(tau, 3)
                beside(3)

            def beside_first(tau, g):
                if tau == 0 and g < 2:
                    for q in LAST_BANKS[g + 1]:
                        weight_low(NS - 1, q)
                if (tau, g) == (0, 1):
                    second_norm(LAST, 0, ln_last)
                if (tau, g) == (0, 2):
                    for q in range(MOMENT_STEPS):
                        group_moment(NT // GROUP - 1, q)
                    dve.wait_ge(sm["moment_step"], MOMENT_STEPS * (NT // GROUP))
                z = last_norm(tau, g)
                if z is not None and z < NT:
                    if z + 1 < NT:
                        second_norm(z + 1, (z + 1) % 4, ln_last)
                    low(z, z % 4, ln_last)

            def over_experts(t):
                return t.rearrange("p (i a) -> p i a", a=1).to_broadcast([P, NT, E])

            def choose():
                dve.wait_ge(sm["lg_ps"], AHEAD + NT)
                link(dve.tensor_copy(lg, pLG))
                first = efirst[:, :].rearrange("p (a e) -> p a e", a=1).to_broadcast([P, NT, E])
                for src, m, sel, oh in ((lg, m1, sel1, oh1), (lg2, m2, sel2, oh2)):
                    link(dve.tensor_reduce(m, by_token(src), AX.X, ALU.max))
                    link(dve.tensor_tensor(by_token(tmp), by_token(src), over_experts(m), ALU.is_ge))
                    link(dve.tensor_tensor(by_token(tmp), by_token(tmp), first, ALU.mult))
                    link(dve.tensor_reduce(sel, by_token(tmp), AX.X, ALU.max))
                    link(dve.tensor_tensor(by_token(oh), by_token(tmp), over_experts(sel), ALU.is_equal))
                    if src is lg:
                        link(dve.scalar_tensor_tensor(out=lg2, in0=oh, scalar=-3.0e38, in1=lg,
                                                      op0=ALU.mult, op1=ALU.add))
                link(dve.tensor_tensor(m2, m2, m1, ALU.subtract))
                dve.memset(rmask, 1.0).then_inc(sm["gate_diff"], 1)
                dve.tensor_tensor(by_expert(slotf[:, 0:128].bitcast(BF16)),
                                  oh1.rearrange("p (i e) -> p e i", e=E),
                                  oh2.rearrange("p (i e) -> p e i", e=E), ALU.add)\
                    .then_inc(sm["mask_ready"], 1)

            def places():
                ones_e, ct, cinc, base = (esm[:, q, :] for q in range(4))
                dve.wait_ge(sm["gate_diff"], 1)
                link(dve.memset(by_expert(rmask)[:, :, 0:1], 0.0))
                link(dve.memset(ones_e, 1.0))
                dve.wait_ge(sm["count_ps"], 1)
                link(dve.tensor_tensor_scan(incl, rmask, pTot[:, 0:NT * E], 0.0, ALU.mult, ALU.add))
                link(dve.tensor_scalar(cnt_i[:, :], by_expert(incl)[:, :, NT - 1], float(R - 1), None, ALU.add))
                link(dve.tensor_scalar(cnt_i[:, :], cnt_i[:, :], R.bit_length() - 1, None,
                                       ALU.logical_shift_right))
                link(dve.tensor_copy(ct, cnt_i[:, :]))
                link(dve.tensor_tensor_scan(cinc, ones_e, ct, 0.0, ALU.mult, ALU.add))
                link(dve.tensor_tensor(base, cinc, ct, ALU.subtract))
                link(dve.tensor_scalar(base, base, float(R), None, ALU.mult))
                link(dve.tensor_tensor(slotf, incl, pTot[:, 0:NT * E], ALU.subtract))
                link(dve.tensor_tensor(slotf, slotf, pPre[:, 0:NT * E], ALU.add))
                link(dve.tensor_tensor(by_expert(slotf), by_expert(slotf),
                                       base.rearrange("p (e a) -> p e a", a=1).to_broadcast([P, E, NT]),
                                       ALU.add))
                for k, oh in enumerate((oh1, oh2)):
                    link(dve.tensor_tensor(by_token(tmp), by_token(oh),
                                           slotf.rearrange("p (e i) -> p i e", e=E), ALU.mult))
                    link(dve.tensor_reduce(posf[:, k, :], by_token(tmp), AX.X, ALU.add))
                pair = lg2[:, 0:2 * NT].bitcast(U32).rearrange("p (k i) -> p k i", k=2)
                link(dve.tensor_copy(slot_u[:, :, :], posf))
                link(dve.tensor_scalar(pair, slot_u[:, :, :], 7, None, ALU.logical_shift_right))
                link(dve.tensor_copy(halff, pair))
                link(dve.tensor_scalar(pair, slot_u[:, :, :], P - 1, None, ALU.bitwise_and))
                link(dve.tensor_copy(posf, pair))

            def one_hot(c):
                k, i0 = c * RC // NT, c * RC % NT

                def spread(t, w):
                    return t.rearrange("p (q a) -> p q a", a=1).to_broadcast([P, RC, w])

                if c:
                    dve.wait_ge(sm["tok_ps"], c)
                link(dve.tensor_tensor(oh_pos, iota_b[:, :].rearrange("p (a n) -> p a n", a=1)
                                       .to_broadcast([P, RC, P]), spread(posf[:, k, i0:i0 + RC], P),
                                       ALU.is_equal))
                link(dve.tensor_tensor(oh_row[0], iota_b[:, 0:HALVES].rearrange("p (a n) -> p a n", a=1)
                                       .to_broadcast([P, RC, HALVES]),
                                       spread(halff[:, k, i0:i0 + RC], HALVES), ALU.is_equal))
                link(dve.tensor_scalar(oh_row[1], oh_row[0], iota_p[:, 0:1], None, ALU.mult))
                dve.tensor_tensor(oh_row[0], oh_row[0], spread(iot[:, i0:i0 + RC], HALVES), ALU.mult)\
                    .then_inc(sm["oneh_ready"], 1)

            def slot_rows():
                dve.wait_ge(sm["tok_ps"], CHUNKS)
                link(dve.tensor_copy(tkf, pTok[:, 0:2 * HALVES]))
                dve.scalar_tensor_tensor(out=tok[:, :], in0=tkf[:, 0:HALVES], scalar=float(P),
                                         in1=tkf[:, HALVES:2 * HALVES], op0=ALU.mult, op1=ALU.add)\
                    .then_inc(sm["slots_ready"], 1)

            def tables():
                cinc = esm[:, 2, :]

                def tiles(t):
                    return t.rearrange("p (j a) -> p j a", a=1).to_broadcast([P, ROUTED, E])

                def experts(t):
                    return t.rearrange("p (a e) -> p a e", a=1).to_broadcast([P, ROUTED, E])

                link(dve.tensor_tensor(eoh, tiles(iot[:, :]), experts(cinc), ALU.is_ge))
                link(dve.tensor_reduce(ejf, eoh, AX.X, ALU.add))
                link(dve.tensor_scalar(ejf, ejf, float(E - 1), None, ALU.min))
                link(dve.tensor_scalar(woff[:, SH1:SH1 + ROUTED], ejf, 1.0, float(SLOT), ALU.add, ALU.mult))
                link(dve.tensor_tensor(eoh, experts(ioe[:, :]), tiles(ejf), ALU.is_equal))
                for q, src in enumerate((inv1, hsc, inv2)):
                    link(dve.tensor_tensor(eot, eoh, experts(src[:, 1:NS]), ALU.mult))
                    link(dve.tensor_reduce(tab[:, q, SH1:SH1 + ROUTED], eot, AX.X, ALU.add))
                dve.sem_inc(sm["routed_ready"], 1)

            def gate_weights():
                dve.wait_ge(sm["gate_exp"], 1)
                link(dve.tensor_scalar(den, ex, 1.0, None, ALU.add))
                link(dve.reciprocal(gates[:, 0, :], den))
                link(dve.tensor_tensor(gates[:, 1, :], ex, gates[:, 0, :], ALU.mult))

            for tau in range(SH1):
                ffn(tau, tau % 2, front if tau else None, more=tau < SH1 - 1,
                    beside=lambda g: beside_first(tau, g))
                if tau == 2:
                    choose()
                if tau == 3:
                    places()
                if tau == 3:
                    tables()
                    gate_weights()
                if 4 <= tau < 4 + CHUNKS:
                    one_hot(tau - 4)
            slot_rows()
            rows_to_sbuf(SH1, SH1 % 2)
            ffn(SH1, SH1 % 2, front)
            tile_pairs(dve, SH1 + 1, SH1 + ROUTED, lambda tau, u: ffn(tau, u, expert_rows))

            def combine(i):
                q = i % 4
                dve.wait_ge(grow_in[q], 32 * (i // 4 + 1))
                for k in range(2):
                    last = dve.scalar_tensor_tensor(out=xres[:, i, :], in0=grow[:, q, k, :],
                                                    scalar=gates[:, k, i:i + 1], in1=xres[:, i, :],
                                                    op0=ALU.mult, op1=ALU.add)
                    if k == 0:
                        link(last)
                last.then_inc(sm["comb_done"], 1)

            for m in range(SH2):
                tau = SH1 + ROUTED + m
                ffn(tau, tau % 2, back if m else expert_rows, more=m < SH2 - 1)
                if m >= 1:
                    for i in combined(m):
                        combine(i)
            back(NF - 1)
            dve.wait_ge(sm["y_done"], NF)
            for i in combined(SH2):
                combine(i)


_INS = ['x', 'ctx_1024', 'L0_xattn_Wk', 'L0_xattn_Wv', 'L0_xattn_bv', 'L0_xattn_Wq', 'L0_xattn_bq',
        'L0_xattn_Wo', 'L0_xattn_bo', 'L0_ffn_shared_w1', 'L0_ffn_shared_w2', 'L0_ffn_experts_w1',
        'L0_ffn_experts_w2', 'L0_ffn_gate_w']
_OUTS = [((4, 1024, 256), 'float32')]


def kernel(**inputs):
    import numpy as _np
    import concourse.bacc as _bacc
    from concourse import mybir as _mybir
    from concourse.bass_utils import run_bass_kernel_spmd as _run

    nc = _bacc.Bacc("TRN2", target_bir_lowering=False, num_devices=1, dynamic_dma_scratch_size=4096)
    arrays, args = {}, []
    for name in _INS:
        a = _np.ascontiguousarray(inputs[name])
        arrays[f"in_{name}_dram"] = a
        args.append(nc.dram_tensor(f"in_{name}_dram", a.shape, _mybir.dt.from_np(a.dtype), kind="ExternalInput").ap())
    for i, (shape, dtype) in enumerate(_OUTS):
        dt = _mybir.dt.from_np(_np.dtype(dtype))
        args.append(nc.dram_tensor(f"out_{i}_dram", shape, dt, kind="ExternalOutput").ap())
    xattn_moe_kernel(nc, *args)
    r = _run(nc, [arrays], core_ids=[0])
    got = tuple(r.results[0][f"out_{i}_dram"] for i in range(len(_OUTS)))
    return got[0]
```

```python
from contextlib import ExitStack

import concourse.bass as bass
from concourse import mybir

F32 = mybir.dt.float32
F16 = mybir.dt.float16
BF16 = mybir.dt.bfloat16
I32 = mybir.dt.int32
U32 = mybir.dt.uint32
ALU = mybir.AluOpType
ACT = mybir.ActivationFunctionType
AX = mybir.AxisListType
SUM = bass.bass_isa.ReduceOp.add

P = 128


def xattn_moe_kernel(nc, x, ctx_in, Wk, Wv, bv, Wq, bq, Wo, bo, sw1, sw2, ew1, ew2, gate_w, out):
    B, S, D = x.shape
    C = ctx_in.shape[1]
    E, HID, _ = ew1.shape
    KD = D // P
    KH = HID // P
    C2 = C - P
    NT = B * S // P
    JT = S // P
    R = 2 * P
    SHARED = B * S // R
    ROUTED = (2 * B * S + E * (R - 1)) // R
    SH1 = 9
    SH2 = SHARED - SH1
    NF = SHARED + ROUTED
    HALVES = 2 * ROUTED
    BANKS = HID * R // P // 512
    CB = KH // BANKS
    NS = E + 1
    SLOT = 4 * KD * HID
    EPS = 1e-5
    ROW_SCALE_LOG = 11
    ROW_SCALE = float(1 << ROW_SCALE_LOG)
    NEG_SCALE = -float(D) ** -0.5
    LAST = NT - JT
    GROUP = 4
    MOMENT_STEPS = 17
    LN_LAG = 12
    AHEAD = 4
    CONSTANTS = 7
    assert B == 4 and KD == 2 and CB * R == 512 and D * 2 == 512 and NT % 4 == 0

    with ExitStack() as es:
        def sb(name, shape, dt):
            return es.enter_context(nc.sbuf_tensor(name, shape, dt))

        def sem(name):
            return es.enter_context(nc.semaphore(name))

        rows_dram = nc.dram_tensor("ln_rows", [NT * P, 2 * D], F16, kind="Internal").ap()
        y_dram = nc.dram_tensor("expert_rows", [ROUTED * R, D], F32, kind="Internal").ap()

        wts = sb("wts", [P, NS, SLOT], F16)
        xres = sb("xres", [P, NT, D], F32)
        stage = sb("stage", [P, 2048], F32)
        work = sb("work", [P, 5120], F32)
        identf = sb("identf", [P, P], F32)
        ident16 = sb("ident16", [P, P], F16)
        upper = sb("upper", [P, P], BF16)
        ones_b = sb("ones_b", [P, P], BF16)
        iota_b = sb("iota_b", [P, P], BF16)
        iota_p = sb("iota_p", [P, 1], F32)
        gateT = sb("gateT", [P, KD, E], F32)
        stats = sb("stats", [P, NT, 6], F32)
        mean = sb("mean", [P, NT], F32)
        rstd = sb("rstd", [P, NT], F32)
        nt_a = sb("nt_a", [P, NT], F32)
        nt_v = sb("nt_v", [P, NT], F32)
        nt_b = sb("nt_b", [P, NT], F32)
        rowsum = sb("rowsum", [P, 4], F32)
        rinv = sb("rinv", [P, 2], F32)
        negmax = sb("negmax", [P, 2], F32)
        unread = sb("unread", [P, 1], F32)
        psq = sb("psq", [P, 2, 2], F32)
        asq = sb("asq", [P, 2, 2], F32)
        norm2 = sb("norm2", [P, 2], F32)
        ebits = sb("ebits", [P, 2], I32)
        wscale = sb("wscale", [P, 2, NS], F32)
        inv1 = sb("inv1", [P, NS], F32)
        hsc = sb("hsc", [P, NS], F32)
        inv2 = sb("inv2", [P, NS], F32)
        tab = sb("tab", [P, 3, NF], F32)
        woff = sb("woff", [P, NF], I32)
        tok = sb("tok", [P, HALVES], U32)
        idx = sb("idx", [P, 2], U32)
        slot_u = sb("slot_u", [P, 2, NT], U32)
        gates = sb("gates", [P, 2, NT], F32)

        wflat = wts[:, :, :].rearrange("p s n -> p (s n)")
        NSL = NS - 1
        att = wts[:, NSL, :].bitcast(F32)
        ktn = att[:, 0:B * KD * C].rearrange("p (b k c) -> p b k c", b=B, k=KD)
        o = B * KD * C
        vct = att[:, o:o + B * 2 * D].rearrange("p (b k d) -> p b k d", b=B, k=2)
        o += B * 2 * D
        biasn = att[:, o:o + B * C].rearrange("p (b c) -> p b c", b=B)
        su = wts[:, NSL - 3:NSL, :].rearrange("p s n -> p (s n)").bitcast(F32)
        rawk, rawv, rawq, rawo, woT, fa, fc = (
            su[:, 512 * i:512 * i + 512].rearrange("p (c d) -> p c d", c=2) for i in range(7))
        o = 3584
        craw = su[:, o:o + B * 512].rearrange("p (b k d) -> p b k d", b=B, k=2)
        o += B * 512
        ctxT = su[:, o:o + B * KD * C].rearrange("p (b k c) -> p b k c", b=B, k=KD)
        o += B * KD * C
        ones_f = su[:, o:o + 128]
        ubc = su[:, o + 128:o + 384].rearrange("p (k n) -> p k n", k=2)
        bvbc = su[:, o + 384:o + 640].rearrange("p (k n) -> p k n", k=2)
        cbs = su[:, o + 640:o + 896]
        bq_c = su[:, o + 896:o + 898]
        bv_c = su[:, o + 898:o + 900]
        u_c = su[:, o + 900:o + 902]
        bo_r = su[0:1, o + 902:o + 1158]
        graw = su[0:E, o + 1158:o + 1158 + D]
        assert o + 1158 + D <= 3 * SLOT // 2

        xn = work[:, 0:512].rearrange("p (u d) -> p u d", u=2)
        xnT = work[:, 512:1024].rearrange("p (u k t) -> p u k t", u=2, k=2)
        sc = work[:, 1024:1024 + 2 * C].rearrange("p (u c) -> p u c", u=2)
        pT = work[:, 1408:1920].rearrange("p (u k t) -> p u k t", u=2, k=2)
        rout = sb("rout", [P, 2048], F32)
        raws = [stage[:, :], rout[:, :]]
        squares = work[:, 4608:5120].bitcast(BF16)

        def ln_buffers(t):
            return (t[:, 0:512].rearrange("p (u d) -> p u d", u=2),
                    t[:, 512:1024].rearrange("p (u k t) -> p u k t", u=2, k=2),
                    t[:, 1024:2048].bitcast(F16).rearrange("p (u d) -> p u d", u=4))

        ln_beside = ln_buffers(work[:, 1920:3968])
        ln_last = ln_buffers(stage[:, :])
        hring = work[:, 0:2048].bitcast(F16).rearrange("p (g s n) -> p g s n", g=BANKS, s=2)
        sring = work[:, 2048:3072].rearrange("p (g n) -> p g n", g=2)
        xT = [work[:, a:a + 512].bitcast(F16).rearrange("p (s k t) -> p s k t", s=2, k=2)
              for a in (4608, 3072)]
        xg = work[:, 4096:4608].bitcast(F16).rearrange("p (h d) -> p h d", h=2)
        ybuf = work[:, 3584:4096]

        def table(i):
            return rout[:, 256 * i:256 * (i + 1)]
        lg, tmp, oh1, oh2, lg2, incl, slotf, rmask = (table(i) for i in range(8))

        def by_token(t):
            return t.rearrange("p (i e) -> p i e", e=E)

        def by_expert(t):
            return t.rearrange("p (e i) -> p e i", e=E)

        nt32 = sb("nt32", [P, 8, NT], F32)
        m1, m2, sel1, sel2, ex, den = (nt32[:, i, :] for i in range(6))
        posf = nt32[:, 6:8, :]
        half_b = sb("half_b", [P, 2, NT], BF16)
        place_b = sb("place_b", [P, 2, NT], BF16)
        esm = sb("esm", [P, 6, E], F32)
        cnt_i = sb("cnt_i", [P, E], I32)
        efirst = sb("efirst", [P, E], F32)
        RC = 8
        CHUNKS = 2 * NT // RC
        oh_pos = [stage[:, RC * P // 2 * u:RC * P // 2 * (u + 1)].bitcast(BF16)
                  .rearrange("p (q n) -> p q n", q=RC) for u in range(2)]
        hw = RC * HALVES // 2
        oh_row = [[rout[:, hw * q:hw * (q + 1)].bitcast(BF16).rearrange("p (q n) -> p q n", q=RC)
                   for q in (2 * u, 2 * u + 1)] for u in range(2)]
        assert 4 * hw <= 1280 and NT % RC == 0
        tkf = rout[:, 1280:1280 + 2 * HALVES]
        eoh = stage[:, 1024:1024 + ROUTED * E].rearrange("p (j e) -> p j e", e=E)
        eot = stage[:, 1344:1344 + ROUTED * E].rearrange("p (j e) -> p j e", e=E)
        ejf = stage[:, 1664:1664 + ROUTED]
        iot = sb("iot", [P, ROUTED], F32)
        ioe = sb("ioe", [P, E], F32)
        grow = stage[:, 0:2048].rearrange("p (u k d) -> p u k d", u=4, k=2)

        ps = [es.enter_context(nc.psum_tensor(f"bank{i}", [P, 512], F32)) for i in range(8)]
        pXT, pSC, pPT, pPV = ps[0:4]
        pW = [ps[4 + q] for q in (0, 1, 2, 0, 1, 2, 0, 1)]
        W_BACK = (2, 2, 5, 3, 3, 3, 3, 3)
        pZT, pLG = ps[7][:, 0:D], ps[7][:, D:D + NT * E]
        pH = [ps[i] for i in range(BANKS)]
        pY, pT16 = ps[4], ps[5][:, :].bitcast(F16).rearrange("p (s k t) -> p s k t", s=2, k=2)
        pPre, pTot, pTok = ps[6], ps[7], ps[6]

        names = """x0 x1 x2 x3 w_in c_in b_in const_ready ones_ready u_ready bv_bc u_bc su_pe su_ev values_ready dchain
            pchain raw_in0 raw_in1 raw_sq all_sq scale_step moment_step scale_ready wt_ps whi wlo xn_done xt_ps
            xnt_done sc_ps sc_sum sc_done exp_done pt_ps ptt_done pv_ps rinv_done x2_done stat_done
            z_done z_hi z_lo zt_ps ztt_done lg_ps rows0 rows1 rows2 rows3 gate_diff gate_exp mask_ready count_ps
            oneh_ready tok_ps routed_ready offsets_ready slots_ready tabs0 rows_in back_rows xg_t xt_done h_ps
            silu_done hi_done lo_done y_ps y_done y_store idx_ready grow_in0 grow_in1 grow_in2 grow_in3 comb_part
            comb_done out_st passed""".split()
        sm = {n: sem(n) for n in names}
        raw_in = [sm["raw_in0"], sm["raw_in1"]]
        rows_st = [sm[f"rows{i}"] for i in range(4)]
        grow_in = [sm[f"grow_in{i}"] for i in range(4)]

        block = es.enter_context(nc.Block())

        def alone(eng):
            eng.sem_inc(sm["passed"], 1)

        def combined(m):
            ends = [0] + [min(-(-NT * q // (SH2 - 1)), 2 * (SH1 + q)) for q in range(1, SH2)] + [NT]
            return range(ends[m - 1], ends[m])

        FULL = -(-LN_LAG // JT)

        def of_first(b):
            return isinstance(b, int) and b == 0

        CHOOSE, COUNT, PLACES, ONE_HOT = 10, 13, 13, 16
        TABLES = ONE_HOT + 2 * CHUNKS
        assert TABLES + 3 <= BANKS * SH1

        def last_norm(tau, g):
            z = LAST + BANKS * tau + g - 1
            return z if LAST <= z <= NT else None

        def w1_part(slot_off, s, k, lo, n):
            at = slot_off + (s * KD + k) * HID + lo
            return wflat[:, bass.ds(at, n)]

        def w2_part(slot_off, s, c):
            at = slot_off + 2 * KD * HID + (s * KH + c) * D
            return wflat[:, bass.ds(at, D)]

        def tile_pairs(eng, lo, hi, body):
            if lo % 2 and lo < hi:
                body(lo, 1)
                lo += 1
            pairs = (hi - lo) // 2
            if pairs > 1:
                with eng.Fori(lo // 2, lo // 2 + pairs) as t:
                    body(2 * t, 0)
                    body(2 * t + 1, 1)
                lo += 2 * pairs
            while lo < hi:
                body(lo, lo % 2)
                lo += 1

        @block.sync
        def _(sp):
            sp.dma_start(craw[:, :, 0, :], ctx_in[:, 0:P, :].rearrange("b p d -> p b d")).then_inc(sm["c_in"], 16)
            sp.dma_start(craw[0:C2, :, 1, :], ctx_in[:, P:C, :].rearrange("b p d -> p b d"))\
                .then_inc(sm["c_in"], 16)
            for t, w in ((rawk, Wk), (rawq, Wq), (rawv, Wv)):
                sp.dma_start(t, w.rearrange("(p c) d -> p c d", c=2)).then_inc(sm["w_in"], 16)
            sp.dma_start(rawo, Wo.rearrange("(c p) d -> p c d", p=P)).then_inc(sm["w_in"], 16)
            sp.dma_start(bq_c, bq.rearrange("(p c) -> p c", c=2)).then_inc(sm["b_in"], 16)
            sp.dma_start(bv_c, bv.rearrange("(p c) -> p c", c=2)).then_inc(sm["b_in"], 16)
            sp.dma_start(bo_r, bo.rearrange("(a d) -> a d", a=1)).then_inc(sm["b_in"], 16)
            sp.dma_start(graw, gate_w).then_inc(sm["b_in"], 16)
            for b in range(B):
                sp.dma_start(xres[:, b * JT:(b + 1) * JT, :],
                             x[b].rearrange("(p j) d -> p j d", j=JT)).then_inc(sm[f"x{b}"], 16)

            def load_w1(t, src):
                if not isinstance(t, int) or t > 0:
                    sp.wait_ge(sm["wt_ps"], 8 * t - 4)
                sp.dma_start(raws[0].rearrange("p (c d) -> p c d", c=KH), src).then_inc(raw_in[0], 16)

            def load_w2(t, src):
                if not isinstance(t, int) or t > 0:
                    sp.wait_ge(sm["wt_ps"], 8 * t)
                sp.dma_start(raws[1].rearrange("p (a h) -> p a h", a=KD), src).then_inc(raw_in[1], 16)

            load_w1(0, sw1.rearrange("(c p) d -> p c d", p=P))
            load_w2(0, sw2.rearrange("(a p) h -> p a h", p=P))

            def load_expert_w1(t):
                load_w1(t, ew1[bass.ds(t - 1, 1)].rearrange("a (c p) d -> p (a c) d", p=P))

            def load_expert_w2(t):
                load_w2(t, ew2[bass.ds(t - 1, 1)].rearrange("a (q p) h -> p (a q) h", p=P))

            def store_rows(z, w, zrow):
                sp.wait_ge(sm["z_lo"], AHEAD + z + 1)
                sp.dma_start(rows_dram[bass.ds(z * P, P), :], zrow[:, w, :]).then_inc(rows_st[w], 16)

            for q in range(4):
                sp.sem_inc(rows_st[q], 4 * AHEAD)
            SLOTS0 = LN_LAG // 4
            for t in range(SLOTS0):
                load_expert_w1(t + 1)
                load_expert_w2(t + 1)
            with sp.Fori(SLOTS0, NS - 1) as t:
                z = 4 * t - LN_LAG
                store_rows(z, 0, ln_beside[2])
                load_expert_w1(t + 1)
                store_rows(z + 1, 1, ln_beside[2])
                store_rows(z + 2, 2, ln_beside[2])
                load_expert_w2(t + 1)
                store_rows(z + 3, 3, ln_beside[2])
            for q in range(4):
                store_rows(LAST - 4 + q, q, ln_beside[2])
            for z in range(LAST, NT):
                store_rows(z, z % 4, ln_last[2])

            def store_y(j, u):
                sp.wait_ge(sm["y_done"], j + SH1 + 1)
                sp.dma_start(y_dram[bass.ds(j * R, R), :].rearrange("(h p) d -> p h d", p=P),
                             ybuf.rearrange("p (h d) -> p h d", h=2)).then_inc(sm["y_store"], 16)

            tile_pairs(sp, 0, ROUTED, store_y)

            def store_result(i):
                sp.wait_ge(sm["comb_done"], i + 2)
                if i // 2 >= SH1:
                    sp.wait_ge(sm["y_done"], ROUTED + i // 2 + 1)
                b, j = i // JT, i % JT
                sp.dma_start(out[b].rearrange("(p j) d -> p j d", j=JT)[:, j:j + 2, :],
                             xres[:, i:i + 2, :]).then_inc(sm["out_st"], 16)

            stored = 0
            for m in range(1, SH2 + 1):
                if m + 1 < SH2:
                    tau = SH1 + ROUTED + m + 1
                    sp.wait_ge(sm["xg_t"], tau)
                    for h in range(2):
                        sp.dma_start(xg[:, h, :], rows_dram[bass.ds((tau - ROUTED) * R + h * P, P), :])\
                            .then_inc(sm["back_rows"], 16)
                done = NT if m == SH2 else combined(m - 1).stop if m > 1 else 0
                while stored + 2 <= done:
                    store_result(stored)
                    stored += 2
            sp.wait_ge(sm["out_st"], 16 * NT // 2)

        @block.gpsimd
        def _(pool):
            n = [0]

            def link(ins):
                n[0] += 1
                ins.then_inc(sm["pchain"], 1)
                pool.wait_ge(sm["pchain"], n[0])

            link(pool.memset(identf[:, :], 0.0))
            pool.affine_select(out=identf[:, :], in_=identf[:, :], compare_op=ALU.not_equal, fill=1.0,
                               base=0, pattern=[[-1, P]], channel_multiplier=1).then_inc(sm["const_ready"], 1)
            link(pool.memset(ident16[:, :], 0.0))
            link(pool.affine_select(out=ident16[:, :], in_=ident16[:, :], compare_op=ALU.not_equal, fill=1.0,
                                    base=0, pattern=[[-1, P]], channel_multiplier=1))
            link(pool.memset(ones_b[:, :], 1.0))
            link(pool.affine_select(out=upper[:, :], in_=ones_b[:, :], compare_op=ALU.is_gt, fill=0.0,
                                    base=0, pattern=[[1, P]], channel_multiplier=-1))
            pool.iota(iota_b[:, :], pattern=[[1, P]], base=0, channel_multiplier=0,
                      allow_small_or_imprecise_dtypes=True).then_inc(sm["const_ready"], 1)
            pool.iota(iota_p[:, :], pattern=[[1, 1]], base=0, channel_multiplier=1,
                      allow_small_or_imprecise_dtypes=True).then_inc(sm["const_ready"], 1)
            pool.iota(efirst[:, :], pattern=[[-1, E]], base=E, channel_multiplier=0,
                      allow_small_or_imprecise_dtypes=True).then_inc(sm["const_ready"], 1)
            pool.memset(woff[:, :], 0).then_inc(sm["const_ready"], 1)
            for t_, n_ in ((iot, ROUTED), (ioe, E)):
                pool.iota(t_[:, :], pattern=[[1, n_]], base=0, channel_multiplier=0,
                          allow_small_or_imprecise_dtypes=True).then_inc(sm["const_ready"], 1)

            def across(t, m):
                pool.wait_ge(sm["raw_sq"], 4 * t + 2 * m + 2)
                if not isinstance(t, int) or t > 0:
                    pool.wait_ge(sm["scale_ready"], 2 * t + m - 1)
                alone(pool)
                pool.partition_all_reduce(asq[:, m, :], psq[:, m, :], P, SUM)\
                    .then_inc(sm["all_sq"], 1)

            def split(z, w):
                zf, _, zrow = ln_beside
                pool.wait_ge(sm["z_done"], z + 1)
                pool.wait_ge(rows_st[w], 4 * (AHEAD + z - w))
                alone(pool)
                pool.tensor_copy(zrow[:, w % 4, 0:D], zf[:, w % 2, :]).then_inc(sm["z_hi"], 1)
                pool.wait_ge(sm["z_hi"], z + 1)
                pool.tensor_tensor(zrow[:, w % 4, D:2 * D], zf[:, w % 2, :], zrow[:, w % 4, 0:D],
                                   ALU.subtract).then_inc(sm["z_lo"], 1)

            pool.sem_inc(sm["z_lo"], AHEAD)
            across(0, 0)
            for t in range(LN_LAG // 4):
                across(t, 1)
                across(t + 1, 0)

            def slot_part(t):
                z = 4 * t - LN_LAG
                split(z, 0)
                across(t, 1)
                split(z + 1, 1)
                split(z + 2, 2)
                if not isinstance(t, int):
                    across(t + 1, 0)
                split(z + 3, 3)

            with pool.Fori(LN_LAG // 4, NS - 1) as t:
                slot_part(t)
            for q in range(2):
                pool.wait_ge(rows_st[q], 4 * (AHEAD + 4))
            pool.dma_start(xg[:, :, :], rows_dram[0:R, :].rearrange("(h p) d -> p h d", p=P))\
                .then_inc(sm["rows_in"], 32)
            slot_part(NS - 1)

            for q in range(4):
                pool.wait_ge(rows_st[q], 4 * (AHEAD + LAST))

            def rows_in_order(i, tau, u):
                pool.wait_ge(sm["xg_t"], tau)
                alone(pool)
                pool.dma_start(xg[:, :, :], rows_dram[bass.ds(i * R, R), :].rearrange("(h p) d -> p h d", p=P))\
                    .then_inc(sm["rows_in"], 32)

            def rows_by_slot(j, u):
                pool.wait_ge(sm["xg_t"], j + SH1)
                alone(pool)
                pool.tensor_copy(idx[:, :], tok[:, bass.ds(2 * j, 2)]).then_inc(sm["idx_ready"], 1)
                pool.wait_ge(sm["idx_ready"], j + 1)
                alone(pool)
                for h in range(2):
                    pool.indirect_dma_start(xg[:, h, :], None, rows_dram,
                                            bass.IndirectOffsetOnAxis(idx[:, h:h + 1], 0))\
                        .then_inc(sm["rows_in"], 16)

            tile_pairs(pool, 1, SH1, lambda i, u: rows_in_order(i, i, u))
            for q in range(4):
                pool.wait_ge(rows_st[q], 4 * (AHEAD + NT))
            pool.wait_ge(sm["slots_ready"], 1)
            tile_pairs(pool, 0, ROUTED, rows_by_slot)

            def gather_outputs(i):
                q = i % 4
                if i >= 4:
                    pool.wait_ge(sm["comb_done"], i - 3)
                for k in range(2):
                    pool.indirect_dma_start(grow[:, q, k, :], None, y_dram,
                                            bass.IndirectOffsetOnAxis(slot_u[:, k, i:i + 1], 0))\
                        .then_inc(grow_in[q], 16)

            for m in range(2):
                rows_in_order(SH1 + m, SH1 + ROUTED + m, 0)
            pool.wait_ge(sm["y_store"], 16 * ROUTED)
            for m in range(1, SH2):
                for i in combined(m):
                    gather_outputs(i)
            for i in combined(SH2):
                gather_outputs(i)

        @block.tensor
        def _(pe):
            pe.wait_ge(sm["const_ready"], 1)
            pe.wait_ge(sm["c_in"], 16 * 2)
            n = [0]

            def bank_read(step):
                batch, part = divmod(step - 9, 3)
                if step < 9:
                    pe.wait_ge(sm["su_ev"], step + 1)
                elif part < 2:
                    pe.wait_ge(sm["su_ev"], 9 + 2 * batch + part + 1)
                else:
                    pe.wait_ge(sm["values_ready"], batch + 1)

            def bank():
                b = n[0] % 4
                if n[0] >= 4:
                    bank_read(n[0] - 4)
                n[0] += 1
                return ps[b]

            for b in range(B):
                q = bank()
                for k in range(KD):
                    pe.transpose(q[:, k * 256:k * 256 + P], craw[:, b, 0, k * P:(k + 1) * P], identf[:, :])
                    last = pe.transpose(q[:, k * 256 + P:k * 256 + C], craw[0:C2, b, 1, k * P:(k + 1) * P],
                                        identf[0:C2, 0:C2])
                last.then_inc(sm["su_pe"], 1)
            pe.wait_ge(sm["w_in"], 64)
            pe.wait_ge(sm["b_in"], 64)
            q = bank()
            for c in range(2):
                for r in range(2):
                    last = pe.transpose(q[:, c * 256 + r * P:c * 256 + (r + 1) * P],
                                        rawo[:, r, c:D:2], identf[:, :])
            last.then_inc(sm["su_pe"], 1)
            q = bank()
            for a in range(KD):
                for c in range(2):
                    last = pe.matmul(q[:, a * 256:(a + 1) * 256], rawk[:, c, a * P:(a + 1) * P], rawq[:, c, :],
                                     start=(c == 0), stop=(c == 1))
            last.then_inc(sm["su_pe"], 1)
            q = bank()
            for a in range(KD):
                for c in range(2):
                    pe.matmul(q[:, a:a + 1], rawk[:, c, a * P:(a + 1) * P], bq_c[:, c:c + 1],
                              start=(c == 0), stop=(c == 1))
            for k in range(KD):
                last = pe.transpose(q[:, 16 + k * E:16 + (k + 1) * E], graw[:, k * P:(k + 1) * P],
                                    identf[0:E, 0:E])
            last.then_inc(sm["su_pe"], 1)
            pe.wait_ge(sm["su_ev"], 5)
            q = bank()
            for a in range(KD):
                for c in range(2):
                    last = pe.matmul(q[:, a * 256:(a + 1) * 256], rawv[:, c, a * P:(a + 1) * P], woT[:, c, :],
                                     start=(c == 0), stop=(c == 1))
            last.then_inc(sm["su_pe"], 1)
            q = bank()
            pe.wait_ge(sm["bv_bc"], 1)
            for c in range(2):
                pe.matmul(q[:, 0:D], bvbc[:, c, :], woT[:, c, :], start=(c == 0), stop=False)
            pe.matmul(q[:, 0:D], ones_f[0:1, :], bo_r, start=False, stop=True).then_inc(sm["su_pe"], 1)
            for b in range(B):
                q = bank()
                pe.wait_ge(sm["su_ev"], 6)
                for r in range(KD):
                    for a in range(KD):
                        last = pe.matmul(q[:, r * 256:r * 256 + C], fa[:, a, r * P:(r + 1) * P],
                                         ctxT[:, b, a, :], start=(a == 0), stop=(a == 1))
                last.then_inc(sm["su_pe"], 1)
                q = bank()
                pe.wait_ge(sm["u_bc"], 1)
                for a in range(KD):
                    last = pe.matmul(q[:, 0:C], ubc[:, a, :], ctxT[:, b, a, :], start=(a == 0), stop=(a == 1))
                last.then_inc(sm["su_pe"], 1)
                q = bank()
                pe.wait_ge(sm["su_ev"], 9)
                for r, rows in ((0, P), (1, C2)):
                    for a in range(KD):
                        last = pe.matmul(q[0:rows, r * 256:(r + 1) * 256], ctxT[:, b, a, r * P:r * P + rows],
                                         fc[:, a, :], start=(a == 0), stop=(a == 1))
                last.then_inc(sm["su_pe"], 1)
            bank_read(n[0] - 2)
            bank_read(n[0] - 1)

            def transpose_x(i, u):
                pe.wait_ge(sm["xn_done"], i + 1)
                if not isinstance(i, int) or i > 0:
                    pe.wait_ge(sm["xnt_done"], i)
                for k in range(KD):
                    last = pe.transpose(pXT[:, k * P:(k + 1) * P], xn[:, u, k * P:(k + 1) * P], identf[:, :])
                last.then_inc(sm["xt_ps"], 1)

            def scores(i, u, b):
                pe.wait_ge(sm["xnt_done"], i + 1)
                if not isinstance(i, int) or i > 0:
                    pe.wait_ge(sm["sc_done"], i)
                for k in range(KD):
                    last = pe.matmul(pSC[:, 0:C], xnT[:, u, k, :],
                                     ktn[:, bass.ds(b, 1), k, :].rearrange("p a c -> p (a c)"),
                                     start=(k == 0), stop=(k == 1))
                last.then_inc(sm["sc_ps"], 1)

            def transpose_p(i, u):
                pe.wait_ge(sm["exp_done"], i + 1)
                if not isinstance(i, int) or i > 0:
                    pe.wait_ge(sm["ptt_done"], 2 * i)
                pe.transpose(pPT[:, 0:P], sc[:, u, 0:P], identf[:, :])
                pe.transpose(pPT[0:C2, P:2 * P], sc[:, u, P:C], identf[:, :]).then_inc(sm["pt_ps"], 1)

            def values(i, u, b):
                pe.wait_ge(sm["ptt_done"], 2 * i + 2)
                if not isinstance(i, int) or i > 0:
                    pe.wait_ge(sm["x2_done"], i)
                pe.matmul(pPV[:, 0:D], pT[:, u, 0, :], vct[:, bass.ds(b, 1), 0, :].rearrange("p a d -> p (a d)"),
                          start=True, stop=False)
                pe.matmul(pPV[:, 0:D], pT[0:C2, u, 1, :],
                          vct[0:C2, bass.ds(b, 1), 1, :].rearrange("p a d -> p (a d)"),
                          start=False, stop=True).then_inc(sm["pv_ps"], 1)

            def weight_bank(t, g):
                q = pW[g]
                m = g // 4
                if g % 4 == 0:
                    pe.wait_ge(raw_in[m], 16 * t + 16)
                if g >= 3 or not isinstance(t, int) or t > 0:
                    pe.wait_ge(sm["wlo"], 8 * t + g + 1 - W_BACK[g])
                for r in range(4):
                    if m == 0:
                        k, c = g // 2, (g % 2) * 4 + r
                        src = raws[0][:, c * D + k * P:c * D + (k + 1) * P]
                    else:
                        c, a = 2 * (g - 4) + r // 2, r % 2
                        src = raws[1][:, a * HID + c * P:a * HID + (c + 1) * P]
                    last = pe.transpose(q[:, r * P:(r + 1) * P], src, identf[:, :])
                last.then_inc(sm["wt_ps"], 1)

            TRANSFERS = ((None, 0, 1), (2, 3, None), (4, 5, None), (6, 7, None))

            def step(i, t, s, b1, b3, beside=lambda place: None):
                start, middle, end = TRANSFERS[s]
                if not isinstance(i, int) or i >= 1:
                    scores(i - 1, (s - 1) % 2, b1)
                transpose_x(i, s % 2)
                if start is not None:
                    weight_bank(t, start)
                weight_bank(t, middle)
                beside(0)
                if not isinstance(i, int) or i >= 2:
                    transpose_p(i - 2, s % 2)
                if not isinstance(i, int) or i >= 3:
                    values(i - 3, (s - 3) % 2, b3)
                if end is not None:
                    weight_bank(t, end)
                beside(1)

            def transpose_z(z, w, bufs):
                pe.wait_ge(sm["z_done"], z + 1)
                for k in range(KD):
                    last = pe.transpose(pZT[:, k * P:(k + 1) * P],
                                        bufs[0][:, w % 2, k * P:(k + 1) * P], identf[:, :])
                last.then_inc(sm["zt_ps"], 1)

            def logits(z, w, bufs):
                pe.wait_ge(sm["ztt_done"], AHEAD + z + 1)
                for k in range(KD):
                    last = pe.matmul(pLG[:, bass.ds(z * E, E)], bufs[1][:, w % 2, k, :], gateT[:, k, :],
                                     start=(k == 0), stop=(k == 1))
                last.then_inc(sm["lg_ps"], 1)

            pe.sem_inc(sm["zt_ps"], AHEAD)
            pe.sem_inc(sm["lg_ps"], AHEAD)

            def norm_beside(i, s):
                z = i - LN_LAG
                if not isinstance(i, int) or z > 0:
                    logits(z - 1, (s + 3) % 4, ln_beside)
                transpose_z(z, s, ln_beside)

            def batch(b):
                for j in range(JT):
                    i = b * JT + j

                    def beside(place):
                        if place == 0 and (not isinstance(i, int) or i >= LN_LAG):
                            norm_beside(i, j % 4)

                    step(i, b * (JT // 4) + j // 4, j % 4, b if j >= 1 or of_first(b) else b - 1,
                         b if j >= 3 or of_first(b) else b - 1, beside)

            for b in range(FULL):
                batch(b)
            with pe.Fori(FULL, B) as b:
                batch(b)
            for i in range(NT, NT + 4):
                if i - 1 < NT:
                    scores(i - 1, (i - 1) % 2, B - 1)
                if i - 2 < NT:
                    transpose_p(i - 2, i % 2)
                norm_beside(i, i % 4)
                if i - 3 < NT:
                    values(i - 3, (i - 3) % 2, B - 1)
            for g in range(4):
                weight_bank(NS - 1, g)
            logits(LAST - 1, 3, ln_beside)

            def transpose_rows(tau, u, by_sp=False):
                if by_sp:
                    pe.wait_ge(sm["back_rows"], 32 * (tau - SH1 - ROUTED - 1))
                else:
                    pe.wait_ge(sm["rows_in"], 32 * tau + 32)
                if not isinstance(tau, int) or tau > 0:
                    pe.wait_ge(sm["xt_done"], tau)
                if isinstance(tau, int) and tau == 1:
                    pe.wait_ge(sm["wlo"], 8 * NS)
                for h in range(2):
                    for s in range(2):
                        for k in range(KD):
                            last = pe.transpose(pT16[:, s, k, h * P:(h + 1) * P],
                                                xg[:, h, s * D + k * P:s * D + (k + 1) * P], ident16[:, :])
                last.then_inc(sm["xg_t"], 1)

            def up(tau, u, g, off):
                n = BANKS * tau + g
                if g == 0:
                    pe.wait_ge(sm["xt_done"], tau + 1)
                if not isinstance(tau, int) or tau > 0:
                    pe.wait_ge(sm["silu_done"], n - BANKS + 1)
                for r in range(CB):
                    c = g * CB + r
                    first = True
                    for k in range(KD):
                        for sw, sx in ((0, 0), (0, 1), (1, 0)):
                            last = pe.matmul(pH[g][:, r * R:(r + 1) * R], w1_part(off, sw, k, c * P, P),
                                             xT[u][:, sx, k, :], start=first, stop=(k == 1 and sw == 1))
                            first = False
                last.then_inc(sm["h_ps"], 1)

            def down(tau, g, off):
                pe.wait_ge(sm["lo_done"], BANKS * tau + g + 1)
                if g == 0 and (not isinstance(tau, int) or tau > 0):
                    pe.wait_ge(sm["y_done"], tau)
                for r in range(CB):
                    c = g * CB + r
                    for sw, sh in ((0, 0), (0, 1), (1, 0)):
                        for h in range(2):
                            first = g == 0 and r == 0 and sw == 0 and sh == 0
                            last = pe.matmul(
                                pY[:, h * D:(h + 1) * D],
                                hring[:, g, sh, r * R + h * P:r * R + (h + 1) * P],
                                w2_part(off, sw, c), start=first and h == 0,
                                stop=(g == BANKS - 1 and r == CB - 1 and sw == 1), skip_group_check=True)
                last.then_inc(sm["y_ps"], 1)

            def offset(tau):
                if isinstance(tau, int) and (tau < SH1 or tau >= SH1 + ROUTED):
                    return 0
                return pe.value_load(woff[0:1, bass.ds(tau, 1)], min_val=0, max_val=E * SLOT)

            def ffn(tau, u, now, before, more=True, beside=lambda g: None, late=False,
                    by_sp=False):
                off = now(tau)
                if late:
                    transpose_rows(tau, u)
                    down(tau - 1, 2, before(tau - 1))
                up(tau, u, 0, off)
                beside(0)
                if before is not None:
                    old = before(tau - 1)
                    if not late:
                        down(tau - 1, 2, old)
                up(tau, u, 1, off)
                beside(1)
                if before is not None:
                    down(tau - 1, 3, old)
                if more:
                    transpose_rows(tau + 1, 1 - u, by_sp)
                up(tau, u, 2, off)
                beside(2)
                down(tau, 0, off)
                up(tau, u, 3, off)
                beside(3)
                down(tau, 1, off)

            def fixed(tau):
                return 0

            def count():
                mask = slotf[:, 0:128].bitcast(BF16)
                pe.wait_ge(sm["mask_ready"], 1)
                pe.matmul(pPre[:, 0:NT * E], upper[:, :], mask, start=True, stop=True)
                pe.matmul(pTot[:, 0:NT * E], ones_b[:, :], mask, start=True, stop=True)\
                    .then_inc(sm["count_ps"], 1)

            def invert(c):
                pe.wait_ge(sm["oneh_ready"], c + 1)
                for q in range(RC):
                    for h in range(2):
                        last = pe.matmul(pTok[:, h * HALVES:(h + 1) * HALVES], oh_pos[c % 2][:, q, :],
                                         oh_row[c % 2][h][:, q, :], start=(c == 0 and q == 0 and h == 0),
                                         stop=(c == CHUNKS - 1 and q == RC - 1), skip_group_check=True)
                last.then_inc(sm["tok_ps"], 1)

            pe.wait_ge(sm["const_ready"], CONSTANTS)
            pe.wait_ge(sm["wlo"], 8 * (NS - 1) + 2)
            transpose_rows(0, 0)
            pe.wait_ge(sm["xt_done"], 1)
            for g in (4, 5, 6):
                weight_bank(NS - 1, g)

            def beside_first(tau, g):
                if tau == 0 and g == 0:
                    weight_bank(NS - 1, 7)
                step = BANKS * tau + g
                if step == COUNT:
                    count()
                c, half = divmod(step - ONE_HOT - 3, 2)
                if half == 0 and 0 <= c < CHUNKS - 1:
                    invert(c)
                if step == TABLES:
                    invert(CHUNKS - 1)
                z = last_norm(tau, g)
                if z is not None:
                    if z > LAST:
                        logits(z - 1, (z - 1) % 4, ln_last)
                    if z < NT:
                        transpose_z(z, z % 4, ln_last)

            ffn(0, 0, fixed, None, beside=lambda g: beside_first(0, g))
            for tau in range(1, SH1):
                ffn(tau, tau % 2, fixed, fixed, more=tau < SH1 - 1, beside=lambda g: beside_first(tau, g))
            pe.wait_ge(sm["offsets_ready"], 1)
            ffn(SH1, SH1 % 2, offset, fixed, late=True)
            tile_pairs(pe, SH1 + 1, SH1 + ROUTED, lambda tau, u: ffn(tau, u, offset, offset))
            tau = SH1 + ROUTED
            ffn(tau, tau % 2, fixed, offset)
            tile_pairs(pe, tau + 1, NF - 1, lambda tau, u: ffn(tau, u, fixed, fixed, by_sp=True))
            ffn(NF - 1, (NF - 1) % 2, fixed, fixed, more=False)
            down(NF - 1, 2, 0)
            down(NF - 1, 3, 0)

        @block.scalar
        def _(act):
            def raw_squares(t, m, h):
                n = 4 * t + 2 * m + h
                act.wait_ge(raw_in[m], 16 * t + 16)
                if not isinstance(t, int) or t > 0:
                    act.wait_ge(sm["all_sq"], 2 * t + m - 1)
                if not isinstance(t, int) or n > 0:
                    act.wait_ge(sm["raw_sq"], n)
                act.activation(squares, raws[m][:, h * 1024:(h + 1) * 1024], ACT.Square,
                               accum_out=psq[:, m, h:h + 1]).then_inc(sm["raw_sq"], 1)

            def take(step):
                act.wait_ge(sm["su_pe"], step + 1)
                return ps[step % 4]

            for b in range(B):
                q = take(b)
                act.activation(ctxT[:, b, :, :], q[:, :].rearrange("p (k n) -> p k n", k=2)[:, :, 0:C],
                               ACT.Copy).then_inc(sm["su_ev"], 1)
            q = take(4)
            act.activation(woT.rearrange("p c d -> p (c d)"), q[:, :], ACT.Copy).then_inc(sm["su_ev"], 1)
            q = take(5)
            act.activation(fa.rearrange("p c d -> p (c d)"), q[:, :], ACT.Copy).then_inc(sm["su_ev"], 1)
            q = take(6)
            act.activation(u_c, q[:, 0:2], ACT.Copy).then_inc(sm["u_ready"], 1)
            act.activation(gateT[:, :, :].rearrange("p k e -> p (k e)"), q[:, 16:16 + 2 * E], ACT.Copy)\
                .then_inc(sm["su_ev"], 1)
            q = take(7)
            act.activation(fc.rearrange("p c d -> p (c d)"), q[:, :], ACT.Copy).then_inc(sm["su_ev"], 1)
            q = take(8)
            act.activation(cbs, q[:, 0:D], ACT.Copy).then_inc(sm["su_ev"], 1)
            for b in range(B):
                q = take(9 + 3 * b)
                act.activation(ktn[:, b, :, :], q[:, :].rearrange("p (k n) -> p k n", k=2)[:, :, 0:C],
                               ACT.Copy, scale=NEG_SCALE).then_inc(sm["su_ev"], 1)
                q = take(10 + 3 * b)
                act.activation(biasn[:, b, :], q[:, 0:C], ACT.Copy, scale=NEG_SCALE).then_inc(sm["su_ev"], 1)
            for h in range(2):
                raw_squares(0, 0, h)

            def x_to_sbuf(i, u):
                act.wait_ge(sm["xt_ps"], i + 1)
                if not isinstance(i, int) or i >= 2:
                    act.wait_ge(sm["sc_ps"], i - 1)
                act.activation(xnT[:, u, :, :].rearrange("p k t -> p (k t)"), pXT[:, 0:D], ACT.Copy)\
                    .then_inc(sm["xnt_done"], 1)

            def exponentials(i, u, r):
                act.wait_ge(sm["sc_done"], i + 1)
                act.activation(sc[:, u, :], sc[:, u, :], ACT.Exp, bias=negmax[:, u:u + 1], scale=-1.0,
                               accum_out=rowsum[:, r:r + 1]).then_inc(sm["exp_done"], 1)

            def p_to_sbuf(i, u):
                act.wait_ge(sm["pt_ps"], i + 1)
                if not isinstance(i, int) or i >= 2:
                    act.wait_ge(sm["pv_ps"], i - 1)
                act.activation(pT[:, u, 0, :], pPT[:, 0:P], ACT.Copy).then_inc(sm["ptt_done"], 1)
                act.activation(pT[0:C2, u, 1, :], pPT[0:C2, P:2 * P], ACT.Copy).then_inc(sm["ptt_done"], 1)

            def weight_high(t, g):
                m, q = g // 4, pW[g]
                if g % 4 == 0:
                    act.wait_ge(sm["scale_ready"], 2 * t + m + 1)
                act.wait_ge(sm["wt_ps"], 8 * t + g + 1)
                alone(act)
                at = t * SLOT + (m * 2 * KD * HID) + (g % 4) * 512
                act.activation(wflat[:, bass.ds(at, 512)], q[:, :], ACT.Copy,
                               scale=wscale[:, m, bass.ds(t, 1)]).then_inc(sm["whi"], 1)

            def high(z, w, bufs):
                act.wait_ge(sm["z_done"], z + 1)
                act.wait_ge(rows_st[w % 4], 4 * (AHEAD + z - w % 4))
                act.activation(bufs[2][:, w % 4, 0:D], bufs[0][:, w % 2, :], ACT.Copy).then_inc(sm["z_hi"], 1)

            def z_to_sbuf(z, w, bufs):
                act.wait_ge(sm["zt_ps"], AHEAD + z + 1)
                act.wait_ge(sm["lg_ps"], AHEAD + z - 1)
                act.activation(bufs[1][:, w % 2, :, :].rearrange("p k t -> p (k t)"), pZT, ACT.Copy)\
                    .then_inc(sm["ztt_done"], 1)

            def att(i, b, j):
                one = not isinstance(i, int)
                s = j % 4
                t, tp = b * (JT // 4) + j // 4, b * (JT // 4) + (j - 1) // 4
                z = i - LN_LAG
                if one or 0 < i <= NT:
                    weight_high(tp, 2 * ((j - 1) % 4) + 1)
                if (one or i < NT or s < 2) and s % 2 == 1:
                    raw_squares(t + s // 2, 1 - s // 2, 1)
                if one or i < NT:
                    x_to_sbuf(i, s % 2)
                if one or i < NT:
                    weight_high(t, 2 * s)
                if one or z >= 0:
                    z_to_sbuf(z, s, ln_beside)
                if one or 0 <= i - 2 < NT:
                    p_to_sbuf(i - 2, s % 2)
                if one or 0 <= i - 1 < NT:
                    exponentials(i - 1, (s - 1) % 2, (s - 1) % 4)
                if (one or i < NT or s < 2) and s % 2 == 0:
                    raw_squares(t + s // 2, 1 - s // 2, 0)

            act.sem_inc(sm["ztt_done"], AHEAD)
            for i in range(FULL * JT):
                att(i, i // JT, i % JT)
            with act.Fori(FULL, B) as b:
                for j in range(JT):
                    att(b * JT + j, b, j)
            for j in range(4):
                att(NT + j, B, j)
            act.wait_ge(sm["sc_ps"], NT)
            for g in range(4):
                weight_high(NS - 1, g)
            act.activation(unread[:, :], identf[:, 0:1], ACT.Silu)
            act.wait_ge(sm["x2_done"], NT)
            for g in (4, 5, 6):
                weight_high(NS - 1, g)
            def hidden(tau, u, beside=lambda g: None):
                for g in range(BANKS):
                    n = BANKS * tau + g
                    act.wait_ge(sm["h_ps"], n + 1)
                    if not isinstance(tau, int) or n >= 2:
                        act.wait_ge(sm["lo_done"], n - 1)
                    alone(act)
                    act.activation(sring[:, g % 2, :], pH[g][:, :], ACT.Silu,
                                   scale=tab[:, 0, bass.ds(tau, 1)]).then_inc(sm["silu_done"], 1)
                    act.wait_ge(sm["silu_done"], n + 1)
                    if not isinstance(tau, int) or tau > 0:
                        act.wait_ge(sm["y_ps"], n - BANKS + 1)
                    alone(act)
                    act.activation(hring[:, g, 0, :], sring[:, g % 2, :], ACT.Copy,
                                   scale=tab[:, 1, bass.ds(tau, 1)]).then_inc(sm["hi_done"], 1)
                    beside(g)

            def beside_first(tau, g):
                if tau == 0 and g == 0:
                    weight_high(NS - 1, 7)
                z = last_norm(tau, g)
                if z is not None and z < NT:
                    high(z, z % 4, ln_last)
                    z_to_sbuf(z, z % 4, ln_last)

            act.wait_ge(sm["z_lo"], AHEAD + LAST)
            for q in range(4):
                act.wait_ge(rows_st[q], 4 * (AHEAD + LAST))
            act.wait_ge(sm["tabs0"], 6)
            for tau in range(5):
                hidden(tau, tau % 2, lambda g: beside_first(tau, g))
            act.wait_ge(sm["gate_diff"], 1)
            act.activation(ex, m2, ACT.Exp, scale=1.0 / ROW_SCALE).then_inc(sm["gate_exp"], 1)
            tile_pairs(act, 5, SH1, hidden)
            act.wait_ge(sm["routed_ready"], 1)
            tile_pairs(act, SH1, SH1 + ROUTED, hidden)
            tile_pairs(act, SH1 + ROUTED, NF, hidden)

        @block.vector
        def _(dve):
            n = [0]

            def link(ins):
                n[0] += 1
                ins.then_inc(sm["dchain"], 1)
                dve.wait_ge(sm["dchain"], n[0])

            def moment_step(q, at, n, target, linked):
                st, mu = stats[:, bass.ds(at, n), :], mean[:, bass.ds(at, n)]
                y, a, v, b = rstd[:, bass.ds(at, n)], nt_a[:, 0:n], nt_v[:, 0:n], nt_b[:, 0:n]
                k = 1.0 / target ** 2
                if q == 0:
                    linked(dve.tensor_tensor(a, st[:, :, 1], st[:, :, 4], ALU.add))
                elif q == 1:
                    linked(dve.tensor_scalar(mu, a, 0.5, None, ALU.mult))
                elif q == 2:
                    linked(dve.tensor_tensor(a, st[:, :, 1], st[:, :, 4], ALU.subtract))
                elif q == 3:
                    linked(dve.scalar_tensor_tensor(out=b, in0=a, scalar=0.25 * k, in1=a,
                                                    op0=ALU.mult, op1=ALU.mult))
                elif q == 4:
                    linked(dve.tensor_tensor(v, st[:, :, 2], st[:, :, 5], ALU.add))
                elif q == 5:
                    linked(dve.tensor_scalar(v, v, k / D, k * EPS, ALU.mult, ALU.add))
                elif q == 6:
                    linked(dve.tensor_tensor(v, v, b, ALU.add))
                elif q == 7:
                    linked(dve.tensor_scalar(b.bitcast(I32), v.bitcast(I32), -0.5, float(0x5F3759DF),
                                             ALU.mult, ALU.add))
                elif (q - 8) % 3 == 0:
                    linked(dve.scalar_tensor_tensor(out=a, in0=b, scalar=-0.5, in1=b,
                                                    op0=ALU.mult, op1=ALU.mult))
                elif (q - 8) % 3 == 1:
                    linked(dve.tensor_tensor(a, a, v, ALU.mult))
                else:
                    linked(dve.scalar_tensor_tensor(out=b if q < MOMENT_STEPS - 1 else y, in0=a, scalar=1.5,
                                                    in1=b, op0=ALU.add, op1=ALU.mult))

            def row(i):
                return xres[:, bass.ds(i, 1), :].rearrange("p a d -> p (a d)")

            dve.memset(ones_f, 1.0).then_inc(sm["ones_ready"], 1)
            dve.wait_ge(sm["ones_ready"], 1)
            dve.wait_ge(sm["b_in"], 64)
            link(dve.tensor_scalar(bvbc[:, 0, :], ones_f, bv_c[:, 0:1], None, ALU.mult))
            dve.tensor_scalar(bvbc[:, 1, :], ones_f, bv_c[:, 1:2], None, ALU.mult).then_inc(sm["bv_bc"], 1)

            def values_to_sbuf(b):
                dve.wait_ge(sm["su_pe"], 9 + 3 * b + 3)
                q = ps[(11 + 3 * b) % 4]
                dve.wait_ge(sm["su_ev"], 9)
                link(dve.tensor_tensor(vct[:, b, 0, :], q[:, 0:D], cbs, ALU.add))
                dve.tensor_tensor(vct[0:C2, b, 1, :], q[0:C2, D:2 * D], cbs[0:C2, :], ALU.add)\
                    .then_inc(sm["values_ready"], 1)

            for i in range(NT):
                if i % JT == 0:
                    dve.wait_ge(sm[f"x{i // JT}"], 16)
                last = dve.bn_stats(stats[:, i, :], xres[:, i, :])
                if i == JT - 1:
                    dve.wait_ge(sm["u_ready"], 1)
                    link(dve.tensor_scalar(ubc[:, 0, :], ones_f, u_c[:, 0:1], None, ALU.mult))
                    dve.tensor_scalar(ubc[:, 1, :], ones_f, u_c[:, 1:2], None, ALU.mult)\
                        .then_inc(sm["u_bc"], 1)
                if i == 3 * JT - 1:
                    values_to_sbuf(0)
            link(last)
            values_to_sbuf(1)
            for q in range(MOMENT_STEPS):
                moment_step(q, 0, NT, 1.0, link)
                if q == MOMENT_STEPS // 2:
                    values_to_sbuf(2)
            values_to_sbuf(3)

            def scale(t, m):
                dve.wait_ge(sm["all_sq"], 2 * t + m + 1)
                q = 3 * (2 * t + m)
                dve.tensor_tensor(norm2[:, 0:1], asq[:, m, 0:1], asq[:, m, 1:2], ALU.add)\
                    .then_inc(sm["scale_step"], 1)
                dve.wait_ge(sm["scale_step"], q + 1)
                dve.tensor_scalar(ebits[:, 0:1], norm2[:, 0:1].bitcast(I32), 24, None,
                                  ALU.logical_shift_right).then_inc(sm["scale_step"], 1)
                dve.wait_ge(sm["scale_step"], q + 2)
                dve.tensor_scalar(ebits[:, 1:2], ebits[:, 0:1], 17.0, -float(1 << 23), ALU.max, ALU.mult)\
                    .then_inc(sm["scale_step"], 1)
                dve.wait_ge(sm["scale_step"], q + 3)
                dve.tensor_scalar(wscale[:, m, bass.ds(t, 1)].bitcast(I32), ebits[:, 1:2], float(204 << 23),
                                  None, ALU.add).then_inc(sm["scale_ready"], 1)
                dve.wait_ge(sm["scale_ready"], 2 * t + m + 1)

            def weight_low(t, g):
                m, q = g // 4, pW[g]
                at = t * SLOT + (m * 2 * KD * HID) + (g % 4) * 512
                dve.wait_ge(sm["whi"], 8 * t + g + 1)
                dve.scalar_tensor_tensor(out=wflat[:, bass.ds(at + KD * HID, 512)], in0=q[:, :],
                                         scalar=wscale[:, m, bass.ds(t, 1)], in1=wflat[:, bass.ds(at, 512)],
                                         op0=ALU.mult, op1=ALU.subtract).then_inc(sm["wlo"], 1)

            def normalize(i, u):
                if not isinstance(i, int) or i >= 2:
                    dve.wait_ge(sm["xt_ps"], i - 1)
                dve.tensor_scalar(xn[:, u, :], row(i), mean[:, bass.ds(i, 1)], rstd[:, bass.ds(i, 1)],
                                  ALU.subtract, ALU.mult).then_inc(sm["xn_done"], 1)

            def negated_scores(i, u, b):
                dve.wait_ge(sm["sc_ps"], i + 1)
                if not isinstance(i, int) or i >= 2:
                    dve.wait_ge(sm["pt_ps"], i - 1)
                dve.tensor_tensor(sc[:, u, :], pSC[:, 0:C], biasn[:, bass.ds(b, 1), :]
                                  .rearrange("p a c -> p (a c)"), ALU.add).then_inc(sm["sc_sum"], 1)

            def score_maximum(i, u):
                dve.wait_ge(sm["sc_sum"], i + 1)
                dve.tensor_reduce(negmax[:, u:u + 1], sc[:, u, :], AX.X, ALU.min).then_inc(sm["sc_done"], 1)

            def row_factor(i, u, r):
                dve.wait_ge(sm["exp_done"], i + 1)
                dve.reciprocal(rinv[:, u:u + 1], rowsum[:, r:r + 1]).then_inc(sm["rinv_done"], 1)

            def add_attention(i, u):
                dve.wait_ge(sm["rinv_done"], i + 1)
                dve.wait_ge(sm["pv_ps"], i + 1)
                dve.scalar_tensor_tensor(out=row(i), in0=pPV[:, 0:D], scalar=rinv[:, u:u + 1], in1=row(i),
                                         op0=ALU.mult, op1=ALU.add).then_inc(sm["x2_done"], 1)

            def statistics(i):
                dve.wait_ge(sm["x2_done"], i + 1)
                alone(dve)
                dve.bn_stats(stats[:, bass.ds(i, 1), :].rearrange("p a s -> p (a s)"), row(i))\
                    .then_inc(sm["stat_done"], 1)

            def rows_to_sbuf(tau, u):
                dve.wait_ge(sm["xg_t"], tau + 1)
                dve.tensor_copy(xT[u].rearrange("p s k t -> p (s k t)"),
                                pT16.rearrange("p s k t -> p (s k t)")).then_inc(sm["xt_done"], 1)

            def second_norm(z, w, bufs):
                dve.wait_ge(sm["zt_ps"], AHEAD + z - 1)
                dve.wait_ge(sm["z_lo"], AHEAD + z - 1)
                dve.tensor_scalar(bufs[0][:, w % 2, :], row(z), mean[:, bass.ds(z, 1)], rstd[:, bass.ds(z, 1)],
                                  ALU.subtract, ALU.mult).then_inc(sm["z_done"], 1)

            def low(z, w, bufs):
                dve.wait_ge(sm["z_hi"], z + 1)
                dve.tensor_tensor(bufs[2][:, w % 4, D:2 * D], bufs[0][:, w % 2, :], bufs[2][:, w % 4, 0:D],
                                  ALU.subtract).then_inc(sm["z_lo"], 1)

            def group_moment(g, q):
                if q == 0:
                    dve.wait_ge(sm["stat_done"], (g + 1) * GROUP)
                else:
                    dve.wait_ge(sm["moment_step"], g * MOMENT_STEPS + q)
                moment_step(q, g * GROUP, GROUP, ROW_SCALE,
                            lambda ins: ins.then_inc(sm["moment_step"], 1))

            def att(i, b, j):
                one = not isinstance(i, int)
                s, sp_ = j % 4, (j - 1) % 4
                t, tp = b * (JT // 4) + j // 4, b * (JT // 4) + (j - 1) // 4
                moments_beside = one or i >= 2 * GROUP

                def moment(place):
                    q = 5 * s + place
                    if moments_beside and q < MOMENT_STEPS:
                        group_moment(b * (JT // GROUP) + j // GROUP - 2, q)

                scored, added = one or 0 <= i - 1 < NT, one or 0 <= i - 4 < NT
                if s % 2 == 0:
                    scale(t, s // 2)
                if one or i >= LN_LAG:
                    dve.wait_ge(sm["moment_step"], MOMENT_STEPS * (b * (JT // GROUP) + j // GROUP - 2))
                    second_norm(i - LN_LAG, s, ln_beside)
                moment(0)
                if added:
                    row_factor(i - 4, s % 2, s)
                if one or 0 < i <= NT:
                    weight_low(tp, 2 * sp_)
                if scored:
                    negated_scores(i - 1, (s - 1) % 2, b if j >= 1 else b - 1)
                moment(1)
                if added:
                    add_attention(i - 4, s % 2)
                if scored:
                    score_maximum(i - 1, (s - 1) % 2)
                moment(2)
                if added:
                    statistics(i - 4)
                moment(3)
                if one or 0 < i <= NT:
                    weight_low(tp, 2 * sp_ + 1)
                moment(4)
                if one or i + 2 < NT:
                    normalize(i + 2, s % 2)

            normalize(0, 0)
            normalize(1, 1)
            for i in range(FULL * JT):
                att(i, i // JT, i % JT)
            with dve.Fori(FULL, B - 1) as b:
                for j in range(JT):
                    att(b * JT + j, b, j)
            for j in range(JT):
                att(LAST + j, B - 1, j)
            for j in range(4):
                att(NT + j, B, j)
            ONE2 = float(254 << 23)
            link(dve.tensor_scalar(inv1[:, :].bitcast(I32), wscale[:, 0, :].bitcast(I32), -1.0,
                                   ONE2 - float(ROW_SCALE_LOG << 23), ALU.mult, ALU.add))
            link(dve.tensor_scalar(hsc[:, :], wscale[:, 0, :], 2.0 ** -8, None, ALU.mult))
            link(dve.tensor_tensor(inv2[:, :], hsc[:, :], wscale[:, 1, :], ALU.mult))
            link(dve.tensor_scalar(inv2[:, :].bitcast(I32), inv2[:, :].bitcast(I32), -1.0, ONE2,
                                   ALU.mult, ALU.add))
            for a, z in ((0, SH1), (SH1 + ROUTED, NF)):
                for q, src in enumerate((inv1, hsc, inv2)):
                    dve.tensor_copy(tab[:, q, a:z], src[:, 0:1].to_broadcast([P, z - a]))\
                        .then_inc(sm["tabs0"], 1)
            for g in range(4):
                weight_low(NS - 1, g)
            dve.wait_ge(sm["z_lo"], AHEAD + LAST)
            dve.wait_ge(sm["raw_sq"], 4 * NS)
            rows_to_sbuf(0, 0)
            for g in (4, 5, 6):
                weight_low(NS - 1, g)
            dve.wait_ge(sm["moment_step"], MOMENT_STEPS * (NT // GROUP - 1))
            dve.wait_ge(sm["const_ready"], CONSTANTS)

            def hidden_low(tau, g):
                dve.wait_ge(sm["hi_done"], BANKS * tau + g + 1)
                dve.scalar_tensor_tensor(out=hring[:, g, 1, :], in0=sring[:, g % 2, :],
                                         scalar=tab[:, 1, bass.ds(tau, 1)], in1=hring[:, g, 0, :],
                                         op0=ALU.mult, op1=ALU.subtract).then_inc(sm["lo_done"], 1)

            def add_shared(i, tau):
                dve.wait_ge(sm["y_ps"], BANKS * tau + BANKS)
                two = xres[:, bass.ds(2 * i, 2), :].rearrange("p a d -> p (a d)")
                dve.scalar_tensor_tensor(out=two, in0=pY[:, :], scalar=inv2[:, 0:1], in1=two,
                                         op0=ALU.mult, op1=ALU.add).then_inc(sm["y_done"], 1)

            def front(tau):
                add_shared(tau, tau)

            def back(tau):
                add_shared(tau - ROUTED, tau)

            def expert_rows(tau):
                dve.wait_ge(sm["y_ps"], BANKS * tau + BANKS)
                if not isinstance(tau, int) or tau > SH1:
                    dve.wait_ge(sm["y_store"], 16 * (tau - SH1))
                dve.tensor_scalar(ybuf, pY[:, :], tab[:, 2, bass.ds(tau, 1)], None, ALU.mult)\
                    .then_inc(sm["y_done"], 1)

            def ffn(tau, u, finish, more=True, beside=lambda g: None):
                hidden_low(tau, 0)
                beside(0)
                if finish is not None:
                    finish(tau - 1)
                hidden_low(tau, 1)
                beside(1)
                if more:
                    rows_to_sbuf(tau + 1, 1 - u)
                hidden_low(tau, 2)
                beside(2)
                hidden_low(tau, 3)
                beside(3)

            def beside_first(tau, g):
                step = BANKS * tau + g
                if step == 0:
                    weight_low(NS - 1, 7)
                if step == 0:
                    second_norm(LAST, 0, ln_last)
                if step in (1, 2, 3):
                    for q in range(6 * (step - 1), min(6 * step, MOMENT_STEPS)):
                        group_moment(NT // GROUP - 1, q)
                if step == 3:
                    dve.wait_ge(sm["moment_step"], MOMENT_STEPS * (NT // GROUP))
                if step in (CHOOSE, CHOOSE + 1):
                    choose(step - CHOOSE)
                if step == PLACES:
                    places()
                if step in (PLACES + 1, PLACES + 2):
                    split_places(step - PLACES - 1)
                c, half = divmod(step - ONE_HOT, 2)
                if 0 <= c < CHUNKS:
                    one_hot(c, half)
                if step == TABLES:
                    slot_rows()
                if step == TABLES + 1:
                    tile_weights()
                if step == TABLES + 2:
                    tile_scales()
                z = last_norm(tau, g)
                if z is not None and z < NT:
                    if z + 1 < NT:
                        second_norm(z + 1, (z + 1) % 4, ln_last)
                    low(z, z % 4, ln_last)

            def over_experts(t):
                return t.rearrange("p (i a) -> p i a", a=1).to_broadcast([P, NT, E])

            def choose(k):
                first = efirst[:, :].rearrange("p (a e) -> p a e", a=1).to_broadcast([P, NT, E])
                if k == 0:
                    dve.wait_ge(sm["lg_ps"], AHEAD + NT)
                    link(dve.tensor_copy(lg, pLG))
                src, m, sel, oh = ((lg, m1, sel1, oh1), (lg2, m2, sel2, oh2))[k]
                link(dve.tensor_reduce(m, by_token(src), AX.X, ALU.max))
                link(dve.tensor_tensor(by_token(tmp), by_token(src), over_experts(m), ALU.is_ge))
                link(dve.tensor_tensor(by_token(tmp), by_token(tmp), first, ALU.mult))
                link(dve.tensor_reduce(sel, by_token(tmp), AX.X, ALU.max))
                link(dve.tensor_tensor(by_token(oh), by_token(tmp), over_experts(sel), ALU.is_equal))
                if k == 0:
                    link(dve.scalar_tensor_tensor(out=lg2, in0=oh, scalar=-3.0e38, in1=lg,
                                                  op0=ALU.mult, op1=ALU.add))
                else:
                    dve.tensor_tensor(by_expert(slotf[:, 0:128].bitcast(BF16)),
                                      oh1.rearrange("p (i e) -> p e i", e=E),
                                      oh2.rearrange("p (i e) -> p e i", e=E), ALU.add)\
                        .then_inc(sm["mask_ready"], 1)
                    dve.tensor_tensor(m2, m2, m1, ALU.subtract).then_inc(sm["gate_diff"], 1)
                    link(dve.memset(rmask, 1.0))

            def places():
                ones_e, ct, cinc, base = (esm[:, q, :] for q in range(4))
                link(dve.memset(by_expert(rmask)[:, :, 0:1], 0.0))
                link(dve.memset(ones_e, 1.0))
                dve.wait_ge(sm["count_ps"], 1)
                link(dve.tensor_tensor_scan(incl, rmask, pTot[:, 0:NT * E], 0.0, ALU.mult, ALU.add))
                link(dve.tensor_scalar(cnt_i[:, :], by_expert(incl)[:, :, NT - 1], float(R - 1), None, ALU.add))
                link(dve.tensor_scalar(cnt_i[:, :], cnt_i[:, :], R.bit_length() - 1, None,
                                       ALU.logical_shift_right))
                link(dve.tensor_copy(ct, cnt_i[:, :]))
                link(dve.tensor_tensor_scan(cinc, ones_e, ct, 0.0, ALU.mult, ALU.add))
                link(dve.tensor_tensor(base, cinc, ct, ALU.subtract))
                link(dve.tensor_scalar(base, base, float(R), None, ALU.mult))
                link(dve.tensor_tensor(slotf, incl, pTot[:, 0:NT * E], ALU.subtract))
                link(dve.tensor_tensor(slotf, slotf, pPre[:, 0:NT * E], ALU.add))
                link(dve.tensor_tensor(by_expert(slotf), by_expert(slotf),
                                       base.rearrange("p (e a) -> p e a", a=1).to_broadcast([P, E, NT]),
                                       ALU.add))

            def split_places(k):
                link(dve.tensor_tensor(by_token(tmp), by_token((oh1, oh2)[k]),
                                       slotf.rearrange("p (e i) -> p i e", e=E), ALU.mult))
                link(dve.tensor_reduce(posf[:, k, :], by_token(tmp), AX.X, ALU.add))
                if k == 0:
                    return
                pair = lg2[:, 0:2 * NT].bitcast(U32).rearrange("p (k i) -> p k i", k=2)
                link(dve.tensor_copy(slot_u[:, :, :], posf))
                link(dve.tensor_scalar(pair, slot_u[:, :, :], 7, None, ALU.logical_shift_right))
                link(dve.tensor_copy(half_b[:, :, :], pair))
                link(dve.tensor_scalar(pair, slot_u[:, :, :], P - 1, None, ALU.bitwise_and))
                link(dve.tensor_copy(place_b[:, :, :], pair))

            def one_hot(c, half):
                k, i0 = c * RC // NT, c * RC % NT
                row = oh_row[c % 2]

                def spread(t, w):
                    return t.rearrange("p (q a) -> p q a", a=1).to_broadcast([P, RC, w])

                if half == 0:
                    if c >= 2:
                        dve.wait_ge(sm["tok_ps"], c - 1)
                    link(dve.tensor_tensor(oh_pos[c % 2], iota_b[:, :].rearrange("p (a n) -> p a n", a=1)
                                           .to_broadcast([P, RC, P]), spread(place_b[:, k, i0:i0 + RC], P),
                                           ALU.is_equal))
                    link(dve.tensor_tensor(row[0], iota_b[:, 0:HALVES].rearrange("p (a n) -> p a n", a=1)
                                           .to_broadcast([P, RC, HALVES]),
                                           spread(half_b[:, k, i0:i0 + RC], HALVES), ALU.is_equal))
                else:
                    link(dve.tensor_scalar(row[1], row[0], iota_p[:, 0:1], None, ALU.mult))
                    dve.tensor_tensor(row[0], row[0], spread(iota_b[:, i0:i0 + RC], HALVES), ALU.mult)\
                        .then_inc(sm["oneh_ready"], 1)

            def slot_rows():
                dve.wait_ge(sm["tok_ps"], CHUNKS)
                link(dve.tensor_copy(tkf, pTok[:, 0:2 * HALVES]))
                dve.scalar_tensor_tensor(out=tok[:, :], in0=tkf[:, 0:HALVES], scalar=float(P),
                                         in1=tkf[:, HALVES:2 * HALVES], op0=ALU.mult, op1=ALU.add)\
                    .then_inc(sm["slots_ready"], 1)

            def routed_tiles(t):
                return t.rearrange("p (j a) -> p j a", a=1).to_broadcast([P, ROUTED, E])

            def experts(t):
                return t.rearrange("p (a e) -> p a e", a=1).to_broadcast([P, ROUTED, E])

            def tile_weights():
                cinc = esm[:, 2, :]
                for q in range(4):
                    dve.wait_ge(rows_st[q], 4 * (AHEAD + NT))
                link(dve.tensor_tensor(eoh, routed_tiles(iot[:, :]), experts(cinc), ALU.is_ge))
                link(dve.tensor_reduce(ejf, eoh, AX.X, ALU.add))
                link(dve.tensor_scalar(ejf, ejf, float(E - 1), None, ALU.min))
                dve.tensor_scalar(woff[:, SH1:SH1 + ROUTED], ejf, 1.0, float(SLOT), ALU.add, ALU.mult)\
                    .then_inc(sm["offsets_ready"], 1)
                link(dve.tensor_tensor(eoh, experts(ioe[:, :]), routed_tiles(ejf), ALU.is_equal))

            def tile_scales():
                for q, src in enumerate((inv1, hsc)):
                    link(dve.tensor_tensor(eot, eoh, experts(src[:, 1:NS]), ALU.mult))
                    link(dve.tensor_reduce(tab[:, q, SH1:SH1 + ROUTED], eot, AX.X, ALU.add))
                dve.sem_inc(sm["routed_ready"], 1)

            def output_scales():
                link(dve.tensor_tensor(eot, eoh, experts(inv2[:, 1:NS]), ALU.mult))
                link(dve.tensor_reduce(tab[:, 2, SH1:SH1 + ROUTED], eot, AX.X, ALU.add))

            def gate_weights():
                dve.wait_ge(sm["gate_exp"], 1)
                link(dve.tensor_scalar(den, ex, 1.0, None, ALU.add))
                link(dve.reciprocal(gates[:, 0, :], den))
                link(dve.tensor_tensor(gates[:, 1, :], ex, gates[:, 0, :], ALU.mult))

            for tau in range(SH1):
                ffn(tau, tau % 2, front if tau else None, more=tau < SH1 - 1,
                    beside=lambda g: beside_first(tau, g))
            rows_to_sbuf(SH1, SH1 % 2)
            ffn(SH1, SH1 % 2, front, beside=lambda g: (output_scales, gate_weights)[g - 2]() if g >= 2 else None)
            tile_pairs(dve, SH1 + 1, SH1 + ROUTED, lambda tau, u: ffn(tau, u, expert_rows))

            def combine(i):
                q = i % 4
                dve.wait_ge(grow_in[q], 32 * (i // 4 + 1))
                for k in range(2):
                    last = dve.scalar_tensor_tensor(out=xres[:, i, :], in0=grow[:, q, k, :],
                                                    scalar=gates[:, k, i:i + 1], in1=xres[:, i, :],
                                                    op0=ALU.mult, op1=ALU.add)
                    if k == 0:
                        link(last)
                last.then_inc(sm["comb_done"], 1)

            for m in range(SH2):
                tau = SH1 + ROUTED + m

                def beside(g):
                    tiles = combined(m) if m else ()
                    for i in tiles[max(g - 1, 0) * len(tiles) // 3:g * len(tiles) // 3]:
                        combine(i)

                ffn(tau, tau % 2, back if m else expert_rows, more=m < SH2 - 1, beside=beside)
            back(NF - 1)
            dve.wait_ge(sm["y_done"], NF)
            for i in combined(SH2):
                combine(i)


_INS = ['x', 'ctx_1024', 'L0_xattn_Wk', 'L0_xattn_Wv', 'L0_xattn_bv', 'L0_xattn_Wq', 'L0_xattn_bq',
        'L0_xattn_Wo', 'L0_xattn_bo', 'L0_ffn_shared_w1', 'L0_ffn_shared_w2', 'L0_ffn_experts_w1',
        'L0_ffn_experts_w2', 'L0_ffn_gate_w']
_OUTS = [((4, 1024, 256), 'float32')]


def kernel(**inputs):
    import numpy as _np
    import concourse.bacc as _bacc
    from concourse import mybir as _mybir
    from concourse.bass_utils import run_bass_kernel_spmd as _run

    nc = _bacc.Bacc("TRN2", target_bir_lowering=False, num_devices=1, dynamic_dma_scratch_size=4096)
    arrays, args = {}, []
    for name in _INS:
        a = _np.ascontiguousarray(inputs[name])
        arrays[f"in_{name}_dram"] = a
        args.append(nc.dram_tensor(f"in_{name}_dram", a.shape, _mybir.dt.from_np(a.dtype), kind="ExternalInput").ap())
    for i, (shape, dtype) in enumerate(_OUTS):
        dt = _mybir.dt.from_np(_np.dtype(dtype))
        args.append(nc.dram_tensor(f"out_{i}_dram", shape, dt, kind="ExternalOutput").ap())
    xattn_moe_kernel(nc, *args)
    r = _run(nc, [arrays], core_ids=[0])
    got = tuple(r.results[0][f"out_{i}_dram"] for i in range(len(_OUTS)))
    return got[0]
```
